# Optimizing a Trainium2 kernel written in Bass

```python
import numpy as np
import jax
import jax.numpy as jnp

def _softmax(x, axis=-1):
    return jax.nn.softmax(x, axis=axis)

def _gelu(x):
    return jax.nn.gelu(x, approximate=True)

def _silu(x):
    return jax.nn.silu(x)

def _sigmoid(x):
    return jax.nn.sigmoid(x)

def _layernorm(x, axis=-1, eps=1e-05):
    m = jnp.mean(x, axis=axis, keepdims=True)
    v = jnp.var(x, axis=axis, keepdims=True)
    return (x - m) / jnp.sqrt(v + eps)

def _scatter_add(tgt, idx, src, axis=0):
    return tgt.at[idx].add(src)

def _segment_sum(src, seg, n):
    return jax.ops.segment_sum(src, seg, n)
kernel_name = 'mk_xattn_ffn_d1_seqx_r4_061e3f'

def setup_inputs(seed: int=0):
    np.random.seed(seed)
    _w = jnp.asarray

    def _rec_inputs():
        import jax
        import jax.numpy as jnp
        _rk = jax.random.key(seed)
        x = -0.0003929 + 0.9999 * jax.random.normal(jax.random.fold_in(_rk, 1), (16, 100, 512), jnp.float32)
        _lenS = 100 - jax.random.randint(jax.random.fold_in(_rk, 7), (16,), 0, max(1, 100 // 4) + 1, jnp.int32)
        _lenS2 = 361 - jax.random.randint(jax.random.fold_in(_rk, 8), (16,), 0, max(1, 361 // 4) + 1, jnp.int32)
        _ctx_2048P = jax.random.normal(jax.random.fold_in(_rk, 11), (16, 16, 512), jnp.float32)
        _ctx_2048c = jax.random.dirichlet(jax.random.fold_in(_rk, 511), 0.3 * jnp.ones((16,), jnp.float32), (16, 361))
        _ctx_2048t = jnp.einsum('bsk,bkd->bsd', _ctx_2048c, _ctx_2048P)
        _ctx_2048t = _ctx_2048t * jax.lax.rsqrt(jnp.mean(jnp.square(_ctx_2048t)) + 1e-12) * 0.953939
        ctx_2048 = -1.39393e-06 + 0.999914 * (_ctx_2048t + 0.3 * jax.random.normal(jax.random.fold_in(_rk, 611), (16, 361, 512), jnp.float32))
        itok_BxS_0_1023 = jax.random.randint(jax.random.fold_in(_rk, 12), (16, 100), 0, 256, jnp.int32)
        return (x, ctx_2048, itok_BxS_0_1023)
    x, ctx_2048, itok_BxS_0_1023 = _rec_inputs()

    def _L0_xattn_setup():
        import jax, jax.numpy as jnp
        import numpy as np
        B, Lq, Lk = (2, 1024, 256)
        Q_DIM, KV_DIM = (512, 512)
        H, HD = (16, 128)
        KVC, QC, R = (128, 192, 64)
        LOOKBACK = 8
        NEG = -1e+30

        def _rope(x, L):
            half = x.shape[-1] // 2
            inv_freq = 1.0 / 10000.0 ** (jnp.arange(half, dtype=jnp.float32) / half)
            ang = jnp.arange(L, dtype=jnp.float32)[:, None] * inv_freq
            cos, sin = (jnp.cos(ang), jnp.sin(ang))
            x1, x2 = (x[..., :half], x[..., half:])
            return jnp.concatenate([x1 * cos - x2 * sin, x1 * sin + x2 * cos], axis=-1)
        key = jax.random.key(seed)
        ks = jax.random.split(key, 11)

        def w(k, shape, fan_in):
            return jax.random.normal(k, shape, jnp.float32) / np.sqrt(fan_in).astype(np.float32)
        return {'q': jax.random.normal(ks[0], (B, Lq, Q_DIM), jnp.float32), 'kv': jax.random.normal(ks[1], (B, Lk, KV_DIM), jnp.float32), 'seg_id': jnp.sort(jax.random.randint(ks[2], (B, Lq), 0, Lk), axis=-1), 'W_kvc': w(ks[3], (KV_DIM, KVC), KV_DIM), 'W_dq': w(ks[4], (Q_DIM, QC), Q_DIM), 'W_uq': w(ks[5], (QC, H * HD), QC), 'W_qr': w(ks[6], (QC, H * R), QC), 'W_uk': w(ks[7], (KVC, H * HD), KVC), 'W_kr': w(ks[8], (KVC, R), KVC), 'W_uv': w(ks[9], (KVC, H * HD), KVC), 'W_o': w(ks[10], (H * HD, Q_DIM), H * HD)}
    _L0_xattn_all = _L0_xattn_setup()
    _L0_xattn_in = {k: v for k, v in _L0_xattn_all.items() if k in ('W_kvc', 'W_dq', 'W_uq', 'W_qr', 'W_uk', 'W_kr', 'W_uv', 'W_o')}
    del _L0_xattn_all

    def _L0_ffn_setup():
        import jax, jax.numpy as jnp
        import numpy as np
        HIDDEN = 512
        INTER = 1408
        B, S = (2, 512)

        def _ternary(key, shape):
            return jax.random.randint(key, shape, -1, 2).astype(jnp.float32)
        key = jax.random.key(seed)
        ks = jax.random.split(key, 7)
        x = jax.random.normal(ks[0], (B, S, HIDDEN), dtype=jnp.float32)
        gate_w = _ternary(ks[1], (INTER, HIDDEN))
        up_w = _ternary(ks[2], (INTER, HIDDEN))
        down_w = _ternary(ks[3], (HIDDEN, INTER))
        gate_s = jax.random.uniform(ks[4], (INTER,), minval=0.01, maxval=0.1, dtype=jnp.float32)
        up_s = jax.random.uniform(ks[5], (INTER,), minval=0.01, maxval=0.1, dtype=jnp.float32)
        down_s = jax.random.uniform(ks[6], (HIDDEN,), minval=0.01, maxval=0.1, dtype=jnp.float32)
        return {'x': x, 'gate_w': gate_w, 'up_w': up_w, 'down_w': down_w, 'gate_s': gate_s, 'up_s': up_s, 'down_s': down_s}
    _L0_ffn_all = _L0_ffn_setup()
    _L0_ffn_in = {k: v for k, v in _L0_ffn_all.items() if k in ('gate_w', 'up_w', 'down_w', 'gate_s', 'up_s', 'down_s')}
    del _L0_ffn_all
    return {'x': x, 'ctx_2048': ctx_2048, 'itok_BxS_0_1023': itok_BxS_0_1023, 'L0_xattn_W_kvc': _L0_xattn_in['W_kvc'], 'L0_xattn_W_dq': _L0_xattn_in['W_dq'], 'L0_xattn_W_uq': _L0_xattn_in['W_uq'], 'L0_xattn_W_qr': _L0_xattn_in['W_qr'], 'L0_xattn_W_uk': _L0_xattn_in['W_uk'], 'L0_xattn_W_kr': _L0_xattn_in['W_kr'], 'L0_xattn_W_uv': _L0_xattn_in['W_uv'], 'L0_xattn_W_o': _L0_xattn_in['W_o'], 'L0_ffn_gate_w': _L0_ffn_in['gate_w'], 'L0_ffn_up_w': _L0_ffn_in['up_w'], 'L0_ffn_down_w': _L0_ffn_in['down_w'], 'L0_ffn_gate_s': _L0_ffn_in['gate_s'], 'L0_ffn_up_s': _L0_ffn_in['up_s'], 'L0_ffn_down_s': _L0_ffn_in['down_s']}

def reference(x, ctx_2048, itok_BxS_0_1023, L0_xattn_W_kvc, L0_xattn_W_dq, L0_xattn_W_uq, L0_xattn_W_qr, L0_xattn_W_uk, L0_xattn_W_kr, L0_xattn_W_uv, L0_xattn_W_o, L0_ffn_gate_w, L0_ffn_up_w, L0_ffn_down_w, L0_ffn_gate_s, L0_ffn_up_s, L0_ffn_down_s):
    import jax
    import jax.numpy as jnp

    def _L0_xattn_ref(q, kv, seg_id, W_kvc, W_dq, W_uq, W_qr, W_uk, W_kr, W_uv, W_o):
        import jax, jax.numpy as jnp
        import numpy as np
        B, Lq, Lk = (2, 1024, 256)
        Q_DIM, KV_DIM = (512, 512)
        H, HD = (16, 128)
        KVC, QC, R = (128, 192, 64)
        LOOKBACK = 8
        NEG = -1e+30

        def _rope(x, L):
            half = x.shape[-1] // 2
            inv_freq = 1.0 / 10000.0 ** (jnp.arange(half, dtype=jnp.float32) / half)
            ang = jnp.arange(L, dtype=jnp.float32)[:, None] * inv_freq
            cos, sin = (jnp.cos(ang), jnp.sin(ang))
            x1, x2 = (x[..., :half], x[..., half:])
            return jnp.concatenate([x1 * cos - x2 * sin, x1 * sin + x2 * cos], axis=-1)
        b, lq, _ = q.shape
        lk = kv.shape[1]
        kv_c = kv @ W_kvc
        q_c = q @ W_dq
        q_nope = (q_c @ W_uq).reshape(b, lq, H, HD).transpose(0, 2, 1, 3)
        q_rope = (q_c @ W_qr).reshape(b, lq, H, R).transpose(0, 2, 1, 3)
        k_nope = (kv_c @ W_uk).reshape(b, lk, H, HD)
        v = (kv_c @ W_uv).reshape(b, lk, H, HD)
        k_rope = kv_c @ W_kr
        q_rope = _rope(q_rope, lq)
        k_rope = _rope(k_rope, lk)
        scale = 1.0 / np.sqrt(HD + R).astype(np.float32)
        scores = (jnp.einsum('bhqd,bkhd->bhqk', q_nope, k_nope) + jnp.einsum('bhqr,bkr->bhqk', q_rope, k_rope)) * scale
        k_ids = jnp.arange(lk)[None, None, :]
        qs = seg_id[:, :, None]
        good = (k_ids <= qs) & (k_ids >= qs - LOOKBACK)
        scores = jnp.where(good[:, None, :, :], scores, NEG)
        attn = jax.nn.softmax(scores, axis=-1)
        out = jnp.einsum('bhqk,bkhd->bqhd', attn, v).reshape(b, lq, H * HD)
        return out @ W_o

    def _L0_ffn_ref(x, gate_w, up_w, down_w, gate_s, up_s, down_s):
        import jax, jax.numpy as jnp
        import numpy as np
        HIDDEN = 512
        INTER = 1408
        B, S = (2, 512)

        def _ternary(key, shape):
            return jax.random.randint(key, shape, -1, 2).astype(jnp.float32)
        b, s, h = x.shape
        xf = x.reshape(b * s, h)
        g = jnp.einsum('th,ih->ti', xf, gate_w) * gate_s
        u = jnp.einsum('th,ih->ti', xf, up_w) * up_s
        hdn = jax.nn.silu(g) * u
        out = jnp.einsum('ti,hi->th', hdn, down_w) * down_s
        return out.reshape(b, s, -1)
    x = x + _L0_xattn_ref(_layernorm(x, axis=-1), ctx_2048, itok_BxS_0_1023, L0_xattn_W_kvc, L0_xattn_W_dq, L0_xattn_W_uq, L0_xattn_W_qr, L0_xattn_W_uk, L0_xattn_W_kr, L0_xattn_W_uv, L0_xattn_W_o)
    x = x + _L0_ffn_ref(_layernorm(x, axis=-1), L0_ffn_gate_w, L0_ffn_up_w, L0_ffn_down_w, L0_ffn_gate_s, L0_ffn_up_s, L0_ffn_down_s)
    return x

_drawn_inputs = setup_inputs


def setup_inputs(seed=0):
    import zlib

    import numpy as np

    out = dict(_drawn_inputs(seed))
    spreads = {}
    factors = {}
    for name, (base, spread) in spreads.items():
        noise = np.random.default_rng([zlib.crc32(name.encode()), seed]).standard_normal(out[name].shape)
        drawn = base * np.exp(spread * noise) if base else spread * noise
        out[name] = jnp.asarray(drawn.astype(out[name].dtype))
    for name, factor in factors.items():
        out[name] = (out[name] * factor).astype(out[name].dtype)
    return out
```

```python
from contextlib import ExitStack

import concourse.bass as bass
from concourse import mybir

F32 = mybir.dt.float32
F32R = mybir.dt.float32r
I32 = mybir.dt.int32
ALU = mybir.AluOpType
ACT = mybir.ActivationFunctionType
AX = mybir.AxisListType

P = 128
NB, LQ, LK, D = 16, 100, 361, 512
H, HD, R = 16, 128, 64
KVC, QC = 128, 192
LOOKBACK = 8
WIN = LOOKBACK + 1
NEG = -1e30
SCALE = 1.0 / float((HD + R) ** 0.5)
EPS = 1e-5
INTER = 1408
KC = D // P
TOK = NB * LQ

GQ = 14
GR = GQ * WIN
GROUPS = 3
GSTART = (0, 13, 26)
STEP = 40
STEPS = 8
TB = STEP * STEPS
BLOCKS = TOK // TB
BG = STEPS * GROUPS
ALLG = BLOCKS * BG
PERIOD = 5
HH = H // 2
SR = GQ * HH
LT = 80
NLT = TB // LT
ROW = KVC + R
KT = 3
TROWS = KT * P
SLOTS = 6
IC = INTER // P


class Count:

    def __init__(self, per):
        self.per = per

    def __call__(self, b, k):
        return b * self.per + k


def build(nc, a):
    with ExitStack() as whole:
        table = nc.dram_tensor("kv_table", [NB * TROWS, ROW], F32, kind="Internal").ap()
        x1 = nc.dram_tensor("x1_rows", [TOK, D], F32, kind="Internal").ap()
        ps = whole.enter_context(nc.psum_tensor("ps", [P, 8, 512], F32))
        ident = whole.enter_context(nc.sbuf_tensor("ident", [P, P], F32))
        half = whole.enter_context(nc.sbuf_tensor("half", [P, NLT], F32))
        with ExitStack() as attn:
            w = {}
            for name, shape, dt in (
                ("wvo_hi", [P, H, D], F32R), ("wvo_lo", [P, H, D], F32R),
                ("wl_hi", [P, H, P], F32R), ("wl_lo", [P, H, P], F32R), ("wl_2", [P, H, P], F32R),
                ("wr_hi", [P, HH, P], F32R), ("wr_lo", [P, HH, P], F32R), ("wr_2", [P, HH, P], F32R),
                ("wdq_hi", [P, KC, 2 * P], F32R), ("wdq_lo", [P, KC, 2 * P], F32R),
                ("mask", [SR, GR], F32), ("cosq", [GR, PERIOD * GROUPS, R // 2], F32),
                ("sinq", [GR, PERIOD * GROUPS, R], F32), ("idx_all", [GR, ALLG], I32),
                ("neg_all", [SR, ALLG * WIN], F32),
            ):
                w[name] = attn.enter_context(nc.sbuf_tensor(name, shape, dt))
            build_table(nc, a, w, ps, ident, half, table)
            build_weights(nc, a, w, ps)
            build_attention(nc, a, w, ps, ident, half, table, x1)
        build_ffn(nc, a, ps, ident, half, x1)


def build_table(nc, a, w, ps, ident, half, table):
    with ExitStack() as ctx:
        def sb(name, shape, dt=F32):
            return ctx.enter_context(nc.sbuf_tensor(name, shape, dt))

        def sem(name):
            return ctx.enter_context(nc.semaphore(name))

        raw = [sb(f"ctx_raw{i}", [P, KC, TROWS]) for i in range(2)]
        hi = [sb(f"ctx_hi{i}", [P, KC, TROWS], F32R) for i in range(2)]
        lo = [sb(f"ctx_lo{i}", [P, KC, TROWS], F32R) for i in range(2)]
        ksum = [sb(f"ctx_sum{i}", [P, KC]) for i in range(2)]
        part = [sb(f"tab_part{i}", [P, KT, ROW]) for i in range(2)]
        tab = [sb(f"tab{i}", [P, KT, ROW]) for i in range(2)]
        rc = sb("rope_cos", [P, KT, R])
        rs = sb("rope_sin", [P, KT, R])
        cosk = sb("cosk", [P, KT, R // 2])
        sink = sb("sink", [P, KT, R])
        wkvcT = sb("wkvcT", [P, D])
        wkr = sb("wkr", [P, R])
        wkv_raw = sb("wkv_raw", [P, KC, ROW])
        wkv = sb("wkv", [P, KC, 2 * ROW], F32R)
        segp = sb("segp", [GR, ALLG], I32)
        segh = sb("segh", [SR, ALLG], I32)
        base = sb("row_base", [GR, ALLG])
        joff = sb("joff", [GR, 1])
        joff9 = sb("joff9", [SR, WIN])
        segf = sb("segf", [GR, ALLG])
        key = sb("key", [GR, ALLG])
        row = sb("row", [GR, ALLG])
        empty = sb("empty", [GR, ALLG])
        over = sb("over", [GR, ALLG])
        seghf = sb("seghf", [SR, ALLG])
        keyh = sb("keyh", [SR, ALLG, WIN])

        w_in, kr_in, seg_in, rk_in, const_in = (sem(s) for s in ("w_in", "kr_in", "seg_in", "rk_in", "const_in"))
        ctx_in = [sem(f"ctx_in{i}") for i in range(2)]
        fold, fold_ev, wkv_hi, wkv_lo = (sem(s) for s in ("fold", "fold_ev", "wkv_hi", "wkv_lo"))
        pad, sums, mean, ctx_hi, ctx_lo = (sem(s) for s in ("pad", "sums", "mean", "ctx_hi", "ctx_lo"))
        mm, part_ev, tab_sum, rope_c, rope_s, tab_done = (
            sem(s) for s in ("mm", "part_ev", "tab_sum", "rope_c", "rope_s", "tab_done"))
        tab_out = [sem(f"tab_out{i}") for i in range(2)]
        chain = sem("index_chain")

        with nc.Block() as block:
            @block.sync
            def _(sp):
                sp.dma_start(wkvcT[:, :], a["wkvcT"]).then_inc(kr_in, 16)
                sp.dma_start(wkr[:, :], a["wkr"]).then_inc(kr_in, 16)
                sp.dma_start(wkv_raw[:, :, 0:KVC], a["wkvc"]).then_inc(w_in, 16)

                def load(n, i):
                    sp.dma_start(raw[i][:, :, 0:LK], a["ctxT"][bass.ds(n, 1), :, :, :].rearrange("o p c k -> (o p) c k")
                                 ).then_inc(ctx_in[i], 16)

                load(0, 0)
                load(1, 1)
                sp.dma_start(cosk[:, :, :], a["cosk"]).then_inc(rk_in, 16)
                sp.dma_start(sink[:, :, :], a["sink"]).then_inc(rk_in, 16)
                for dst, name in ((segp, "segp"), (segh, "segh"), (base, "row_base"), (joff, "joff"), (joff9, "joff9")):
                    sp.dma_start(dst[:, :], a[name]).then_inc(seg_in, 16)
                sp.dma_start(ident[:, :], a["ident"]).then_inc(const_in, 16)
                sp.dma_start(w["mask"][:, :], a["mask"]).then_inc(const_in, 16)
                sp.dma_start(w["cosq"][:, :, :], a["cosq"]).then_inc(const_in, 16)
                sp.dma_start(w["sinq"][:, :, :], a["sinq"]).then_inc(const_in, 16)
                with sp.Fori(1, NB // 2) as j:
                    for i in range(2):
                        sp.wait_ge(ctx_lo, 2 * j + i - 1)
                        load(2 * j + i, i)
                sp.wait_ge(const_in, 64)

            @block.gpsimd
            def _(pool):
                for i in range(2):
                    pool.memset(raw[i][:, :, LK:TROWS], 0.0).then_inc(pad, 1)
                pool.wait_ge(rk_in, 32)

                def rope(n, i, tgt):
                    pool.wait_ge(tab_sum, n + 1)
                    for hf in range(2):
                        pool.tensor_tensor(rc[:, :, hf * 32:hf * 32 + 32], tab[i][:, :, KVC + 32 * hf:KVC + 32 * hf + 32],
                                           cosk[:, :, :], ALU.mult).then_inc(rope_c, 1)
                        pool.tensor_tensor(rs[:, :, hf * 32:hf * 32 + 32],
                                           tab[i][:, :, KVC + 32 - 32 * hf:KVC + 64 - 32 * hf],
                                           sink[:, :, hf * 32:hf * 32 + 32], ALU.mult).then_inc(rope_s, 1)
                    pool.wait_ge(rope_c, 2 * n + 2)
                    pool.wait_ge(rope_s, 2 * n + 2)
                    pool.tensor_tensor(tab[i][:, :, KVC:ROW], rc[:, :, :], rs[:, :, :], ALU.add).then_inc(tab_done, 1)
                    pool.wait_ge(tab_done, n + 1)
                    pool.dma_start(tgt, tab[i][:, :, :]).then_inc(tab_out[i], 16)

                rows = table.rearrange("(b t p) c -> b p t c", t=KT, p=P)
                with pool.Fori(0, NB // 2) as j:
                    for i in range(2):
                        rope(2 * j + i, i, rows[bass.ds(2 * j + i, 1), :, :, :].rearrange("o p t c -> (o p) t c"))
                for i in range(2):
                    pool.wait_ge(tab_out[i], 16 * (NB // 2))

            @block.scalar
            def _(act):
                act.wait_ge(fold, 1)
                act.activation(wkv_raw[:, :, KVC:ROW], ps[:, 7, 0:KC * R].rearrange("p (c r) -> p c r", c=KC),
                               ACT.Copy).then_inc(fold_ev, 1)
                act.wait_ge(fold_ev, 1)
                act.wait_ge(w_in, 16)
                act.activation(wkv[:, :, 0:ROW], wkv_raw[:, :, :], ACT.Copy).then_inc(wkv_hi, 1)
                act.wait_ge(pad, 2)

                def split_hi(n, j, i):
                    act.wait_ge(ctx_in[i], 16 * (j + 1))
                    act.wait_ge(mm, n - 1) if not (isinstance(n, int) and n < 2) else None
                    for c in range(KC):
                        act.activation(hi[i][:, c, 0:LK], raw[i][:, c, 0:LK], ACT.Copy,
                                       accum_out=ksum[i][:, c:c + 1]).then_inc(sums, 1)
                    act.wait_ge(sums, KC * (n + 1))
                    act.activation(raw[i][:, :, LK:LK + 1], ksum[i][:, :].rearrange("p (c o) -> p c o", o=1),
                                   ACT.Copy, scale=1.0 / LK).then_inc(mean, 1)
                    act.wait_ge(mean, n + 1)
                    act.activation(hi[i][:, :, LK:TROWS], raw[i][:, :, LK:TROWS], ACT.Copy).then_inc(ctx_hi, 1)

                def take_part(n, i):
                    act.wait_ge(mm, n + 1)
                    act.activation(part[i][:, :, :], ps[:, 3 * i:3 * i + 3, ROW:2 * ROW], ACT.Copy).then_inc(part_ev, 1)

                split_hi(0, 0, 0)
                split_hi(1, 0, 1)
                take_part(0, 0)
                with act.Fori(1, NB // 2) as j:
                    split_hi(2 * j, j, 0)
                    take_part(2 * j - 1, 1)
                    split_hi(2 * j + 1, j, 1)
                    take_part(2 * j, 0)
                take_part(NB - 1, 1)

            @block.vector
            def _(dve):
                dve.wait_ge(wkv_hi, 1)
                dve.tensor_tensor(wkv[:, :, ROW:2 * ROW], wkv_raw[:, :, :], wkv[:, :, 0:ROW].bitcast(F32),
                                  ALU.subtract).then_inc(wkv_lo, 1)

                def split_lo(n, i):
                    dve.wait_ge(ctx_hi, n + 1)
                    dve.tensor_tensor(lo[i][:, :, :], raw[i][:, :, :], hi[i][:, :, :].bitcast(F32),
                                      ALU.subtract).then_inc(ctx_lo, 1)

                def add_parts(n, j, i):
                    dve.wait_ge(part_ev, n + 1)
                    if not isinstance(j, int) or j > 0:
                        dve.wait_ge(tab_out[i], 16 * j)
                    dve.tensor_tensor(tab[i][:, :, :], ps[:, 3 * i:3 * i + 3, 0:ROW], part[i][:, :, :],
                                      ALU.add).then_inc(tab_sum, 1)

                split_lo(0, 0)
                split_lo(1, 1)
                add_parts(0, 0, 0)
                with dve.Fori(1, NB // 2) as j:
                    split_lo(2 * j, 0)
                    add_parts(2 * j - 1, j - 1, 1)
                    split_lo(2 * j + 1, 1)
                    add_parts(2 * j, j, 0)
                add_parts(NB - 1, NB // 2 - 1, 1)

                done = [0]

                def link(ins):
                    done[0] += 1
                    ins.then_inc(chain, 1)
                    dve.wait_ge(chain, done[0])

                dve.wait_ge(seg_in, 80)
                link(dve.tensor_copy(segf[:, :], segp[:, :]))
                link(dve.tensor_scalar(key[:, :], segf[:, :], joff[:, 0:1], 0.0, ALU.add, ALU.max))
                link(dve.tensor_scalar(key[:, :], key[:, :], float(LK - 1), None, ALU.min))
                link(dve.tensor_tensor(row[:, :], key[:, :], base[:, :], ALU.add))
                link(dve.tensor_scalar(empty[:, :], segf[:, :], 0.0, None, ALU.is_lt))
                link(dve.tensor_scalar(over[:, :], segf[:, :], float(LK - 1 + LOOKBACK), None, ALU.is_gt))
                link(dve.tensor_tensor(empty[:, :], empty[:, :], over[:, :], ALU.add))
                link(dve.tensor_scalar(key[:, :], key[:, :], -1.0, float(LK), ALU.mult, ALU.add))
                link(dve.tensor_tensor(key[:, :], key[:, :], empty[:, :], ALU.mult))
                link(dve.tensor_tensor(row[:, :], row[:, :], key[:, :], ALU.add))
                link(dve.tensor_copy(w["idx_all"][:, :], row[:, :]))
                link(dve.tensor_copy(seghf[:, :], segh[:, :]))
                neg = w["neg_all"][:, :].rearrange("p (g j) -> p g j", j=WIN)
                link(dve.tensor_tensor(keyh[:, :, :], seghf[:, :].unsqueeze(2).to_broadcast([SR, ALLG, WIN]),
                                       joff9[:, :].unsqueeze(1).to_broadcast([SR, ALLG, WIN]), ALU.add))
                link(dve.tensor_scalar(neg, keyh[:, :, :], 0.0, float(LK - 1), ALU.max, ALU.min))
                link(dve.tensor_tensor(neg, neg, keyh[:, :, :], ALU.not_equal))
                link(dve.tensor_scalar(neg, neg, NEG, None, ALU.mult))

            @block.tensor
            def _(pe):
                pe.wait_ge(kr_in, 32)
                for c in range(KC):
                    last = pe.matmul(ps[:, 7, c * R:(c + 1) * R], wkvcT[:, c * P:(c + 1) * P], wkr[:, :],
                                     start=True, stop=True)
                last.then_inc(fold, 1)
                pe.wait_ge(wkv_lo, 1)

                def rows_of(n, i):
                    pe.wait_ge(ctx_hi, n + 1)
                    if not isinstance(n, int) or n >= 2:
                        pe.wait_ge(tab_sum, n - 1)

                    def high(t, c):
                        return pe.matmul(ps[:, 3 * i + t, 0:2 * ROW], hi[i][:, c, t * P:(t + 1) * P],
                                         wkv[:, c, :], start=(c == 0), stop=(c == KC - 1),
                                         skip_group_check=True)

                    for t in range(KT):
                        for c in range(KC - 1):
                            high(t, c)
                    pe.wait_ge(ctx_lo, n + 1)
                    for t in range(KT):
                        for c in range(KC):
                            pe.matmul(ps[:, 3 * i + t, 0:ROW], lo[i][:, c, t * P:(t + 1) * P],
                                      wkv[:, c, 0:ROW], start=False, stop=False, skip_group_check=True)
                        last = high(t, KC - 1)
                    last.then_inc(mm, 1)

                rows_of(0, 0)
                rows_of(1, 1)
                with pe.Fori(1, NB // 2) as j:
                    rows_of(2 * j, 0)
                    rows_of(2 * j + 1, 1)


def build_weights(nc, a, w, ps):
    with ExitStack() as ctx:
        def sb(name, shape, dt=F32):
            return ctx.enter_context(nc.sbuf_tensor(name, shape, dt))

        def sem(name):
            return ctx.enter_context(nc.semaphore(name))

        NWO = 6
        wuqT = sb("wuqT", [P, H, 2 * P])
        wukT = sb("wukT", [P, H, P])
        wuvT = sb("wuvT", [P, H, P])
        wqr1 = sb("wqr1", [P, HH, P])
        wqr2 = sb("wqr2", [P, HH, P])
        wdq = sb("wdq", [P, KC, 2 * P])
        wo = [sb(f"wo{i}", [P, D]) for i in range(NWO)]
        uq_in, uv_in, qr_in, dq_in = (sem(s) for s in ("uq_in", "uv_in", "qr_in", "dq_in"))
        wo_in = [sem(f"wo_in{i}") for i in range(NWO)]
        f_mm, f_hi, f_lo, r_hi, v_mm, v_hi, v_lo, r_lo = (
            sem(s) for s in ("f_mm", "f_hi", "f_lo", "r_hi", "v_mm", "v_hi", "v_lo", "r_lo"))

        with nc.Block() as block:
            @block.sync
            def _(sp):
                sp.dma_start(wukT[:, :, :], a["wukT"]).then_inc(uq_in, 16)
                sp.dma_start(wuqT[:, :, :], a["wuqT"]).then_inc(uq_in, 16)
                sp.dma_start(wuvT[:, :, :], a["wuvT"]).then_inc(uv_in, 16)
                for h in range(H):
                    if h >= NWO:
                        sp.wait_ge(v_mm, h - NWO + 1)
                    sp.dma_start(wo[h % NWO][:, :], a["wo"][h]).then_inc(wo_in[h % NWO], 16)
                    if h == 3:
                        sp.dma_start(wqr1[:, :, :], a["wqr1"]).then_inc(qr_in, 16)
                        sp.dma_start(wqr2[:, :, :], a["wqr2"]).then_inc(qr_in, 16)
                        sp.dma_start(wdq[:, :, :], a["wdq"]).then_inc(dq_in, 16)

            @block.tensor
            def _(pe):
                pe.wait_ge(uq_in, 32)
                for r in range(H // 4):
                    if r >= 2:
                        pe.wait_ge(f_lo, 2 * r - 2)
                    for part in range(2):
                        for h in range(4 * r, 4 * r + 4):
                            last = pe.matmul(ps[:, 2 * (r % 2) + part, (h % 4) * P:(h % 4 + 1) * P],
                                             wuqT[:, h, part * P:(part + 1) * P], wukT[:, h, :],
                                             start=True, stop=True)
                        last.then_inc(f_mm, 1)
                pe.wait_ge(uv_in, 16)
                for h in range(H):
                    pe.wait_ge(wo_in[h % NWO], 16 * (h // NWO + 1))
                    if h >= 4:
                        pe.wait_ge(v_lo, h - 3)
                    pe.matmul(ps[:, 4 + h % 4, :], wuvT[:, h, :], wo[h % NWO][:, :],
                              start=True, stop=True).then_inc(v_mm, 1)

            @block.scalar
            def _(act):
                for r in range(H // 4):
                    for part, dst in enumerate((w["wl_hi"], w["wl_2"])):
                        act.wait_ge(f_mm, 2 * r + part + 1)
                        act.activation(dst[:, 4 * r:4 * r + 4, :],
                                       ps[:, 2 * (r % 2) + part, :].rearrange("p (h c) -> p h c", h=4),
                                       ACT.Copy).then_inc(f_hi, 1)
                for h in range(H):
                    act.wait_ge(v_mm, h + 1)
                    act.activation(w["wvo_hi"][:, h, :], ps[:, 4 + h % 4, :], ACT.Copy).then_inc(v_hi, 1)
                act.wait_ge(qr_in, 32)
                act.activation(w["wr_hi"][:, :, :], wqr1[:, :, :], ACT.Copy).then_inc(r_hi, 1)
                act.activation(w["wr_2"][:, :, :], wqr2[:, :, :], ACT.Copy).then_inc(r_hi, 1)
                act.wait_ge(dq_in, 16)
                act.activation(w["wdq_hi"][:, :, :], wdq[:, :, :], ACT.Copy).then_inc(r_hi, 1)

            @block.vector
            def _(dve):
                for r in range(H // 4):
                    b = 2 * (r % 2)
                    hs = slice(4 * r, 4 * r + 4)
                    dve.wait_ge(f_hi, 2 * r + 1)
                    dve.tensor_tensor(w["wl_lo"][:, hs, :], ps[:, b, :].rearrange("p (h c) -> p h c", h=4),
                                      w["wl_hi"][:, hs, :].bitcast(F32), ALU.subtract).then_inc(f_lo, 1)
                    dve.wait_ge(f_hi, 2 * r + 2)
                    dve.tensor_tensor(w["wl_2"][64:P, hs, :],
                                      ps[64:P, b + 1, :].rearrange("p (h c) -> p h c", h=4),
                                      w["wl_2"][64:P, hs, :].bitcast(F32), ALU.subtract).then_inc(f_lo, 1)
                for h in range(H):
                    dve.wait_ge(v_hi, h + 1)
                    dve.tensor_tensor(w["wvo_lo"][:, h, :], ps[:, 4 + h % 4, :],
                                      w["wvo_hi"][:, h, :].bitcast(F32), ALU.subtract).then_inc(v_lo, 1)
                dve.wait_ge(r_hi, 1)
                dve.tensor_tensor(w["wr_lo"][:, :, :], wqr1[:, :, :], w["wr_hi"][:, :, :].bitcast(F32),
                                  ALU.subtract).then_inc(r_lo, 1)
                dve.wait_ge(r_hi, 2)
                dve.tensor_tensor(w["wr_2"][64:P, :, :], wqr2[64:P, :, :], w["wr_2"][64:P, :, :].bitcast(F32),
                                  ALU.subtract).then_inc(r_lo, 1)
                dve.wait_ge(r_hi, 3)
                dve.tensor_tensor(w["wdq_lo"][:, :, :], wdq[:, :, :], w["wdq_hi"][:, :, :].bitcast(F32),
                                  ALU.subtract).then_inc(r_lo, 1)


class NormStage:

    def __init__(self, tag, sem, rows, scratch, t_hi, t_lo, ps, banks, ident, half):
        self.rows, self.t_hi, self.t_lo, self.ps, self.banks = rows, t_hi, t_lo, ps, banks
        self.st, self.mv, self.var, self.rstd, self.xn = scratch
        self.ident, self.half = ident, half
        self.stats, self.aggr, self.var_ok, self.rstd_ok, self.xn_ok, self.turned, self.hi_ok, self.lo_ok = (
            sem(f"{tag}_{s}") for s in ("stats", "aggr", "var", "rstd", "xn", "turned", "hi", "lo"))
        self.c4, self.c1 = Count(NLT), Count(1)

    def vector(self, dve, b):
        c4, c1 = self.c4, self.c1
        for t in range(NLT):
            dve.bn_stats(self.st[:, t, :], self.rows[:, t, :]).then_inc(self.stats, 1)
        dve.wait_ge(self.stats, c4(b, NLT))
        dve.memset(self.half[0:LT, :], -0.5)
        for t in range(NLT):
            dve.bn_aggr(self.mv[:, t, :], self.st[:, t, :]).then_inc(self.aggr, 1)
        dve.wait_ge(self.aggr, c4(b, NLT))
        dve.tensor_scalar(self.var[:, :], self.mv[:, :, 1], EPS, None, ALU.add).then_inc(self.var_ok, 1)
        dve.wait_ge(self.rstd_ok, c1(b, 1))

        def normalise(t):
            if t >= 2:
                dve.wait_ge(self.turned, c4(b, t - 1))
            dve.tensor_scalar(self.xn[:, t % 2, :], self.rows[:, t, :], self.mv[:, t, 0:1],
                              self.rstd[:, t:t + 1], ALU.subtract, ALU.mult).then_inc(self.xn_ok, 1)

        def low(t):
            dve.wait_ge(self.hi_ok, c4(b, t + 1))
            cols = slice(t * LT, (t + 1) * LT)
            dve.tensor_tensor(self.t_lo[:, :, cols],
                              self.ps[:, self.banks[t % 2], 0:KC * LT].rearrange("p (c t) -> p c t", c=KC),
                              self.t_hi[:, :, cols].bitcast(F32), ALU.subtract).then_inc(self.lo_ok, 1)

        normalise(0)
        for t in range(NLT):
            if t + 1 < NLT:
                normalise(t + 1)
            low(t)

    def gpsimd(self, pool, b):
        pool.wait_ge(self.var_ok, self.c1(b, 1))
        pool.tensor_tensor(self.rstd[:, :], self.var[:, :], self.half[0:LT, :], ALU.pow).then_inc(self.rstd_ok, 1)

    def tensor(self, pe, b):
        for t in range(NLT):
            pe.wait_ge(self.xn_ok, self.c4(b, t + 1))
            if t >= 2:
                pe.wait_ge(self.lo_ok, self.c4(b, t - 1))
            for c in range(KC):
                last = pe.transpose(self.ps[:, self.banks[t % 2], c * LT:(c + 1) * LT],
                                    self.xn[:, t % 2, c * P:(c + 1) * P], self.ident[0:LT, 0:LT])
            last.then_inc(self.turned, 1)

    def scalar(self, act, b):
        for t in range(NLT):
            act.wait_ge(self.turned, self.c4(b, t + 1))
            act.activation(self.t_hi[:, :, t * LT:(t + 1) * LT],
                           self.ps[:, self.banks[t % 2], 0:KC * LT].rearrange("p (c t) -> p c t", c=KC),
                           ACT.Copy).then_inc(self.hi_ok, 1)


def build_attention(nc, a, w, ps, ident, half, table, x1):
    with ExitStack() as ctx:
        def sb(name, shape, dt=F32, stack=ctx):
            return stack.enter_context(nc.sbuf_tensor(name, shape, dt))

        def sem(name):
            return ctx.enter_context(nc.semaphore(name))

        q_lat = sb("q_lat", [P, 2, TB, HH])
        q_rope = sb("q_rope", [P, TB, HH])
        xt = sb("x_rows", [LT, NLT, D])
        kvg = sb("gathered", [GR, SLOTS, GROUPS, ROW])
        ktn = [sb(f"key_latT{i}", [P, GROUPS * GR]) for i in range(2)]
        ktr = [sb(f"key_ropeT{i}", [P, 2, GROUPS * GR]) for i in range(2)]
        idx = sb("idx", [GR, BG], I32)
        neg = sb("neg", [SR, BG * WIN])
        st = (sb("ln_stats", [LT, NLT, 6]), sb("ln_mv", [LT, NLT, 2]), sb("ln_var", [LT, NLT]),
              sb("ln_rstd", [LT, NLT]))
        with ExitStack() as s1:
            xn = sb("xn", [LT, 2, D], stack=s1)
            xT_hi, xT_lo = (sb(f"xT_{s}", [P, KC, TB], F32R, stack=s1) for s in ("hi", "lo"))
            qc_hi, qc_lo, q2_hi, q2_lo = (sb(s, [P, TB], F32R, stack=s1)
                                          for s in ("qc_hi", "qc_lo", "q2_hi", "q2_lo"))
        with ExitStack() as s2:
            rot = [sb(f"rot{i}", [GR, GROUPS, R], stack=s2) for i in range(2)]
            rc = sb("rot_c", [GR, GROUPS, R], stack=s2)
            rs = sb("rot_s", [GR, GROUPS, R], stack=s2)
            sm = sb("score_masked", [SR, 2, GROUPS * GR], stack=s2)
            sc = sb("score", [SR, 2 * GROUPS, WIN], stack=s2)
            sa = sb("score_scaled", [SR, 2 * GROUPS, WIN], stack=s2)
            mx = sb("score_max", [SR, 2 * GROUPS], stack=s2)
            sd = [sb(f"score_shift{i}", [SR, 2 * GROUPS, WIN], stack=s2) for i in range(2)]
            ex = [sb(f"score_exp{i}", [SR, 2 * GROUPS, WIN], stack=s2) for i in range(2)]
            tot = sb("exp_sum", [SR, 2 * GROUPS], stack=s2)
            inv = sb("exp_inv", [SR, 2 * GROUPS], stack=s2)
            pn = sb("prob", [SR, 2 * GROUPS, WIN], stack=s2)
            pf = [sb(f"prob_wide{i}", [SR, 2 * GROUPS, GR], stack=s2) for i in range(2)]
            pt = [sb(f"probT{i}", [GR, GROUPS * 2 * SR], stack=s2) for i in range(2)]
        with ExitStack() as s3:
            o_hi = [sb(f"o_hi{i}", [P, TB], F32R, stack=s3) for i in range(2)]
            o_lo = [sb(f"o_lo{i}", [P, TB], F32R, stack=s3) for i in range(2)]
            oT = sb("oT", [P, KC, TB], stack=s3)
        ctx.enter_context(nc.sbuf_tensor("shared_space", [P, 6200], F32))

        zeros = sem("zeros")
        ln = NormStage("lnq", sem, xt, (*st, xn), xT_hi, xT_lo, ps, (2, 3), ident, half)
        x_in, x_out, x1_ok = sem("x_in"), sem("x1_out"), sem("x1_ok")
        qc_mm, qc_hi_ok, qc_lo_ok, q_mm, q_act, q_dve = (
            sem(s) for s in ("qc_mm", "qc_hi_ok", "qc_lo_ok", "q_mm", "q_act", "q_dve"))
        idx_ok, neg_ok, rot_c, rot_s, rot_ok = (sem(s) for s in ("idx_ok", "neg_ok", "rot_cos", "rot_sin", "rot_ok"))
        gath = [sem(f"gathered{i}") for i in range(SLOTS)]
        t_mm, t_ev, s_mm, s_mul, s_red, s_scl, s_max, s_sub, s_exp, s_sum, s_inv, s_pn, pf_ok = (
            sem(s) for s in ("t_mm", "t_ev", "s_mm", "s_mul", "s_red", "s_scl", "s_max", "s_sub", "s_exp",
                             "s_sum", "s_inv", "s_pn", "pf_ok"))
        p_mm, p_ev, av_mm, lat_ev = (sem(s) for s in ("p_mm", "p_ev", "av_mm", "lat_ev"))
        oh_ok, ol_ok, o_mm, oT_act, oT_dve, bt_mm = (
            sem(s) for s in ("oh_ok", "ol_ok", "o_mm", "oT_act", "oT_dve", "bt_mm"))

        c1, c2, c8, c16, c12, c24 = (Count(n) for n in (1, 2, STEPS, 16, 12, 24))
        slot_uses = [len(range(i, STEPS, SLOTS)) for i in range(SLOTS)]

        def gathered(b, s):
            i = s % SLOTS
            return b * (16 * GROUPS * slot_uses[i]) + 16 * GROUPS * (s // SLOTS + 1)

        q_out = [("lat", h) for h in range(H)] + [("rope", h) for h in range(HH)]
        q_bank = [4 + (o + 2) % 4 for o in range(len(q_out))]

        with nc.Block() as block:
            @block.sync
            def _(sp):
                with sp.Fori(0, BLOCKS) as b:
                    sp.wait_ge(x_out, 16 * NLT * b)
                    sp.dma_start(xt[:, :, :], a["x"][bass.ds(b * TB, TB), :].rearrange("(t p) d -> p t d", p=LT)
                                 ).then_inc(x_in, 16)
                    for t in range(NLT):
                        sp.wait_ge(x1_ok, Count(NLT)(b, t + 1))
                        sp.dma_start(x1[bass.ds(b * TB + t * LT, LT), :], xt[:, t, :]).then_inc(x_out, 16)
                sp.wait_ge(x_out, 16 * NLT * BLOCKS)

            @block.gpsimd
            def _(pool):
                for i in range(2):
                    pool.memset(ktr[i][0:64, 1, :], 0.0).then_inc(zeros, 1)
                    pool.memset(ktr[i][64:P, 0, :], 0.0).then_inc(zeros, 1)
                pool.wait_ge(zeros, 4)
                with pool.Fori(0, BLOCKS) as b:
                    ln.gpsimd(pool, b)
                    pool.wait_ge(av_mm, c8(b, 0))
                    pool.wait_ge(s_scl, c8(b, 0))
                    pool.tensor_copy(idx[:, :], w["idx_all"][:, bass.ds(b * BG, BG)]).then_inc(idx_ok, 1)
                    pool.tensor_copy(neg[:, :], w["neg_all"][:, bass.ds(b * BG * WIN, BG * WIN)]).then_inc(neg_ok, 1)

                    def gather(s):
                        pool.wait_ge(zeros, 4)
                        if s >= SLOTS:
                            pool.wait_ge(av_mm, c8(b, s - SLOTS + 1))
                        else:
                            pool.wait_ge(idx_ok, c1(b, 1))
                        for g in range(GROUPS):
                            k = s * GROUPS + g
                            pool.indirect_dma_start(
                                out=kvg[:, s % SLOTS, g, :], out_offset=None, in_=table,
                                in_offset=bass.IndirectOffsetOnAxis(ap=idx[:, k:k + 1], axis=0),
                            ).then_inc(gath[s % SLOTS], 16)

                    def rotate(s):
                        ph = ((b * STEPS + s) % PERIOD) * GROUPS
                        pool.wait_ge(gath[s % SLOTS], gathered(b, s))
                        if s >= 2:
                            pool.wait_ge(t_mm, c8(b, s - 1))
                        if s >= 1:
                            pool.wait_ge(rot_ok, c8(b, s))
                        kr = kvg[:, s % SLOTS, :, KVC:ROW]
                        for hf in range(2):
                            pool.tensor_tensor(rc[:, :, 32 * hf:32 * hf + 32], kr[:, :, 32 * hf:32 * hf + 32],
                                               w["cosq"][:, bass.ds(ph, GROUPS), :], ALU.mult).then_inc(rot_c, 1)
                            pool.tensor_tensor(rs[:, :, 32 * hf:32 * hf + 32], kr[:, :, 32 - 32 * hf:64 - 32 * hf],
                                               w["sinq"][:, bass.ds(ph, GROUPS), 32 * hf:32 * hf + 32],
                                               ALU.mult).then_inc(rot_s, 1)
                        pool.wait_ge(rot_c, c16(b, 2 * s + 2))
                        pool.wait_ge(rot_s, c16(b, 2 * s + 2))
                        pool.tensor_tensor(rot[s % 2][:, :, :], rc[:, :, :], rs[:, :, :], ALU.add).then_inc(rot_ok, 1)

                    gather(0)
                    gather(1)
                    pool.wait_ge(q_mm, c24(b, 24))
                    for s in range(STEPS):
                        rotate(s)
                        if s + 2 < STEPS:
                            gather(s + 2)

            @block.tensor
            def _(pe):
                pe.wait_ge(zeros, 4)
                with pe.Fori(0, BLOCKS) as b:
                    ln.tensor(pe, b)
                    pe.wait_ge(ln.lo_ok, Count(NLT)(b, NLT))
                    for m in range(2):
                        n = 0
                        for wt, xs in (("wdq_hi", xT_hi), ("wdq_hi", xT_lo), ("wdq_lo", xT_hi)):
                            for c in range(KC):
                                last = pe.matmul(ps[:, 4 + m, 0:TB], w[wt][:, c, m * P:(m + 1) * P], xs[:, c, :],
                                                 start=(n == 0), stop=(n == 3 * KC - 1))
                                n += 1
                        last.then_inc(qc_mm, 1)
                    pe.wait_ge(qc_lo_ok, c2(b, 2))
                    for o, (kind, h) in enumerate(q_out):
                        if o >= 4:
                            e = (o - 4) // 2 + 1
                            pe.wait_ge(q_dve if o % 2 else q_act, c12(b, e))
                        v = "wl" if kind == "lat" else "wr"
                        parts = ((f"{v}_hi", qc_hi), (f"{v}_hi", qc_lo), (f"{v}_lo", qc_hi),
                                 (f"{v}_2", q2_hi), (f"{v}_2", q2_lo))
                        for n, (wt, xs) in enumerate(parts):
                            last = pe.matmul(ps[:, q_bank[o], 0:TB], w[wt][:, h, :], xs[:, :],
                                             start=(n == 0), stop=(n == len(parts) - 1))
                        last.then_inc(q_mm, 1)

                    def turn_keys(s):
                        pe.wait_ge(rot_ok, c8(b, s + 1))
                        if s >= 1:
                            pe.wait_ge(t_ev, c8(b, s))
                        for g in range(GROUPS):
                            pe.transpose(ps[:, 2, g * GR:(g + 1) * GR], kvg[:, s % SLOTS, g, 0:KVC],
                                         ident[0:GR, 0:GR])
                        for g in range(GROUPS):
                            last = pe.transpose(ps[0:R, 3, g * GR:(g + 1) * GR], rot[s % 2][:, g, :],
                                                ident[0:GR, 0:GR])
                        last.then_inc(t_mm, 1)

                    def scores(s):
                        pe.wait_ge(t_ev, c8(b, s + 1))
                        if s == 0:
                            pe.wait_ge(q_act, c12(b, 12))
                            pe.wait_ge(q_dve, c12(b, 12))
                        else:
                            pe.wait_ge(s_mul, c16(b, 2 * s))
                        for e in range(2):
                            for g in range(GROUPS):
                                out = ps[0:SR, e, g * GR:(g + 1) * GR]
                                q0 = s * STEP + GSTART[g]
                                pe.matmul(out, q_lat[:, e, q0:q0 + GQ, :].rearrange("p q i -> p (q i)"), ktn[s % 2][:, g * GR:(g + 1) * GR],
                                          start=True, stop=False)
                                last = pe.matmul(out, q_rope[:, q0:q0 + GQ, :].rearrange("p q i -> p (q i)"),
                                                 ktr[s % 2][:, e, g * GR:(g + 1) * GR], start=False, stop=True)
                        last.then_inc(s_mm, 1)

                    def turn_probs(s):
                        pe.wait_ge(pf_ok, c8(b, s + 1))
                        if s >= 1:
                            pe.wait_ge(p_ev, c16(b, 2 * s))
                        for g in range(GROUPS):
                            for e in range(2):
                                at = (g % 2) * 2 * SR + e * SR
                                last = pe.transpose(ps[0:GR, 4 + g // 2, at:at + SR],
                                                    pf[s % 2][:, e * GROUPS + g, :], ident[0:SR, 0:SR])
                        last.then_inc(p_mm, 1)

                    def values(s):
                        pe.wait_ge(p_ev, c16(b, 2 * s + 2))
                        if s >= 1:
                            pe.wait_ge(lat_ev, c24(b, 3 * s))
                        for g in range(GROUPS):
                            at = (g % 2) * 2 * SR
                            last = pe.matmul(ps[:, 6 + g // 2, at:at + 2 * SR], kvg[:, s % SLOTS, g, 0:KVC],
                                             pt[s % 2][:, g * 2 * SR:(g + 1) * 2 * SR], start=True, stop=True)
                        last.then_inc(av_mm, 1)

                    turn_keys(0)
                    turn_keys(1)
                    scores(0)
                    turn_keys(2)
                    scores(1)
                    for s in range(STEPS):
                        if s + 3 < STEPS:
                            turn_keys(s + 3)
                        if s + 2 < STEPS:
                            scores(s + 2)
                        turn_probs(s)
                        values(s)

                    for h in range(H):
                        pe.wait_ge(ol_ok, c16(b, h + 1))
                        for m in range(KC):
                            cols = slice(m * P, (m + 1) * P)
                            parts = (("wvo_hi", o_hi), ("wvo_hi", o_lo), ("wvo_lo", o_hi))
                            for n, (wt, xs) in enumerate(parts):
                                last = pe.matmul(ps[:, 4 + m, 0:TB], w[wt][:, h, cols], xs[h % 2][:, :],
                                                 start=(h == 0 and n == 0), stop=(h == H - 1 and n == 2))
                        last.then_inc(o_mm, 1)
                    pe.wait_ge(oT_act, c2(b, 2))
                    pe.wait_ge(oT_dve, c2(b, 2))
                    for t in range(NLT):
                        for c in range(KC):
                            last = pe.transpose(ps[0:LT, t, c * P:(c + 1) * P], oT[:, c, t * LT:(t + 1) * LT],
                                                ident[:, :])
                        last.then_inc(bt_mm, 1)

            @block.scalar
            def _(act):
                with act.Fori(0, BLOCKS) as b:
                    ln.scalar(act, b)
                    for m, dst in enumerate((qc_hi, q2_hi)):
                        act.wait_ge(qc_mm, c2(b, m + 1))
                        act.activation(dst[:, :], ps[:, 4 + m, 0:TB], ACT.Copy).then_inc(qc_hi_ok, 1)
                    for o, (kind, h) in enumerate(q_out):
                        if o % 2 == 0:
                            act.wait_ge(q_mm, c24(b, o + 1))
                            dst = q_lat[:, h % 2, :, h // 2] if kind == "lat" else q_rope[:, :, h]
                            act.activation(dst, ps[:, q_bank[o], 0:TB], ACT.Copy).then_inc(q_act, 1)

                    def take_keys(s):
                        act.wait_ge(t_mm, c8(b, s + 1))
                        if s >= 2:
                            act.wait_ge(s_mm, c8(b, s - 1))
                        act.activation(ktn[s % 2][:, :], ps[:, 2, 0:GROUPS * GR], ACT.Copy)
                        act.activation(ktr[s % 2][0:R, 0, :], ps[0:R, 3, 0:GROUPS * GR], ACT.Copy)
                        act.activation(ktr[s % 2][R:P, 1, :], ps[0:R, 3, 0:GROUPS * GR], ACT.Copy).then_inc(t_ev, 1)

                    def exps(s):
                        act.wait_ge(s_sub, c8(b, s + 1))
                        act.activation(ex[s % 2][:, :, :], sd[s % 2][:, :, :], ACT.Exp).then_inc(s_exp, 1)

                    def take_probs(s):
                        act.wait_ge(p_mm, c8(b, s + 1))
                        act.activation(pt[s % 2][:, 0:4 * SR], ps[0:GR, 4, 0:4 * SR], ACT.Copy).then_inc(p_ev, 1)
                        act.activation(pt[s % 2][:, 4 * SR:6 * SR], ps[0:GR, 5, 0:2 * SR], ACT.Copy).then_inc(p_ev, 1)

                    def take_values(s):
                        act.wait_ge(av_mm, c8(b, s + 1))
                        for g in range(GROUPS):
                            q0 = s * STEP + GSTART[g]
                            at = (g % 2) * 2 * SR
                            if g:
                                act.wait_ge(lat_ev, c24(b, 3 * s + g))
                            act.activation(
                                q_lat[:, :, q0:q0 + GQ, :].rearrange("p e q i -> p e (q i)"),
                                ps[:, 6 + g // 2, at:at + 2 * SR].rearrange("p (e r) -> p e r", e=2),
                                ACT.Copy).then_inc(lat_ev, 1)

                    take_keys(0)
                    take_keys(1)
                    exps(0)
                    take_keys(2)
                    for s in range(STEPS):
                        if s + 3 < STEPS:
                            take_keys(s + 3)
                        if s + 1 < STEPS:
                            exps(s + 1)
                        take_probs(s)
                        take_values(s)

                    act.wait_ge(lat_ev, c24(b, 24))
                    for h in range(H):
                        if h >= 2:
                            act.wait_ge(o_mm, c16(b, h - 1))
                        act.activation(o_hi[h % 2][:, :], q_lat[:, h % 2, :, h // 2], ACT.Copy).then_inc(oh_ok, 1)
                    act.wait_ge(o_mm, c16(b, H))
                    for m in (0, 2):
                        act.activation(oT[:, m, :], ps[:, 4 + m, 0:TB], ACT.Copy).then_inc(oT_act, 1)

            @block.vector
            def _(dve):
                with dve.Fori(0, BLOCKS) as b:
                    dve.wait_ge(x_in, 16 * (b + 1))
                    ln.vector(dve, b)
                    for m, (hi, lo) in enumerate(((qc_hi, qc_lo), (q2_hi, q2_lo))):
                        dve.wait_ge(qc_hi_ok, c2(b, m + 1))
                        dve.tensor_tensor(lo[:, :], ps[:, 4 + m, 0:TB], hi[:, :].bitcast(F32),
                                          ALU.subtract).then_inc(qc_lo_ok, 1)
                    for o, (kind, h) in enumerate(q_out):
                        if o % 2 == 1:
                            dve.wait_ge(q_mm, c24(b, o + 1))
                            dst = q_lat[:, h % 2, :, h // 2] if kind == "lat" else q_rope[:, :, h]
                            dve.tensor_copy(dst, ps[:, q_bank[o], 0:TB]).then_inc(q_dve, 1)
                    dve.wait_ge(neg_ok, c1(b, 1))
                    E = 2 * GROUPS

                    def window(s):
                        dve.wait_ge(s_mm, c8(b, s + 1))
                        for e in range(2):
                            dve.tensor_tensor(sm[:, e, :].rearrange("p (g k) -> p g k", g=GROUPS),
                                              ps[0:SR, e, 0:GROUPS * GR].rearrange("p (g k) -> p g k", g=GROUPS),
                                              w["mask"][:, :].unsqueeze(1).to_broadcast([SR, GROUPS, GR]),
                                              ALU.mult).then_inc(s_mul, 1)
                        dve.wait_ge(s_mul, c16(b, 2 * s + 2))
                        dve.tensor_reduce(sc[:, :, :],
                                          sm[:, :, :].rearrange("p e (g q j) -> p (e g) j q", g=GROUPS, q=GQ),
                                          AX.X, ALU.add).then_inc(s_red, 1)
                        dve.wait_ge(s_red, c8(b, s + 1))
                        n = s * GROUPS * WIN
                        dve.scalar_tensor_tensor(
                            out=sa[:, :, :].rearrange("p (e g) j -> p e (g j)", e=2),
                            in0=sc[:, :, :].rearrange("p (e g) j -> p e (g j)", e=2), scalar=SCALE,
                            in1=neg[:, n:n + GROUPS * WIN].unsqueeze(1).to_broadcast([SR, 2, GROUPS * WIN]),
                            op0=ALU.mult, op1=ALU.add).then_inc(s_scl, 1)
                        dve.wait_ge(s_scl, c8(b, s + 1))
                        dve.tensor_reduce(mx[:, :], sa[:, :, :], AX.X, ALU.max).then_inc(s_max, 1)
                        dve.wait_ge(s_max, c8(b, s + 1))
                        dve.tensor_tensor(sd[s % 2][:, :, :], sa[:, :, :],
                                          mx[:, :].unsqueeze(2).to_broadcast([SR, E, WIN]),
                                          ALU.subtract).then_inc(s_sub, 1)

                    def probs(s):
                        dve.wait_ge(s_exp, c8(b, s + 1))
                        dve.tensor_reduce(tot[:, :], ex[s % 2][:, :, :], AX.X, ALU.add).then_inc(s_sum, 1)
                        dve.wait_ge(s_sum, c8(b, s + 1))
                        dve.reciprocal(inv[:, :], tot[:, :]).then_inc(s_inv, 1)
                        dve.wait_ge(s_inv, c8(b, s + 1))
                        dve.tensor_tensor(pn[:, :, :], ex[s % 2][:, :, :],
                                          inv[:, :].unsqueeze(2).to_broadcast([SR, E, WIN]),
                                          ALU.mult).then_inc(s_pn, 1)
                        dve.wait_ge(s_pn, c8(b, s + 1))
                        if s >= 2:
                            dve.wait_ge(p_mm, c8(b, s - 1))
                        dve.tensor_tensor(
                            pf[s % 2][:, :, :].rearrange("p x (q j) -> p x q j", q=GQ),
                            pn[:, :, :].unsqueeze(2).to_broadcast([SR, E, GQ, WIN]),
                            w["mask"][:, :].rearrange("p (q j) -> p q j", q=GQ).unsqueeze(1)
                            .to_broadcast([SR, E, GQ, WIN]), ALU.mult).then_inc(pf_ok, 1)

                    window(0)
                    for s in range(STEPS):
                        if s + 1 < STEPS:
                            window(s + 1)
                        probs(s)

                    for h in range(H):
                        dve.wait_ge(oh_ok, c16(b, h + 1))
                        dve.tensor_tensor(o_lo[h % 2][:, :], q_lat[:, h % 2, :, h // 2], o_hi[h % 2][:, :].bitcast(F32),
                                          ALU.subtract).then_inc(ol_ok, 1)
                    dve.wait_ge(o_mm, c16(b, H))
                    for m in (1, 3):
                        dve.tensor_copy(oT[:, m, :], ps[:, 4 + m, 0:TB]).then_inc(oT_dve, 1)
                    for t in range(NLT):
                        dve.wait_ge(bt_mm, Count(NLT)(b, t + 1))
                        dve.tensor_tensor(xt[:, t, :], ps[0:LT, t, :], xt[:, t, :], ALU.add).then_inc(x1_ok, 1)


def build_ffn(nc, a, ps, ident, half, x1):
    with ExitStack() as ctx:
        def sb(name, shape, dt=F32):
            return ctx.enter_context(nc.sbuf_tensor(name, shape, dt))

        def sem(name):
            return ctx.enter_context(nc.semaphore(name))

        WR = 2 * KC * P + D
        w_hi = sb("ffn_hi", [P, IC, WR], F32R)
        w_lo = sb("ffn_lo", [P, IC, WR], F32R)
        raw = [sb(f"ffn_raw{i}", [P, WR]) for i in range(2)]
        h_hi = sb("h_hi", [P, IC, TB], F32R)
        h_lo = sb("h_lo", [P, IC, TB], F32R)
        scale = sb("ffn_scale", [P, 2 * IC + KC])
        xt = sb("x1_rows_sb", [LT, NLT, D])
        xn = sb("xn2", [LT, 2, D])
        xT_hi, xT_lo = (sb(f"x1T_{s}", [P, KC, TB], F32R) for s in ("hi", "lo"))
        act_g = [sb(f"silu{i}", [P, TB]) for i in range(2)]
        hf = [sb(f"hidden{i}", [P, TB]) for i in range(2)]
        oT = sb("yT", [P, KC, TB])
        st = (sb("ln2_stats", [LT, NLT, 6]), sb("ln2_mv", [LT, NLT, 2]), sb("ln2_var", [LT, NLT]),
              sb("ln2_rstd", [LT, NLT]))
        w_in = [sem(f"ffn_in{i}") for i in range(2)]
        s_in, x_in, y_out = sem("scale_in"), sem("x1_in"), sem("y_out")
        ln = NormStage("lnf", sem, xt, (*st, xn), xT_hi, xT_lo, ps, (6, 7), ident, half)
        whi_ok, wlo_ok, g_mm, u_mm, silu_ok, hf_ok, hh_ok, hl_ok, d_mm, d_act, d_dve, y_mm, y_ok = (
            sem(s) for s in ("whi_ok", "wlo_ok", "g_mm", "u_mm", "silu_ok", "hf_ok", "hh_ok", "hl_ok", "d_mm",
                             "d_act", "d_dve", "y_mm", "y_ok"))
        cI, cN, c2 = Count(IC), Count(NLT), Count(2)
        out = a["out"]

        with nc.Block() as block:
            @block.sync
            def _(sp):
                def rows(b):
                    sp.dma_start(xt[:, :, :], x1[bass.ds(b * TB, TB), :].rearrange("(t p) d -> p t d", p=LT)
                                 ).then_inc(x_in, 16)

                def results(b):
                    for t in range(NLT):
                        sp.wait_ge(y_ok, cN(b, t + 1))
                        sp.dma_start(out[bass.ds(b * TB + t * LT, LT), :], xt[:, t, :]).then_inc(y_out, 16)

                rows(0)
                sp.dma_start(scale[:, :], a["ffn_scale"]).then_inc(s_in, 16)
                for c in range(IC):
                    if c >= 2:
                        sp.wait_ge(wlo_ok, c - 1)
                    sp.dma_start(raw[c % 2][:, :], a["ffn_w"][c]).then_inc(w_in[c % 2], 16)
                results(0)
                with sp.Fori(1, BLOCKS) as b:
                    sp.wait_ge(y_out, 16 * NLT * b)
                    rows(b)
                    results(b)
                sp.wait_ge(y_out, 16 * NLT * BLOCKS)

            @block.gpsimd
            def _(pool):
                with pool.Fori(0, BLOCKS) as b:
                    ln.gpsimd(pool, b)

            def wt(buf, c, which, k):
                return buf[:, c, which * KC * P + k * P:which * KC * P + (k + 1) * P]

            def down(buf, c, m):
                return buf[:, c, 2 * KC * P + m * P:2 * KC * P + (m + 1) * P]

            @block.tensor
            def _(pe):
                with pe.Fori(0, BLOCKS) as b:
                    ln.tensor(pe, b)
                    pe.wait_ge(ln.lo_ok, cN(b, NLT))
                    for c in range(IC):
                        pe.wait_ge(wlo_ok, c + 1)
                        for which, done in ((0, g_mm), (1, u_mm)):
                            if c >= 2:
                                pe.wait_ge(hf_ok if which else silu_ok, cI(b, c - 1))
                            n = 0
                            for buf, xs in ((w_hi, xT_hi), (w_hi, xT_lo), (w_lo, xT_hi)):
                                for k in range(KC):
                                    last = pe.matmul(ps[:, 2 * which + c % 2, 0:TB], wt(buf, c, which, k),
                                                     xs[:, k, :], start=(n == 0), stop=(n == 3 * KC - 1))
                                    n += 1
                            last.then_inc(done, 1)
                    for m in range(KC):
                        if m >= 2:
                            pe.wait_ge(d_dve if m % 2 else d_act, c2(b, m // 2))
                        n = 0
                        for c in range(IC):
                            if m == 0:
                                pe.wait_ge(hl_ok, cI(b, c + 1))
                            for buf, xs in ((w_hi, h_hi), (w_hi, h_lo), (w_lo, h_hi)):
                                last = pe.matmul(ps[:, 4 + m % 2, 0:TB], down(buf, c, m), xs[:, c, :],
                                                 start=(n == 0), stop=(n == 3 * IC - 1))
                                n += 1
                        last.then_inc(d_mm, 1)
                    pe.wait_ge(d_act, c2(b, 2))
                    pe.wait_ge(d_dve, c2(b, 2))
                    for t in range(NLT):
                        if t >= 2:
                            pe.wait_ge(y_ok, cN(b, t - 1))
                        for k in range(KC):
                            last = pe.transpose(ps[0:LT, 6 + t % 2, k * P:(k + 1) * P],
                                                oT[:, k, t * LT:(t + 1) * LT], ident[:, :])
                        last.then_inc(y_mm, 1)

            @block.scalar
            def _(act):
                def split(c):
                    act.wait_ge(w_in[c % 2], 16 * (c // 2 + 1))
                    act.activation(w_hi[:, c, :], raw[c % 2][:, :], ACT.Copy).then_inc(whi_ok, 1)

                def rest(b, first):
                    def high(c):
                        act.wait_ge(hf_ok, cI(b, c + 1))
                        act.activation(h_hi[:, c, :], hf[c % 2][:, :], ACT.Copy).then_inc(hh_ok, 1)

                    for c in range(IC):
                        act.wait_ge(g_mm, cI(b, c + 1))
                        if c >= 2:
                            act.wait_ge(hf_ok, cI(b, c - 1))
                        act.activation(act_g[c % 2][:, :], ps[:, c % 2, 0:TB], ACT.Silu,
                                       scale=scale[:, c:c + 1]).then_inc(silu_ok, 1)
                        if first and c + 2 < IC:
                            split(c + 2)
                        if c:
                            high(c - 1)
                    high(IC - 1)
                    for m in (0, 2):
                        act.wait_ge(d_mm, Count(KC)(b, m + 1))
                        act.activation(oT[:, m, :], ps[:, 4 + m % 2, 0:TB], ACT.Copy,
                                       scale=scale[:, 2 * IC + m:2 * IC + m + 1]).then_inc(d_act, 1)

                act.wait_ge(s_in, 16)
                split(0)
                split(1)
                ln.scalar(act, 0)
                rest(0, True)
                with act.Fori(1, BLOCKS) as b:
                    ln.scalar(act, b)
                    rest(b, False)

            @block.vector
            def _(dve):
                def split(c):
                    dve.wait_ge(whi_ok, c + 1)
                    dve.tensor_tensor(w_lo[:, c, :], raw[c % 2][:, :], w_hi[:, c, :].bitcast(F32),
                                      ALU.subtract).then_inc(wlo_ok, 1)

                def rest(b, first):
                    def low(c):
                        dve.wait_ge(hh_ok, cI(b, c + 1))
                        dve.tensor_tensor(h_lo[:, c, :], hf[c % 2][:, :], h_hi[:, c, :].bitcast(F32),
                                          ALU.subtract).then_inc(hl_ok, 1)

                    for c in range(IC):
                        dve.wait_ge(u_mm, cI(b, c + 1))
                        dve.wait_ge(silu_ok, cI(b, c + 1))
                        if c >= 2:
                            dve.wait_ge(hl_ok, cI(b, c - 1))
                        dve.scalar_tensor_tensor(out=hf[c % 2][:, :], in0=ps[:, 2 + c % 2, 0:TB],
                                                 scalar=scale[:, IC + c:IC + c + 1], in1=act_g[c % 2][:, :],
                                                 op0=ALU.mult, op1=ALU.mult).then_inc(hf_ok, 1)
                        if first and c + 2 < IC:
                            split(c + 2)
                        if c:
                            low(c - 1)
                    low(IC - 1)
                    for m in (1, 3):
                        dve.wait_ge(d_mm, Count(KC)(b, m + 1))
                        dve.tensor_scalar(oT[:, m, :], ps[:, 4 + m % 2, 0:TB],
                                          scale[:, 2 * IC + m:2 * IC + m + 1], None, ALU.mult).then_inc(d_dve, 1)
                    for t in range(NLT):
                        dve.wait_ge(y_mm, cN(b, t + 1))
                        dve.tensor_tensor(xt[:, t, :], ps[0:LT, 6 + t % 2, :], xt[:, t, :],
                                          ALU.add).then_inc(y_ok, 1)

                dve.wait_ge(s_in, 16)
                split(0)
                split(1)
                dve.wait_ge(x_in, 16)
                ln.vector(dve, 0)
                rest(0, True)
                with dve.Fori(1, BLOCKS) as b:
                    dve.wait_ge(x_in, 16 * (b + 1))
                    ln.vector(dve, b)
                    rest(b, False)


def constants():
    import numpy as np

    f = np.float32
    half = R // 2
    inv_freq = (1.0 / (f(10000.0) ** (np.arange(half, dtype=f) / f(half)))).astype(f)
    ang = np.arange(LK, dtype=f)[:, None] * inv_freq
    cos, sin = np.cos(ang).astype(f), np.sin(ang).astype(f)
    kpos = np.minimum(np.arange(TROWS), LK - 1).reshape(KT, P).T
    first = np.array([s * STEP + g for s in range(TOK // STEP) for g in GSTART])
    tok = first[None, :] + (np.arange(GR) // WIN)[:, None]
    qpos = tok[:, :PERIOD * GROUPS] % LQ
    same = (np.arange(SR) // HH)[:, None] == (np.arange(GR) // WIN)[None, :]
    return tok, first, {
        "ident": np.eye(P, dtype=f),
        "mask": same.astype(f),
        "cosk": cos[kpos], "sink": np.concatenate([-sin[kpos], sin[kpos]], -1),
        "cosq": cos[qpos], "sinq": np.concatenate([sin[qpos], -sin[qpos]], -1),
        "row_base": (tok // LQ * TROWS).astype(f),
        "joff": (np.arange(GR) % WIN - LOOKBACK).astype(f)[:, None],
        "joff9": np.broadcast_to((np.arange(WIN) - LOOKBACK).astype(f), (SR, WIN)),
    }


def kernel(x, ctx_2048, itok_BxS_0_1023, L0_xattn_W_kvc, L0_xattn_W_dq, L0_xattn_W_uq, L0_xattn_W_qr,
           L0_xattn_W_uk, L0_xattn_W_kr, L0_xattn_W_uv, L0_xattn_W_o, L0_ffn_gate_w, L0_ffn_up_w,
           L0_ffn_down_w, L0_ffn_gate_s, L0_ffn_up_s, L0_ffn_down_s):
    import numpy as np
    import concourse.bacc as bacc
    from concourse.bass_utils import run_bass_kernel_spmd

    def twice(m):
        return np.concatenate([m, m[..., P:]], -1)

    tok, first, arrays = constants()
    seg = np.asarray(itok_BxS_0_1023).reshape(TOK)
    arrays["x"] = np.asarray(x).reshape(TOK, D)
    arrays["ctxT"] = np.asarray(ctx_2048).reshape(NB, LK, KC, P).transpose(0, 3, 2, 1)
    arrays["segp"] = seg[tok]
    arrays["segh"] = seg[first[None, :] + (np.arange(SR) // HH)[:, None]]
    arrays["wkvc"] = np.asarray(L0_xattn_W_kvc).reshape(KC, P, KVC).transpose(1, 0, 2)
    arrays["wkvcT"] = np.asarray(L0_xattn_W_kvc).T
    arrays["wkr"] = np.asarray(L0_xattn_W_kr)
    arrays["wdq"] = twice(np.asarray(L0_xattn_W_dq).reshape(KC, P, QC).transpose(1, 0, 2))
    arrays["wuqT"] = twice(np.asarray(L0_xattn_W_uq).reshape(QC, H, HD).transpose(2, 1, 0))
    arrays["wukT"] = np.asarray(L0_xattn_W_uk).reshape(KVC, H, HD).transpose(2, 1, 0)
    arrays["wuvT"] = np.asarray(L0_xattn_W_uv).reshape(KVC, H, HD).transpose(2, 1, 0)
    wqr = np.asarray(L0_xattn_W_qr).reshape(QC, HH, P)
    arrays["wqr1"], arrays["wqr2"] = wqr[:P], np.concatenate([wqr[P:], wqr[P:]])
    arrays["wo"] = np.asarray(L0_xattn_W_o).reshape(H, HD, D)
    gate, up = (np.asarray(m).reshape(IC, P, KC, P).transpose(0, 3, 2, 1).reshape(IC, P, KC * P)
                for m in (L0_ffn_gate_w, L0_ffn_up_w))
    arrays["ffn_w"] = np.concatenate([gate, up, np.asarray(L0_ffn_down_w).T.reshape(IC, P, D)], -1)
    arrays["ffn_scale"] = np.concatenate(
        [np.asarray(m).reshape(-1, P).T for m in (L0_ffn_gate_s, L0_ffn_up_s, L0_ffn_down_s)], -1)

    nc = bacc.Bacc("TRN2", target_bir_lowering=False, num_devices=1)
    aps = {}
    for name in arrays:
        arrays[name] = np.ascontiguousarray(arrays[name])
        aps[name] = nc.dram_tensor(name + "_dram", arrays[name].shape, mybir.dt.from_np(arrays[name].dtype),
                                   kind="ExternalInput").ap()
    aps["out"] = nc.dram_tensor("out_dram", [TOK, D], F32, kind="ExternalOutput").ap()
    build(nc, aps)
    r = run_bass_kernel_spmd(nc, [{name + "_dram": v for name, v in arrays.items()}], core_ids=[0])
    return r.results[0]["out_dram"].reshape(NB, LQ, D)
```

```python
from contextlib import ExitStack

import concourse.bass as bass
from concourse import mybir

F32 = mybir.dt.float32
F32R = mybir.dt.float32r
I32 = mybir.dt.int32
BF16 = mybir.dt.bfloat16
ALU = mybir.AluOpType
ACT = mybir.ActivationFunctionType
AX = mybir.AxisListType

P = 128
NB, LQ, LK, D = 16, 100, 361, 512
H, HD, R = 16, 128, 64
KVC, QC = 128, 192
LOOKBACK = 8
WIN = LOOKBACK + 1
NEG = -1e30
SCALE = 1.0 / float((HD + R) ** 0.5)
EPS = 1e-5
INTER = 1408
KC = D // P
TOK = NB * LQ

GQ = 14
GR = GQ * WIN
GROUPS = 3
GSTART = (0, 13, 26)
STEP = 40
STEPS = 8
TB = STEP * STEPS
BLOCKS = TOK // TB
BG = STEPS * GROUPS
ALLG = BLOCKS * BG
PERIOD = 5
HH = H // 2
SR = GQ * HH
LT = 80
NLT = TB // LT
ROW = KVC + R
KT = 3
TROWS = KT * P
SLOTS = 6
FAR = -2.0 ** 127
IC = INTER // P


class Count:

    def __init__(self, per):
        self.per = per

    def __call__(self, b, k):
        return b * self.per + k


def build(nc, a):
    with ExitStack() as whole:
        table = nc.dram_tensor("kv_table", [NB * TROWS, ROW], F32, kind="Internal").ap()
        x1 = nc.dram_tensor("x1_rows", [TOK, D], F32, kind="Internal").ap()
        ps = whole.enter_context(nc.psum_tensor("ps", [P, 8, 512], F32))
        ident = whole.enter_context(nc.sbuf_tensor("ident", [P, P], F32))
        with ExitStack() as attn:
            w = {}
            for name, shape, dt in (
                ("wvo_hi", [P, H, D], F32R), ("wvo_lo", [P, H, D], F32R),
                ("wl_hi", [P, H, P], F32R), ("wl_lo", [P, H, P], F32R), ("wl_2", [P, H, P], F32R),
                ("wr_hi", [P, H, R], F32R), ("wr_lo", [P, H, R], F32R), ("wr_2", [P, H, R], F32R),
                ("wdq", [P, KC, 2 * P], F32),
                ("mask", [SR, GR], F32), ("other", [P, SR], BF16), ("blocks", [P, GROUPS * GR], BF16),
                ("cosq", [GR, PERIOD * GROUPS, R // 2], F32),
                ("sinq", [GR, PERIOD * GROUPS, R], F32), ("idx_all", [GR, ALLG], I32),
                ("neg_all", [SR, ALLG * WIN], F32),
            ):
                w[name] = attn.enter_context(nc.sbuf_tensor(name, shape, dt))
            build_setup(nc, a, w, ps, ident, table)
            build_attention(nc, a, w, ps, ident, table, x1)
        build_ffn(nc, a, ps, ident, x1)




def build_setup(nc, a, w, ps, ident, table):
    with ExitStack() as ctx:
        def sb(name, shape, dt=F32):
            return ctx.enter_context(nc.sbuf_tensor(name, shape, dt))

        def sem(name):
            return ctx.enter_context(nc.semaphore(name))

        RAWS = 4
        UQ, UK, UV, QR, WO = 0, 2 * P, 3 * P, 4 * P, 5 * P
        HW = WO + D
        raw = [sb(f"ctx_raw{i}", [P, KC, TROWS]) for i in range(RAWS)]
        hi = [sb(f"ctx_hi{i}", [P, KC, TROWS], F32R) for i in range(2)]
        lo = [sb(f"ctx_lo{i}", [P, KC, TROWS], F32R) for i in range(2)]
        ksum = [sb(f"ctx_sum{i}", [P, KC]) for i in range(2)]
        part = [sb(f"tab_part{i}", [P, KT, ROW]) for i in range(2)]
        tab = [sb(f"tab{i}", [P, KT, ROW]) for i in range(2)]
        rc = sb("rope_cos", [P, KT, R])
        rs = sb("rope_sin", [P, KT, R])
        cosk = sb("cosk", [P, KT, R // 2])
        sink = sb("sink", [P, KT, R])
        wkvcT = sb("wkvcT", [P, D])
        wkr = sb("wkr", [P, R])
        wkv_raw = sb("wkv_raw", [P, KC, ROW])
        wkv = sb("wkv", [P, KC, 2 * ROW], F32R)
        hw = [sb(f"head_w{i}", [P, HW]) for i in range(2)]
        segp = sb("segp", [GR, ALLG], I32)
        segh = sb("segh", [SR, ALLG], I32)
        base = sb("row_base", [GR, ALLG])
        joff = sb("joff", [GR, 1])
        joff9 = sb("joff9", [SR, WIN])
        segf = sb("segf", [GR, ALLG])
        key = sb("key", [GR, ALLG])
        empty = sb("empty", [GR, ALLG])
        over = sb("over", [GR, ALLG])
        keyh = sb("keyh", [SR, ALLG, WIN])
        other32 = sb("other32", [P, SR])
        blocks32 = sb("blocks32", [P, GR])

        w_in, kr_in, seg_in, rk_in, const_in, mask_in = (
            sem(s) for s in ("w_in", "kr_in", "seg_in", "rk_in", "const_in", "mask_in"))
        ctx_in = [sem(f"ctx_in{i}") for i in range(RAWS)]
        hw_in = [sem(f"head_in{i}") for i in range(2)]
        fold, fold_ev, wkv_hi, wkv_lo = (sem(s) for s in ("fold", "fold_ev", "wkv_hi", "wkv_lo"))
        pad, sums, mean, ctx_hi, ctx_lo = (sem(s) for s in ("pad", "sums", "mean", "ctx_hi", "ctx_lo"))
        mm, part_ev, tab_sum, rope_c, rope_s, tab_done = (
            sem(s) for s in ("mm", "part_ev", "tab_sum", "rope_c", "rope_s", "tab_done"))
        tab_out = [sem(f"tab_out{i}") for i in range(2)]
        l_mm, l_hi, l_lo, v_mm, v_hi, v_lo, r_hi, r_lo = (
            sem(s) for s in ("l_mm", "l_hi", "l_lo", "v_mm", "v_hi", "v_lo", "r_hi", "r_lo"))
        chain = sem("index_chain")

        def turns(eng, turn, first=0):
            for n in range(4):
                turn(n, 0, n)
            with eng.Fori(1, NB // 4) as q:
                for i in range(4):
                    turn(4 * q + i, q, i)

        with nc.Block() as block:
            @block.sync
            def _(sp):
                def load_ctx(n, i):
                    sp.dma_start(raw[i][:, :, 0:LK], a["ctxT"][bass.ds(n, 1), :, :, :].rearrange("o p c k -> (o p) c k")
                                 ).then_inc(ctx_in[i], 16)

                def load_head(n, i):
                    sp.dma_start(hw[i][:, :], a["head_w"][bass.ds(n, 1), :, :].rearrange("o p c -> (o p) c")
                                 ).then_inc(hw_in[i], 16)

                sp.dma_start(wkvcT[:, :], a["wkvcT"]).then_inc(kr_in, 16)
                sp.dma_start(wkr[:, :], a["wkr"]).then_inc(kr_in, 16)
                sp.dma_start(wkv_raw[:, :, 0:KVC], a["wkvc"]).then_inc(w_in, 16)
                load_ctx(0, 0)
                load_ctx(1, 1)
                load_head(0, 0)
                load_ctx(2, 2)
                load_head(1, 1)
                load_ctx(3, 3)
                with sp.Fori(0, NB // 4 - 1) as q:
                    for i in range(4):
                        n = 4 * q + i + 2
                        sp.wait_ge(v_mm, n - 1)
                        sp.wait_ge(r_lo, 2 * n - 2)
                        load_head(n, i % 2)
                        sp.wait_ge(ctx_lo, n - 1)
                        load_ctx(n + 2, i)
                for n in (H - 2, H - 1):
                    sp.wait_ge(v_mm, n - 1)
                    sp.wait_ge(r_lo, 2 * n - 2)
                    load_head(n, n % 2)
                sp.wait_ge(const_in, 80)

            @block.gpsimd
            def _(pool):
                for i in range(RAWS):
                    pool.memset(raw[i][:, :, LK:TROWS], 0.0).then_inc(pad, 1)
                pool.dma_start(cosk[:, :, :], a["cosk"]).then_inc(rk_in, 16)
                pool.dma_start(sink[:, :, :], a["sink"]).then_inc(rk_in, 16)
                pool.dma_start(ident[:, :], a["ident"]).then_inc(const_in, 16)
                pool.dma_start(w["mask"][:, :], a["mask"]).then_inc(const_in, 16)
                pool.dma_start(w["cosq"][:, :, :], a["cosq"]).then_inc(const_in, 16)
                pool.dma_start(w["sinq"][:, :, :], a["sinq"]).then_inc(const_in, 16)
                pool.dma_start(w["wdq"][:, :, :], a["wdq"]).then_inc(const_in, 16)
                pool.wait_ge(pad, RAWS)
                pool.wait_ge(rk_in, 32)
                rows = table.rearrange("(b t p) c -> b p t c", t=KT, p=P)

                def rope(n, q, i):
                    t = tab[i % 2]
                    pool.wait_ge(tab_sum, n + 1)
                    for hf in range(2):
                        pool.tensor_tensor(rc[:, :, 32 * hf:32 * hf + 32], t[:, :, KVC + 32 * hf:KVC + 32 * hf + 32],
                                           cosk[:, :, :], ALU.mult).then_inc(rope_c, 1)
                        pool.tensor_tensor(rs[:, :, 32 * hf:32 * hf + 32],
                                           t[:, :, KVC + 32 - 32 * hf:KVC + 64 - 32 * hf],
                                           sink[:, :, 32 * hf:32 * hf + 32], ALU.mult).then_inc(rope_s, 1)
                    pool.wait_ge(rope_c, 2 * n + 2)
                    pool.wait_ge(rope_s, 2 * n + 2)
                    pool.tensor_tensor(t[:, :, KVC:ROW], rc[:, :, :], rs[:, :, :], ALU.add).then_inc(tab_done, 1)
                    pool.wait_ge(tab_done, n + 1)
                    pool.dma_start(rows[bass.ds(n, 1), :, :, :].rearrange("o p t c -> (o p) t c"),
                                   t[:, :, :]).then_inc(tab_out[i % 2], 16)

                turns(pool, rope)
                for i in range(2):
                    pool.wait_ge(tab_out[i], 16 * (NB // 2))

            @block.scalar
            def _(act):
                for dst, name in ((segp, "segp"), (segh, "segh"), (base, "row_base"), (joff, "joff"), (joff9, "joff9")):
                    act.dma_start(dst[:, :], a[name]).then_inc(seg_in, 16)
                act.dma_start(other32[:, :], a["other"]).then_inc(mask_in, 16)
                act.dma_start(blocks32[:, :], a["blocks"]).then_inc(mask_in, 16)
                act.wait_ge(fold, 1)
                act.activation(wkv_raw[:, :, KVC:ROW], ps[:, 7, 0:KC * R].rearrange("p (c r) -> p c r", c=KC),
                               ACT.Copy).then_inc(fold_ev, 1)
                act.wait_ge(fold_ev, 1)
                act.wait_ge(w_in, 16)
                act.activation(wkv[:, :, 0:ROW], wkv_raw[:, :, :], ACT.Copy).then_inc(wkv_hi, 1)
                act.wait_ge(pad, RAWS)

                def high_context(n, q, i):
                    act.wait_ge(ctx_in[i], 16 * (q + 1))
                    if not isinstance(n, int) or n >= 2:
                        act.wait_ge(mm, n - 1)
                    for c in range(KC):
                        act.activation(hi[i % 2][:, c, 0:LK], raw[i][:, c, 0:LK], ACT.Copy,
                                       accum_out=ksum[i % 2][:, c:c + 1]).then_inc(sums, 1)
                    act.wait_ge(sums, KC * (n + 1))
                    act.activation(raw[i][:, :, LK:LK + 1], ksum[i % 2][:, :].rearrange("p (c o) -> p c o", o=1),
                                   ACT.Copy, scale=1.0 / LK).then_inc(mean, 1)
                    act.wait_ge(mean, n + 1)
                    act.activation(hi[i % 2][:, :, LK:TROWS], raw[i][:, :, LK:TROWS], ACT.Copy).then_inc(ctx_hi, 1)

                def high_weights(n, i):
                    act.wait_ge(mm, n + 1)
                    b = 3 * (i % 2)
                    act.activation(part[i % 2][:, :, :], ps[:, b:b + 3, ROW:2 * ROW], ACT.Copy).then_inc(part_ev, 1)
                    act.wait_ge(l_mm, n + 1)
                    for k, name in enumerate(("wl_hi", "wl_2")):
                        act.activation(w[name][:, bass.ds(n, 1), :].rearrange("p o c -> p (o c)"),
                                       ps[:, 6, k * P:(k + 1) * P], ACT.Copy).then_inc(l_hi, 1)
                    act.wait_ge(v_mm, n + 1)
                    act.activation(w["wvo_hi"][:, bass.ds(n, 1), :].rearrange("p o c -> p (o c)"), ps[:, 7, :],
                                   ACT.Copy).then_inc(v_hi, 1)
                    for k, name in enumerate(("wr_hi", "wr_2")):
                        act.activation(w[name][:, bass.ds(n, 1), :].rearrange("p o c -> p (o c)"),
                                       hw[i % 2][:, QR + k * R:QR + (k + 1) * R], ACT.Copy).then_inc(r_hi, 1)

                def turn(n, q, i):
                    high_context(n, q, i)
                    if not isinstance(n, int) or n >= 1:
                        high_weights(n - 1, i - 1)

                turns(act, turn)
                high_weights(NB - 1, NB - 1)

            @block.vector
            def _(dve):
                done = [0]

                def link(ins):
                    done[0] += 1
                    ins.then_inc(chain, 1)
                    dve.wait_ge(chain, done[0])

                dve.wait_ge(seg_in, 80)
                link(dve.tensor_copy(segf[:, :], segp[:, :]))
                link(dve.tensor_scalar(key[:, :], segf[:, :], joff[:, 0:1], 0.0, ALU.add, ALU.max))
                link(dve.tensor_scalar(key[:, :], key[:, :], float(LK - 1), None, ALU.min))
                link(dve.tensor_scalar(empty[:, :], segf[:, :], 0.0, None, ALU.is_lt))
                link(dve.tensor_scalar(over[:, :], segf[:, :], float(LK - 1 + LOOKBACK), None, ALU.is_gt))
                link(dve.tensor_tensor(empty[:, :], empty[:, :], over[:, :], ALU.add))
                link(dve.tensor_scalar(over[:, :], key[:, :], -1.0, float(LK), ALU.mult, ALU.add))
                link(dve.tensor_tensor(over[:, :], over[:, :], empty[:, :], ALU.mult))
                link(dve.tensor_tensor(key[:, :], key[:, :], over[:, :], ALU.add))
                link(dve.tensor_tensor(key[:, :], key[:, :], base[:, :], ALU.add))
                link(dve.tensor_copy(w["idx_all"][:, :], key[:, :]))
                neg = w["neg_all"][:, :].rearrange("p (g j) -> p g j", j=WIN)
                link(dve.tensor_copy(segf[0:SR, :], segh[:, :]))
                link(dve.tensor_tensor(keyh[:, :, :], segf[0:SR, :].unsqueeze(2).to_broadcast([SR, ALLG, WIN]),
                                       joff9[:, :].unsqueeze(1).to_broadcast([SR, ALLG, WIN]), ALU.add))
                link(dve.tensor_scalar(neg, keyh[:, :, :], 0.0, float(LK - 1), ALU.max, ALU.min))
                link(dve.tensor_tensor(neg, neg, keyh[:, :, :], ALU.not_equal))
                link(dve.tensor_scalar(neg, neg, NEG, None, ALU.mult))
                dve.wait_ge(mask_in, 32)
                link(dve.tensor_copy(w["other"][:, :], other32[:, :]))
                link(dve.tensor_copy(w["blocks"][:, :].rearrange("p (g k) -> p g k", g=GROUPS),
                                     blocks32[:, :].unsqueeze(1).to_broadcast([P, GROUPS, GR])))

                dve.wait_ge(wkv_hi, 1)
                dve.tensor_tensor(wkv[:, :, ROW:2 * ROW], wkv_raw[:, :, :], wkv[:, :, 0:ROW].bitcast(F32),
                                  ALU.subtract).then_inc(wkv_lo, 1)

                def low_weights(n, q, i):
                    dve.wait_ge(part_ev, n + 1)
                    if not isinstance(n, int) or n >= 2:
                        dve.wait_ge(tab_out[i % 2], 16 * (2 * q + i // 2))
                    b = 3 * (i % 2)
                    dve.tensor_tensor(tab[i % 2][:, :, :], ps[:, b:b + 3, 0:ROW], part[i % 2][:, :, :],
                                      ALU.add).then_inc(tab_sum, 1)

                    def at(name, rows=slice(0, P)):
                        return w[name][rows, bass.ds(n, 1), :].rearrange("p o c -> p (o c)")

                    dve.wait_ge(l_hi, 2 * n + 2)
                    dve.tensor_tensor(at("wl_lo"), ps[:, 6, 0:P], at("wl_hi").bitcast(F32),
                                      ALU.subtract).then_inc(l_lo, 1)
                    low = slice(R, P)
                    dve.tensor_tensor(at("wl_2", low), ps[low, 6, P:2 * P], at("wl_2", low).bitcast(F32),
                                      ALU.subtract).then_inc(l_lo, 1)
                    dve.wait_ge(v_hi, n + 1)
                    dve.tensor_tensor(at("wvo_lo"), ps[:, 7, :], at("wvo_hi").bitcast(F32),
                                      ALU.subtract).then_inc(v_lo, 1)
                    dve.wait_ge(r_hi, 2 * n + 2)
                    dve.tensor_tensor(at("wr_lo"), hw[i % 2][:, QR:QR + R], at("wr_hi").bitcast(F32),
                                      ALU.subtract).then_inc(r_lo, 1)
                    dve.tensor_tensor(at("wr_2", low), hw[i % 2][low, QR + R:QR + 2 * R],
                                      at("wr_2", low).bitcast(F32), ALU.subtract).then_inc(r_lo, 1)

                def turn(n, q, i):
                    dve.wait_ge(ctx_hi, n + 1)
                    dve.tensor_tensor(lo[i % 2][:, :, :], raw[i][:, :, :], hi[i % 2][:, :, :].bitcast(F32),
                                      ALU.subtract).then_inc(ctx_lo, 1)
                    if not isinstance(n, int) or n >= 1:
                        low_weights(n - 1, q, i - 1)

                turns(dve, turn)
                low_weights(NB - 1, 0, NB - 1)

            @block.tensor
            def _(pe):
                pe.wait_ge(kr_in, 32)
                for c in range(KC):
                    last = pe.matmul(ps[:, 7, c * R:(c + 1) * R], wkvcT[:, c * P:(c + 1) * P], wkr[:, :],
                                     start=True, stop=True)
                last.then_inc(fold, 1)
                pe.wait_ge(wkv_lo, 1)

                def turn(n, q, i):
                    later = not isinstance(n, int)
                    b = 3 * (i % 2)
                    pe.wait_ge(ctx_hi, n + 1)
                    if later or n >= 2:
                        pe.wait_ge(tab_sum, n - 1)

                    def high(t, c):
                        return pe.matmul(ps[:, b + t, 0:2 * ROW], hi[i % 2][:, c, t * P:(t + 1) * P],
                                         wkv[:, c, :], start=(c == 0), stop=(c == KC - 1),
                                         skip_group_check=True)

                    for t in range(KT):
                        for c in range(KC - 1):
                            high(t, c)
                    pe.wait_ge(ctx_lo, n + 1)
                    for t in range(KT):
                        for c in range(KC):
                            pe.matmul(ps[:, b + t, 0:ROW], lo[i % 2][:, c, t * P:(t + 1) * P],
                                      wkv[:, c, 0:ROW], start=False, stop=False, skip_group_check=True)
                        last = high(t, KC - 1)
                    last.then_inc(mm, 1)

                    hd = hw[i % 2]
                    pe.wait_ge(hw_in[i % 2], 16 * (2 * q + i // 2 + 1))
                    if later or n >= 1:
                        pe.wait_ge(l_lo, 2 * n)
                        pe.wait_ge(v_lo, 1 * n)
                    for k in range(2):
                        last = pe.matmul(ps[:, 6, k * P:(k + 1) * P], hd[:, UQ + k * P:UQ + (k + 1) * P],
                                         hd[:, UK:UK + P], start=True, stop=True)
                    last.then_inc(l_mm, 1)
                    pe.matmul(ps[:, 7, :], hd[:, UV:UV + P], hd[:, WO:HW], start=True, stop=True).then_inc(v_mm, 1)

                turns(pe, turn)


class NormStage:

    def __init__(self, tag, sb, sem, rows, t_hi, t_lo, ps, banks, ident):
        self.rows, self.t_hi, self.t_lo, self.ps, self.banks, self.ident = rows, t_hi, t_lo, ps, banks, ident
        self.st = sb(f"{tag}_st", [LT, NLT, 6])
        self.mv = sb(f"{tag}_mv", [LT, NLT, 2])
        self.var = sb(f"{tag}_var", [LT, NLT])
        self.rstd = sb(f"{tag}_rstd", [LT, NLT])
        self.power = sb(f"{tag}_power", [LT, NLT])
        self.stats_ok, self.power_ok, self.aggr_ok, self.var_ok, self.rstd_ok, self.norm_ok, self.turned, \
            self.hi_ok, self.lo_ok = (
                sem(f"{tag}_{s}") for s in ("stats", "power", "aggr", "var", "rstd", "norm", "turned", "hi", "lo"))
        self.read = self.hi_ok if t_lo is None else self.lo_ok
        self.c4, self.c1 = Count(NLT), Count(1)

    def stats(self, dve, b, t):
        dve.bn_stats(self.st[:, t, :], self.rows[:, t, :]).then_inc(self.stats_ok, 1)

    def variance(self, dve, b):
        dve.wait_ge(self.stats_ok, self.c4(b, NLT))
        dve.memset(self.power[:, :], -0.5).then_inc(self.power_ok, 1)
        for t in range(NLT):
            dve.bn_aggr(self.mv[:, t, :], self.st[:, t, :]).then_inc(self.aggr_ok, 1)
        dve.wait_ge(self.aggr_ok, self.c4(b, NLT))
        dve.tensor_scalar(self.var[:, :], self.mv[:, :, 1], EPS, None, ALU.add).then_inc(self.var_ok, 1)

    def root(self, pool, b):
        pool.wait_ge(self.power_ok, self.c1(b, 1))
        pool.wait_ge(self.var_ok, self.c1(b, 1))
        pool.tensor_tensor(self.rstd[:, :], self.var[:, :], self.power[:, :], ALU.pow).then_inc(self.rstd_ok, 1)

    def normalise(self, dve, b, t):
        dve.wait_ge(self.rstd_ok, self.c1(b, 1))
        dve.tensor_scalar(self.rows[:, t, :], self.rows[:, t, :], self.mv[:, t, 0:1],
                          self.rstd[:, t:t + 1], ALU.subtract, ALU.mult).then_inc(self.norm_ok, 1)

    def turn(self, pe, b, t):
        pe.wait_ge(self.norm_ok, self.c4(b, t + 1))
        if t >= 2:
            pe.wait_ge(self.read, self.c4(b, t - 1))
        for c in range(KC):
            last = pe.transpose(self.ps[:, self.banks[t % 2], c * LT:(c + 1) * LT],
                                self.rows[:, t, c * P:(c + 1) * P], self.ident[0:LT, 0:LT])
        last.then_inc(self.turned, 1)

    def _bank(self, t):
        return self.ps[:, self.banks[t % 2], 0:KC * LT].rearrange("p (c t) -> p c t", c=KC)

    def high(self, act, b, t):
        act.wait_ge(self.turned, self.c4(b, t + 1))
        act.activation(self.t_hi[:, :, t * LT:(t + 1) * LT], self._bank(t), ACT.Copy).then_inc(self.hi_ok, 1)

    def low(self, dve, b, t):
        dve.wait_ge(self.hi_ok, self.c4(b, t + 1))
        cols = slice(t * LT, (t + 1) * LT)
        dve.tensor_tensor(self.t_lo[:, :, cols], self._bank(t), self.t_hi[:, :, cols].bitcast(F32),
                          ALU.subtract).then_inc(self.lo_ok, 1)


def blocks_of(eng, body):
    body(0, True, False)
    with eng.Fori(1, BLOCKS - 1) as b:
        body(b, False, False)
    body(BLOCKS - 1, False, True)


class Residual:

    def __init__(self, tag, sb, sem, src, dst):
        self.src, self.dst = src, dst
        self.rows = [sb(f"{tag}{i}", [LT, D]) for i in range(2)]
        self.loaded = [sem(f"{tag}_in{i}") for i in range(2)]
        self.summed = sem(f"{tag}_sum")
        self.stored = [sem(f"{tag}_out{i}") for i in range(2)]

    def _tile(self, ap, b, t):
        return ap[bass.ds(b * TB + t * LT, LT), :]

    def load(self, sp, b, t, fresh=False):
        i = t % 2
        if not fresh:
            sp.wait_ge(self.stored[i], b * 32 + 16 * (t // 2))
        sp.dma_start(self.rows[i][:, :], self._tile(self.src, b, t)).then_inc(self.loaded[i], 16)

    def store(self, sp, b, t):
        sp.wait_ge(self.summed, Count(NLT)(b, t + 1))
        sp.dma_start(self._tile(self.dst, b, t), self.rows[t % 2][:, :]).then_inc(self.stored[t % 2], 16)

    def start(self, sp, b, fresh=False):
        self.load(sp, b, 0, fresh)
        self.load(sp, b, 1, fresh)

    def rest(self, sp, b):
        for t in range(NLT):
            self.store(sp, b, t)
            if t + 2 < NLT:
                self.load(sp, b, t + 2)

    def add(self, dve, b, t, done, bank):
        i = t % 2
        dve.wait_ge(self.loaded[i], b * 32 + 16 * (t // 2) + 16)
        dve.wait_ge(done, Count(NLT)(b, t + 1))
        dve.tensor_tensor(self.rows[i][:, :], bank, self.rows[i][:, :], ALU.add).then_inc(self.summed, 1)

    def finish(self, sp):
        for s in self.stored:
            sp.wait_ge(s, 32 * BLOCKS)


def build_attention(nc, a, w, ps, ident, table, x1):
    with ExitStack() as ctx:
        def sb(name, shape, dt=F32, stack=ctx):
            return stack.enter_context(nc.sbuf_tensor(name, shape, dt))

        def sem(name):
            return ctx.enter_context(nc.semaphore(name))

        E = 2 * GROUPS
        q_lat = sb("q_lat", [P, 2, TB, HH])
        q_rope = sb("q_rope", [P, TB, HH])
        xq = sb("x_rows", [LT, NLT, D])
        xT = sb("xT", [P, KC, TB])
        qc_hi, qc_lo, q2_hi, q2_lo = (sb(s, [P, TB], F32R) for s in ("qc_hi", "qc_lo", "q2_hi", "q2_lo"))
        kvg = sb("gathered", [GR, SLOTS, GROUPS, ROW])
        ktn = [sb(f"key_latT{i}", [P, GROUPS * GR]) for i in range(2)]
        ktr = [sb(f"key_ropeT{i}", [P, 2, GROUPS * GR]) for i in range(2)]
        idx = sb("idx", [GR, BG], I32)
        waited = sb("waited", [GR, STEPS])
        rot = [sb(f"rot{i}", [GR, GROUPS, R]) for i in range(2)]
        rc = sb("rot_c", [GR, GROUPS, R])
        rs = sb("rot_s", [GR, GROUPS, R])
        sc = sb("score", [SR, E, WIN])
        sa = sb("score_scaled", [SR, E, WIN])
        mx = sb("score_max", [SR, E])
        sd = [sb(f"score_shift{i}", [SR, E, WIN]) for i in range(2)]
        ex = [sb(f"score_exp{i}", [SR, E, WIN]) for i in range(2)]
        tot = sb("exp_sum", [SR, E])
        inv = sb("exp_inv", [SR, E])
        pn = sb("prob", [SR, E, WIN])
        with ExitStack() as s1:
            pf = [sb(f"prob_wide{i}", [SR, E, GR], stack=s1) for i in range(2)]
            pt = [sb(f"probT{i}", [GR, GROUPS * 2 * SR], stack=s1) for i in range(2)]
        with ExitStack() as s2:
            oT = sb("oT", [P, KC, TB], stack=s2)
            sb("oT_gap", [P, 2 * E * GR - KC * TB + 16], stack=s2)
            o_hi = [sb(f"o_hi{i}", [P, TB], F32R, stack=s2) for i in range(2)]
            o_lo = [sb(f"o_lo{i}", [P, TB], F32R, stack=s2) for i in range(2)]
        ctx.enter_context(nc.sbuf_tensor("shared_space", [P, 2 * E * GR + 4 * GROUPS * SR + 16], F32))

        zeros = sem("zeros")
        ln = NormStage("lnq", sb, sem, xq, xT, None, ps, (2, 3), ident)
        res = Residual("res", sb, sem, a["x"], x1)
        x_in, tick = sem("x_in"), sem("waited_tick")
        qc_mm, qc_hi_ok, qc_lo_ok, q_mm, q_act, q_dve = (
            sem(s) for s in ("qc_mm", "qc_hi_ok", "qc_lo_ok", "q_mm", "q_act", "q_dve"))
        idx_ok, rot_cs, rot_ok = (sem(s) for s in ("idx_ok", "rot_cos_sin", "rot_ok"))
        gath = [sem(f"gathered{i}") for i in range(SLOTS)]
        t_mm, t_ev, s_mm, s_red, s_scl, s_max, s_sub, s_exp, s_sum, s_inv, s_pn, pf_ok = (
            sem(s) for s in ("t_mm", "t_ev", "s_mm", "s_red", "s_scl", "s_max", "s_sub", "s_exp",
                             "s_sum", "s_inv", "s_pn", "pf_ok"))
        p_mm, p_ev, av_mm, lat_ev = (sem(s) for s in ("p_mm", "p_ev", "av_mm", "lat_ev"))
        oh_ok, ol_ok, o_mm, oT_act, oT_dve, bt_mm = (
            sem(s) for s in ("oh_ok", "ol_ok", "o_mm", "oT_act", "oT_dve", "bt_mm"))

        c1, c2, c4, c8, c16, c12, c24 = (Count(n) for n in (1, 2, NLT, STEPS, 16, 12, 24))
        slot_uses = [len(range(i, STEPS, SLOTS)) for i in range(SLOTS)]

        def gathered(b, s):
            i = s % SLOTS
            return b * (16 * GROUPS * slot_uses[i]) + 16 * GROUPS * (s // SLOTS + 1)

        q_out = [("lat", h) for h in range(H)] + [("rope", h) for h in range(HH)]

        def q_dst(o):
            kind, h = q_out[o]
            return q_lat[:, h % 2, :, h // 2] if kind == "lat" else q_rope[:, :, h]

        with nc.Block() as block:
            @block.sync
            def _(sp):
                def rows(b):
                    sp.dma_start(xq[:, :, :], a["x"][bass.ds(b * TB, TB), :].rearrange("(t p) d -> p t d", p=LT)
                                 ).then_inc(x_in, 16)

                def body(b, first, last):
                    if not last:
                        sp.wait_ge(ln.turned, c4(b, NLT))
                        rows(b + 1)
                    if not first:
                        res.rest(sp, b - 1)
                    res.start(sp, b, fresh=first)

                rows(0)
                blocks_of(sp, body)
                res.rest(sp, BLOCKS - 1)
                res.finish(sp)

            @block.gpsimd
            def _(pool):
                for i in range(2):
                    pool.memset(ktr[i][0:R, 1, :], 0.0).then_inc(zeros, 1)
                    pool.memset(ktr[i][R:P, 0, :], 0.0).then_inc(zeros, 1)
                pool.wait_ge(zeros, 4)

                def body(b, first, last):
                    if not first:
                        pool.wait_ge(av_mm, c8(b, 0))
                        pool.wait_ge(tick, Count(1 + STEPS - SLOTS)(b, 0))
                    pool.tensor_copy(idx[:, :], w["idx_all"][:, bass.ds(b * BG, BG)]).then_inc(idx_ok, 1)
                    if first:
                        ln.root(pool, b)
                    for s in range(STEPS):
                        if s == 0:
                            pool.wait_ge(idx_ok, c1(b, 1))
                        elif s >= SLOTS:
                            pool.wait_ge(av_mm, c8(b, s - SLOTS + 1))
                        if s == 0 or s >= SLOTS:
                            pool.tensor_tensor(waited[:, s:s + 1], ident[0:GR, 0:1], ident[0:GR, 0:1],
                                               ALU.add).then_inc(tick, 1)
                        for g in range(GROUPS):
                            k = s * GROUPS + g
                            pool.indirect_dma_start(
                                out=kvg[:, s % SLOTS, g, :], out_offset=None, in_=table,
                                in_offset=bass.IndirectOffsetOnAxis(ap=idx[:, k:k + 1], axis=0),
                            ).then_inc(gath[s % SLOTS], 16)
                    if not last:
                        ln.root(pool, b + 1)

                blocks_of(pool, body)

            @block.tensor
            def _(pe):
                pe.wait_ge(zeros, 4)

                def compress(b):
                    pe.wait_ge(ln.hi_ok, c4(b, NLT))
                    for m in range(2):
                        for c in range(KC):
                            last = pe.matmul(ps[:, m, 0:TB], w["wdq"][:, c, m * P:(m + 1) * P], xT[:, c, :],
                                             start=(c == 0), stop=(c == KC - 1))
                        last.then_inc(qc_mm, 1)

                def query(b, o):
                    kind, h = q_out[o]
                    if o >= 4:
                        pe.wait_ge(q_dve if o % 2 else q_act, c12(b, (o - 4) // 2 + 1))
                    if kind == "lat":
                        v, hs = "wl", slice(h, h + 1)
                    else:
                        v, hs = "wr", slice(2 * h, 2 * h + 2)
                    parts = ((f"{v}_hi", qc_hi), (f"{v}_hi", qc_lo), (f"{v}_lo", qc_hi),
                             (f"{v}_2", q2_hi), (f"{v}_2", q2_lo))
                    for n, (wt, xs) in enumerate(parts):
                        last = pe.matmul(ps[:, o % 4, 0:TB], w[wt][:, hs, :].rearrange("p h c -> p (h c)"), xs[:, :],
                                         start=(n == 0), stop=(n == len(parts) - 1))
                    last.then_inc(q_mm, 1)

                def turn_back(b):
                    pe.wait_ge(oT_act, c2(b, 2))
                    pe.wait_ge(oT_dve, c2(b, 2))
                    for t in range(NLT):
                        for c in range(KC):
                            last = pe.transpose(ps[0:LT, 4 + t, c * P:(c + 1) * P], oT[:, c, t * LT:(t + 1) * LT],
                                                ident[:, :])
                        last.then_inc(bt_mm, 1)

                def turn_keys(b, s):
                    pe.wait_ge(rot_ok, c8(b, s + 1))
                    if s >= 1:
                        pe.wait_ge(t_ev, c8(b, s))
                    for g in range(GROUPS):
                        pe.transpose(ps[:, 2, g * GR:(g + 1) * GR], kvg[:, s % SLOTS, g, 0:KVC],
                                     ident[0:GR, 0:GR])
                    for g in range(GROUPS):
                        last = pe.transpose(ps[0:R, 3, g * GR:(g + 1) * GR], rot[s % 2][:, g, :],
                                            ident[0:GR, 0:GR])
                    last.then_inc(t_mm, 1)

                def scores(b, s):
                    pe.wait_ge(t_ev, c8(b, s + 1))
                    if s >= 1:
                        pe.wait_ge(s_red, c16(b, 2 * s))
                    for e in range(2):
                        pe.matmul(ps[0:SR, e, 0:GROUPS * GR], w["other"][:, :], w["blocks"][:, :],
                                  start=True, stop=False, skip_group_check=True)
                        for g in range(GROUPS):
                            out = ps[0:SR, e, g * GR:(g + 1) * GR]
                            q0 = s * STEP + GSTART[g]
                            pe.matmul(out, q_lat[:, e, q0:q0 + GQ, :].rearrange("p q i -> p (q i)"),
                                      ktn[s % 2][:, g * GR:(g + 1) * GR], start=False, stop=False,
                                      skip_group_check=True)
                            last = pe.matmul(out, q_rope[:, q0:q0 + GQ, :].rearrange("p q i -> p (q i)"),
                                             ktr[s % 2][:, e, g * GR:(g + 1) * GR], start=False, stop=True,
                                             skip_group_check=True)
                        last.then_inc(s_mm, 1)

                def turn_probs(b, s):
                    pe.wait_ge(pf_ok, c8(b, s + 1))
                    if s >= 1:
                        pe.wait_ge(p_ev, c16(b, 2 * s))
                    for g in range(GROUPS):
                        for e in range(2):
                            at = (g % 2) * 2 * SR + e * SR
                            last = pe.transpose(ps[0:GR, 4 + g // 2, at:at + SR],
                                                pf[s % 2][:, e * GROUPS + g, :], ident[0:SR, 0:SR])
                    last.then_inc(p_mm, 1)

                def values(b, s):
                    pe.wait_ge(p_ev, c16(b, 2 * s + 2))
                    if s >= 1:
                        pe.wait_ge(lat_ev, c24(b, 3 * s))
                    for g in range(GROUPS):
                        at = (g % 2) * 2 * SR
                        last = pe.matmul(ps[:, 6 + g // 2, at:at + 2 * SR], kvg[:, s % SLOTS, g, 0:KVC],
                                         pt[s % 2][:, g * 2 * SR:(g + 1) * 2 * SR], start=True, stop=True)
                    last.then_inc(av_mm, 1)

                def body(b, first, last_block):
                    if first:
                        for t in range(NLT):
                            ln.turn(pe, b, t)
                        compress(b)
                    pe.wait_ge(qc_lo_ok, c2(b, 2))
                    for o in range(4):
                        query(b, o)
                    if not first:
                        turn_back(b - 1)
                    for o in range(4, len(q_out)):
                        query(b, o)
                    pe.wait_ge(q_act, c12(b, 12))
                    pe.wait_ge(q_dve, c12(b, 12))
                    turn_keys(b, 0)
                    turn_keys(b, 1)
                    scores(b, 0)
                    turn_keys(b, 2)
                    scores(b, 1)
                    for s in range(STEPS):
                        if s + 3 < STEPS:
                            turn_keys(b, s + 3)
                        if s == 0:
                            scores(b, s + 2)
                        turn_probs(b, s)
                        if s >= 1 and s + 2 < STEPS:
                            scores(b, s + 2)
                        if s >= STEPS - 2 and not last_block:
                            for t in range(2):
                                ln.turn(pe, b + 1, 2 * (s - STEPS + 2) + t)
                        values(b, s)
                    if not last_block:
                        pe.wait_ge(s_red, c16(b, 16))
                        compress(b + 1)
                    for h in range(H):
                        pe.wait_ge(ol_ok, c16(b, h + 1))
                        for m in range(KC):
                            cols = slice(m * P, (m + 1) * P)
                            parts = (("wvo_hi", o_hi), ("wvo_hi", o_lo), ("wvo_lo", o_hi))
                            for n, (wt, xs) in enumerate(parts):
                                last = pe.matmul(ps[:, 4 + m, 0:TB], w[wt][:, h, cols], xs[h % 2][:, :],
                                                 start=(h == 0 and n == 0), stop=(h == H - 1 and n == 2))
                        last.then_inc(o_mm, 1)
                    if last_block:
                        turn_back(b)

                blocks_of(pe, body)

            @block.scalar
            def _(act):
                def split_compressed(b):
                    for m, dst in enumerate((qc_hi, q2_hi)):
                        act.wait_ge(qc_mm, c2(b, m + 1))
                        act.activation(dst[:, :], ps[:, m, 0:TB], ACT.Copy).then_inc(qc_hi_ok, 1)

                def take_keys(b, s):
                    act.wait_ge(t_mm, c8(b, s + 1))
                    if s >= 2:
                        act.wait_ge(s_mm, c16(b, 2 * s - 2))
                    act.activation(ktn[s % 2][:, :], ps[:, 2, 0:GROUPS * GR], ACT.Copy)
                    act.activation(ktr[s % 2][0:R, 0, :], ps[0:R, 3, 0:GROUPS * GR], ACT.Copy)
                    act.activation(ktr[s % 2][R:P, 1, :], ps[0:R, 3, 0:GROUPS * GR], ACT.Copy).then_inc(t_ev, 1)

                def exps(b, s):
                    act.wait_ge(s_sub, c8(b, s + 1))
                    act.activation(ex[s % 2][:, :, :], sd[s % 2][:, :, :], ACT.Exp).then_inc(s_exp, 1)

                def take_probs(b, s):
                    act.wait_ge(p_mm, c8(b, s + 1))
                    act.activation(pt[s % 2][:, 0:4 * SR], ps[0:GR, 4, 0:4 * SR], ACT.Copy).then_inc(p_ev, 1)
                    act.activation(pt[s % 2][:, 4 * SR:6 * SR], ps[0:GR, 5, 0:2 * SR], ACT.Copy).then_inc(p_ev, 1)

                def take_values(b, s):
                    act.wait_ge(av_mm, c8(b, s + 1))
                    for g in range(GROUPS):
                        q0 = s * STEP + GSTART[g]
                        at = (g % 2) * 2 * SR
                        if g:
                            act.wait_ge(lat_ev, c24(b, 3 * s + g))
                        act.activation(
                            q_lat[:, :, q0:q0 + GQ, :].rearrange("p e q i -> p e (q i)"),
                            ps[:, 6 + g // 2, at:at + 2 * SR].rearrange("p (e r) -> p e r", e=2),
                            ACT.Copy).then_inc(lat_ev, 1)

                def high_latent(b, h):
                    if h >= 2:
                        act.wait_ge(o_mm, c16(b, h - 1))
                    act.activation(o_hi[h % 2][:, :], q_lat[:, h % 2, :, h // 2], ACT.Copy).then_inc(oh_ok, 1)

                def body(b, first, last):
                    if first:
                        for t in range(NLT):
                            ln.high(act, b, t)
                        split_compressed(b)
                    for o in range(0, len(q_out), 2):
                        act.wait_ge(q_mm, c24(b, o + 1))
                        act.activation(q_dst(o), ps[:, o % 4, 0:TB], ACT.Copy).then_inc(q_act, 1)
                    take_keys(b, 0)
                    take_keys(b, 1)
                    exps(b, 0)
                    take_keys(b, 2)
                    for s in range(STEPS):
                        if s + 1 < STEPS:
                            exps(b, s + 1)
                        if s + 3 < STEPS:
                            take_keys(b, s + 3)
                        take_probs(b, s)
                        if s >= STEPS - 2 and not last:
                            for t in range(2):
                                ln.high(act, b + 1, 2 * (s - STEPS + 2) + t)
                        take_values(b, s)
                    act.wait_ge(lat_ev, c24(b, 24))
                    high_latent(b, 0)
                    high_latent(b, 1)
                    if not last:
                        split_compressed(b + 1)
                    for h in range(2, H):
                        high_latent(b, h)
                    act.wait_ge(o_mm, c16(b, H))
                    for m in (0, 2):
                        act.activation(oT[:, m, :], ps[:, 4 + m, 0:TB], ACT.Copy).then_inc(oT_act, 1)

                blocks_of(act, body)

            @block.vector
            def _(dve):
                def split_compressed(b):
                    for m, (hi, lo) in enumerate(((qc_hi, qc_lo), (q2_hi, q2_lo))):
                        dve.wait_ge(qc_hi_ok, c2(b, m + 1))
                        dve.tensor_tensor(lo[:, :], ps[:, m, 0:TB], hi[:, :].bitcast(F32),
                                          ALU.subtract).then_inc(qc_lo_ok, 1)

                def rotate(b, s, first):
                    ph = ((b * STEPS + s) % PERIOD) * GROUPS
                    kr = kvg[:, s % SLOTS, :, KVC:ROW]
                    dve.wait_ge(gath[s % SLOTS], gathered(b, s))
                    if s >= 2:
                        dve.wait_ge(t_mm, c8(b, s - 1))
                    if s >= 1 or not first:
                        dve.wait_ge(rot_ok, c8(b, s))
                    dve.tensor_tensor(rc[:, :, :].rearrange("p g (h r) -> p g h r", h=2),
                                      kr.rearrange("p g (h r) -> p g h r", h=2),
                                      w["cosq"][:, bass.ds(ph, GROUPS), :].unsqueeze(2)
                                      .to_broadcast([GR, GROUPS, 2, R // 2]), ALU.mult).then_inc(rot_cs, 1)
                    for hf in range(2):
                        dve.tensor_tensor(rs[:, :, 32 * hf:32 * hf + 32], kr[:, :, 32 - 32 * hf:64 - 32 * hf],
                                          w["sinq"][:, bass.ds(ph, GROUPS), 32 * hf:32 * hf + 32],
                                          ALU.mult).then_inc(rot_cs, 1)
                    dve.wait_ge(rot_cs, c24(b, 3 * s + 3))
                    dve.tensor_tensor(rot[s % 2][:, :, :], rc[:, :, :], rs[:, :, :], ALU.add).then_inc(rot_ok, 1)

                def window(b, s):
                    for e in range(2):
                        dve.wait_ge(s_mm, c16(b, 2 * s + e + 1))
                        dve.tensor_reduce(sc[:, e * GROUPS:(e + 1) * GROUPS, :],
                                          ps[0:SR, e, 0:GROUPS * GR].rearrange("p (g q j) -> p g j q", g=GROUPS, q=GQ),
                                          AX.X, ALU.max).then_inc(s_red, 1)
                    dve.wait_ge(s_red, c16(b, 2 * s + 2))
                    dve.scalar_tensor_tensor(
                        out=sa[:, :, :].rearrange("p (e g) j -> p e (g j)", e=2),
                        in0=sc[:, :, :].rearrange("p (e g) j -> p e (g j)", e=2), scalar=SCALE,
                        in1=w["neg_all"][:, bass.ds((b * STEPS + s) * GROUPS * WIN, GROUPS * WIN)].unsqueeze(1)
                        .to_broadcast([SR, 2, GROUPS * WIN]),
                        op0=ALU.mult, op1=ALU.add).then_inc(s_scl, 1)
                    dve.wait_ge(s_scl, c8(b, s + 1))
                    dve.tensor_reduce(mx[:, :], sa[:, :, :], AX.X, ALU.max).then_inc(s_max, 1)
                    dve.wait_ge(s_max, c8(b, s + 1))
                    dve.tensor_tensor(sd[s % 2][:, :, :], sa[:, :, :],
                                      mx[:, :].unsqueeze(2).to_broadcast([SR, E, WIN]),
                                      ALU.subtract).then_inc(s_sub, 1)

                def probs(b, s):
                    dve.wait_ge(s_exp, c8(b, s + 1))
                    dve.tensor_reduce(tot[:, :], ex[s % 2][:, :, :], AX.X, ALU.add).then_inc(s_sum, 1)
                    dve.wait_ge(s_sum, c8(b, s + 1))
                    dve.reciprocal(inv[:, :], tot[:, :]).then_inc(s_inv, 1)
                    dve.wait_ge(s_inv, c8(b, s + 1))
                    dve.tensor_tensor(pn[:, :, :], ex[s % 2][:, :, :],
                                      inv[:, :].unsqueeze(2).to_broadcast([SR, E, WIN]),
                                      ALU.mult).then_inc(s_pn, 1)
                    dve.wait_ge(s_pn, c8(b, s + 1))
                    if s >= 2:
                        dve.wait_ge(p_mm, c8(b, s - 1))
                    dve.tensor_tensor(
                        pf[s % 2][:, :, :].rearrange("p x (q j) -> p x q j", q=GQ),
                        pn[:, :, :].unsqueeze(2).to_broadcast([SR, E, GQ, WIN]),
                        w["mask"][:, :].rearrange("p (q j) -> p q j", q=GQ).unsqueeze(1)
                        .to_broadcast([SR, E, GQ, WIN]), ALU.mult).then_inc(pf_ok, 1)

                def norm_piece(b, s):
                    if s < NLT:
                        if s == 0:
                            dve.wait_ge(x_in, 16 * (b + 1))
                        ln.stats(dve, b, s)
                    elif s == NLT:
                        ln.variance(dve, b)
                    elif s < NLT + 3:
                        for t in range(2):
                            ln.normalise(dve, b, 2 * (s - NLT - 1) + t)

                def low_latent(b, h):
                    dve.wait_ge(oh_ok, c16(b, h + 1))
                    dve.tensor_tensor(o_lo[h % 2][:, :], q_lat[:, h % 2, :, h // 2], o_hi[h % 2][:, :].bitcast(F32),
                                      ALU.subtract).then_inc(ol_ok, 1)

                def add_back(b, t):
                    res.add(dve, b, t, bt_mm, ps[0:LT, 4 + t, :])

                def body(b, first, last):
                    if first:
                        for s in range(NLT + 3):
                            norm_piece(b, s)
                        split_compressed(b)
                    for o in range(1, len(q_out), 2):
                        dve.wait_ge(q_mm, c24(b, o + 1))
                        dve.tensor_copy(q_dst(o), ps[:, o % 4, 0:TB]).then_inc(q_dve, 1)
                        if not first and 5 <= o < 5 + 2 * NLT:
                            add_back(b - 1, (o - 5) // 2)
                        if o in (15, 19):
                            rotate(b, (o - 15) // 4, first)
                    rotate(b, 2, first)
                    window(b, 0)
                    rotate(b, 3, first)
                    probs(b, 0)
                    for s in range(STEPS):
                        if s + 1 < STEPS:
                            window(b, s + 1)
                        if not last:
                            norm_piece(b + 1, s)
                        if s + 4 < STEPS:
                            rotate(b, s + 4, first)
                        if s + 1 < STEPS:
                            probs(b, s + 1)
                    low_latent(b, 0)
                    low_latent(b, 1)
                    if not last:
                        split_compressed(b + 1)
                    for h in range(2, H):
                        low_latent(b, h)
                    dve.wait_ge(o_mm, c16(b, H))
                    for m in (1, 3):
                        dve.tensor_copy(oT[:, m, :], ps[:, 4 + m, 0:TB]).then_inc(oT_dve, 1)
                    if last:
                        for t in range(NLT):
                            add_back(b, t)

                blocks_of(dve, body)


def build_ffn(nc, a, ps, ident, x1):
    with ExitStack() as ctx:
        def sb(name, shape, dt=F32):
            return ctx.enter_context(nc.sbuf_tensor(name, shape, dt))

        def sem(name):
            return ctx.enter_context(nc.semaphore(name))

        WR = 2 * KC * P + D
        w_hi = sb("ffn_hi", [P, IC, WR], F32R)
        w_lo = sb("ffn_lo", [P, IC, WR], F32R)
        raw = [sb(f"ffn_raw{i}", [P, WR]) for i in range(2)]
        h_hi = sb("h_hi", [P, IC, TB], F32R)
        h_lo = sb("h_lo", [P, IC, TB], F32R)
        scale = sb("ffn_scale", [P, 2 * IC + KC])
        xf = sb("x1_rows_sb", [LT, NLT, D])
        xT_hi, xT_lo = (sb(f"x1T_{s}", [P, KC, TB], F32R) for s in ("hi", "lo"))
        act_g = [sb(f"silu{i}", [P, TB]) for i in range(2)]
        hf = [sb(f"hidden{i}", [P, TB]) for i in range(2)]
        oT = sb("yT", [P, KC, TB])
        w_in = [sem(f"ffn_in{i}") for i in range(2)]
        s_in, x_in = sem("scale_in"), sem("x1_in")
        ln = NormStage("lnf", sb, sem, xf, xT_hi, xT_lo, ps, (6, 7), ident)
        res = Residual("fres", sb, sem, x1, a["out"])
        whi_ok, wlo_ok, g_mm, u_mm, silu_ok, hf_ok, hh_ok, hl_ok, d_mm, d_act, d_dve, y_mm = (
            sem(s) for s in ("whi_ok", "wlo_ok", "g_mm", "u_mm", "silu_ok", "hf_ok", "hh_ok", "hl_ok", "d_mm",
                             "d_act", "d_dve", "y_mm"))
        cI, c4, c2 = Count(IC), Count(NLT), Count(2)

        with nc.Block() as block:
            @block.sync
            def _(sp):
                def rows(b):
                    sp.dma_start(xf[:, :, :], x1[bass.ds(b * TB, TB), :].rearrange("(t p) d -> p t d", p=LT)
                                 ).then_inc(x_in, 16)

                def body(b, first, last):
                    if not last:
                        sp.wait_ge(ln.turned, c4(b, NLT))
                        rows(b + 1)
                    if not first:
                        res.rest(sp, b - 1)
                    res.start(sp, b, fresh=first)

                rows(0)
                sp.dma_start(scale[:, :], a["ffn_scale"]).then_inc(s_in, 16)
                blocks_of(sp, body)
                res.rest(sp, BLOCKS - 1)
                res.finish(sp)

            @block.gpsimd
            def _(pool):
                for c in range(IC):
                    if c >= 2:
                        pool.wait_ge(wlo_ok, c - 1)
                    pool.dma_start(raw[c % 2][:, :], a["ffn_w"][c]).then_inc(w_in[c % 2], 16)
                    if c == 3:
                        ln.root(pool, 0)
                with pool.Fori(1, BLOCKS) as b:
                    ln.root(pool, b)

            def wt(buf, c, which, k):
                return buf[:, c, which * KC * P + k * P:which * KC * P + (k + 1) * P]

            def down(buf, c, m):
                return buf[:, c, 2 * KC * P + m * P:2 * KC * P + (m + 1) * P]

            @block.tensor
            def _(pe):
                def turn_back(b, t):
                    if t == 0:
                        pe.wait_ge(d_act, c2(b, 2))
                        pe.wait_ge(d_dve, c2(b, 2))
                    if t >= 2:
                        pe.wait_ge(res.summed, c4(b, t - 1))
                    for k in range(KC):
                        last = pe.transpose(ps[0:LT, 6 + t % 2, k * P:(k + 1) * P],
                                            oT[:, k, t * LT:(t + 1) * LT], ident[:, :])
                    last.then_inc(y_mm, 1)

                def body(b, first, last_block):
                    if first:
                        for t in range(NLT):
                            ln.turn(pe, b, t)
                    pe.wait_ge(ln.lo_ok, c4(b, NLT))
                    for c in range(IC):
                        if first:
                            pe.wait_ge(wlo_ok, c + 1)
                        for which, done in ((0, g_mm), (1, u_mm)):
                            if c >= 2:
                                pe.wait_ge(hf_ok if which else silu_ok, cI(b, c - 1))
                            n = 0
                            for buf, xs in ((w_hi, xT_hi), (w_hi, xT_lo), (w_lo, xT_hi)):
                                for k in range(KC):
                                    last = pe.matmul(ps[:, 2 * which + c % 2, 0:TB], wt(buf, c, which, k),
                                                     xs[:, k, :], start=(n == 0), stop=(n == 3 * KC - 1))
                                    n += 1
                            last.then_inc(done, 1)
                        if not first and c < 2:
                            turn_back(b - 1, 2 * c)
                            turn_back(b - 1, 2 * c + 1)
                    for m in range(KC):
                        if m >= 2:
                            pe.wait_ge(d_dve if m % 2 else d_act, c2(b, m // 2))
                        n = 0
                        for c in range(IC):
                            if m == 0:
                                pe.wait_ge(hl_ok, cI(b, c + 1))
                            for buf, xs in ((w_hi, h_hi), (w_hi, h_lo), (w_lo, h_hi)):
                                last = pe.matmul(ps[:, 4 + m % 2, 0:TB], down(buf, c, m), xs[:, c, :],
                                                 start=(n == 0), stop=(n == 3 * IC - 1))
                                n += 1
                        last.then_inc(d_mm, 1)
                        if m < 2 and not last_block:
                            ln.turn(pe, b + 1, 2 * m)
                            ln.turn(pe, b + 1, 2 * m + 1)
                    if last_block:
                        for t in range(NLT):
                            turn_back(b, t)

                blocks_of(pe, body)

            @block.scalar
            def _(act):
                def split(c):
                    act.wait_ge(w_in[c % 2], 16 * (c // 2 + 1))
                    act.activation(w_hi[:, c, :], raw[c % 2][:, :], ACT.Copy).then_inc(whi_ok, 1)

                def high(b, c):
                    act.wait_ge(hf_ok, cI(b, c + 1))
                    act.activation(h_hi[:, c, :], hf[c % 2][:, :], ACT.Copy).then_inc(hh_ok, 1)

                def body(b, first, last):
                    if first:
                        for t in range(NLT):
                            ln.high(act, b, t)
                    for c in range(IC):
                        act.wait_ge(g_mm, cI(b, c + 1))
                        if c >= 2:
                            act.wait_ge(hf_ok, cI(b, c - 1))
                        act.activation(act_g[c % 2][:, :], ps[:, c % 2, 0:TB], ACT.Silu,
                                       scale=scale[:, c:c + 1]).then_inc(silu_ok, 1)
                        if first and c + 2 < IC:
                            split(c + 2)
                        if c:
                            high(b, c - 1)
                    high(b, IC - 1)
                    for m in range(KC):
                        if m % 2 == 0:
                            act.wait_ge(d_mm, c4(b, m + 1))
                            act.activation(oT[:, m, :], ps[:, 4 + m % 2, 0:TB], ACT.Copy,
                                           scale=scale[:, 2 * IC + m:2 * IC + m + 1]).then_inc(d_act, 1)
                        if m < 2 and not last:
                            ln.high(act, b + 1, 2 * m)
                            ln.high(act, b + 1, 2 * m + 1)

                act.wait_ge(s_in, 16)
                split(0)
                split(1)
                blocks_of(act, body)

            @block.vector
            def _(dve):
                def split(c):
                    dve.wait_ge(whi_ok, c + 1)
                    dve.tensor_tensor(w_lo[:, c, :], raw[c % 2][:, :], w_hi[:, c, :].bitcast(F32),
                                      ALU.subtract).then_inc(wlo_ok, 1)

                def low(b, c):
                    dve.wait_ge(hh_ok, cI(b, c + 1))
                    dve.tensor_tensor(h_lo[:, c, :], hf[c % 2][:, :], h_hi[:, c, :].bitcast(F32),
                                      ALU.subtract).then_inc(hl_ok, 1)

                def norm_piece(b, n):
                    if n < NLT:
                        if n == 0:
                            dve.wait_ge(x_in, 16 * (b + 1))
                        ln.stats(dve, b, n)
                    elif n == NLT:
                        ln.variance(dve, b)
                    else:
                        for t in range(2):
                            ln.normalise(dve, b, 2 * (n - NLT - 1) + t)

                def add_back(b, t):
                    res.add(dve, b, t, y_mm, ps[0:LT, 6 + t % 2, :])

                def body(b, first, last):
                    if first:
                        for n in range(NLT + 3):
                            norm_piece(b, n)
                        for t in range(NLT):
                            ln.low(dve, b, t)
                    for c in range(IC):
                        dve.wait_ge(u_mm, cI(b, c + 1))
                        dve.wait_ge(silu_ok, cI(b, c + 1))
                        if c >= 2:
                            dve.wait_ge(hl_ok, cI(b, c - 1))
                        dve.scalar_tensor_tensor(out=hf[c % 2][:, :], in0=ps[:, 2 + c % 2, 0:TB],
                                                 scalar=scale[:, IC + c:IC + c + 1], in1=act_g[c % 2][:, :],
                                                 op0=ALU.mult, op1=ALU.mult).then_inc(hf_ok, 1)
                        if first and c + 2 < IC:
                            split(c + 2)
                        if c:
                            low(b, c - 1)
                        if not first and c < 2:
                            add_back(b - 1, 2 * c)
                            add_back(b - 1, 2 * c + 1)
                        if c >= IC - 7 and not last:
                            norm_piece(b + 1, c - IC + 7)
                    low(b, IC - 1)
                    for m in range(KC):
                        if m % 2:
                            dve.wait_ge(d_mm, c4(b, m + 1))
                            dve.tensor_scalar(oT[:, m, :], ps[:, 4 + m % 2, 0:TB],
                                              scale[:, 2 * IC + m:2 * IC + m + 1], None, ALU.mult).then_inc(d_dve, 1)
                        if m < 2 and not last:
                            ln.low(dve, b + 1, 2 * m)
                            ln.low(dve, b + 1, 2 * m + 1)
                    if last:
                        for t in range(NLT):
                            add_back(b, t)

                dve.wait_ge(s_in, 16)
                split(0)
                split(1)
                blocks_of(dve, body)


def constants():
    import numpy as np

    f = np.float32
    half = R // 2
    inv_freq = (1.0 / (f(10000.0) ** (np.arange(half, dtype=f) / f(half)))).astype(f)
    ang = np.arange(LK, dtype=f)[:, None] * inv_freq
    cos, sin = np.cos(ang).astype(f), np.sin(ang).astype(f)
    kpos = np.minimum(np.arange(TROWS), LK - 1).reshape(KT, P).T
    first = np.array([s * STEP + g for s in range(TOK // STEP) for g in GSTART])
    tok = first[None, :] + (np.arange(GR) // WIN)[:, None]
    qpos = tok[:, :PERIOD * GROUPS] % LQ
    same = (np.arange(SR) // HH)[:, None] == (np.arange(GR) // WIN)[None, :]
    query = np.arange(P)[:, None]
    other = (query < GQ) & (query != (np.arange(SR) // HH)[None, :])
    blocks = (query < GQ) & (query == (np.arange(GR) // WIN)[None, :])
    return tok, first, {
        "ident": np.eye(P, dtype=f),
        "mask": same.astype(f), "other": other.astype(f), "blocks": np.where(blocks, f(FAR), f(0)),
        "cosk": cos[kpos], "sink": np.concatenate([-sin[kpos], sin[kpos]], -1),
        "cosq": cos[qpos], "sinq": np.concatenate([sin[qpos], -sin[qpos]], -1),
        "row_base": (tok // LQ * TROWS).astype(f),
        "joff": (np.arange(GR) % WIN - LOOKBACK).astype(f)[:, None],
        "joff9": np.broadcast_to((np.arange(WIN) - LOOKBACK).astype(f), (SR, WIN)),
    }


def kernel(x, ctx_2048, itok_BxS_0_1023, L0_xattn_W_kvc, L0_xattn_W_dq, L0_xattn_W_uq, L0_xattn_W_qr,
           L0_xattn_W_uk, L0_xattn_W_kr, L0_xattn_W_uv, L0_xattn_W_o, L0_ffn_gate_w, L0_ffn_up_w,
           L0_ffn_down_w, L0_ffn_gate_s, L0_ffn_up_s, L0_ffn_down_s):
    import numpy as np
    import concourse.bacc as bacc
    from concourse.bass_utils import run_bass_kernel_spmd

    def twice(m):
        return np.concatenate([m, m[..., P:]], -1)

    tok, first, arrays = constants()
    seg = np.asarray(itok_BxS_0_1023).reshape(TOK)
    arrays["x"] = np.asarray(x).reshape(TOK, D)
    arrays["ctxT"] = np.asarray(ctx_2048).reshape(NB, LK, KC, P).transpose(0, 3, 2, 1)
    arrays["segp"] = seg[tok]
    arrays["segh"] = seg[first[None, :] + (np.arange(SR) // HH)[:, None]]
    arrays["wkvc"] = np.asarray(L0_xattn_W_kvc).reshape(KC, P, KVC).transpose(1, 0, 2)
    arrays["wkvcT"] = np.asarray(L0_xattn_W_kvc).T
    arrays["wkr"] = np.asarray(L0_xattn_W_kr)
    arrays["wdq"] = twice(np.asarray(L0_xattn_W_dq).reshape(KC, P, QC).transpose(1, 0, 2))
    uq = twice(np.asarray(L0_xattn_W_uq).reshape(QC, H, HD).transpose(1, 2, 0))
    uk = np.asarray(L0_xattn_W_uk).reshape(KVC, H, HD).transpose(1, 2, 0)
    uv = np.asarray(L0_xattn_W_uv).reshape(KVC, H, HD).transpose(1, 2, 0)
    qr = np.asarray(L0_xattn_W_qr).reshape(QC, H, R).transpose(1, 0, 2)
    arrays["head_w"] = np.concatenate([uq, uk, uv, qr[:, :P], np.concatenate([qr[:, P:], qr[:, P:]], 1),
                                       np.asarray(L0_xattn_W_o).reshape(H, HD, D)], -1)
    gate, up = (np.asarray(m).reshape(IC, P, KC, P).transpose(0, 3, 2, 1).reshape(IC, P, KC * P)
                for m in (L0_ffn_gate_w, L0_ffn_up_w))
    arrays["ffn_w"] = np.concatenate([gate, up, np.asarray(L0_ffn_down_w).T.reshape(IC, P, D)], -1)
    arrays["ffn_scale"] = np.concatenate(
        [np.asarray(m).reshape(-1, P).T for m in (L0_ffn_gate_s, L0_ffn_up_s, L0_ffn_down_s)], -1)

    nc = bacc.Bacc("TRN2", target_bir_lowering=False, num_devices=1)
    aps = {}
    for name in arrays:
        arrays[name] = np.ascontiguousarray(arrays[name])
        aps[name] = nc.dram_tensor(name + "_dram", arrays[name].shape, mybir.dt.from_np(arrays[name].dtype),
                                   kind="ExternalInput").ap()
    aps["out"] = nc.dram_tensor("out_dram", [TOK, D], F32, kind="ExternalOutput").ap()
    build(nc, aps)
    r = run_bass_kernel_spmd(nc, [{name + "_dram": v for name, v in arrays.items()}], core_ids=[0])
    return r.results[0]["out_dram"].reshape(NB, LQ, D)
```

```python
from contextlib import ExitStack

import numpy as np
import concourse.bass as bass
from concourse import mybir

F32 = mybir.dt.float32
F32R = mybir.dt.float32r
I32 = mybir.dt.int32
BF16 = mybir.dt.bfloat16
ALU = mybir.AluOpType
ACT = mybir.ActivationFunctionType
AX = mybir.AxisListType

P = 128
NB, LQ, LK, D = 16, 100, 361, 512
H, HD, R = 16, 128, 64
KVC, QC = 128, 192
LOOKBACK = 8
WIN = LOOKBACK + 1
NEG = -1e30
SCALE = 1.0 / float((HD + R) ** 0.5)
EPS = 1e-5
INTER = 1408
KC = D // P
TOK = NB * LQ

GQ = 14
GR = GQ * WIN
GROUPS = 3
GSTART = (0, 13, 26)
STEP = 40
STEPS = 8
TB = STEP * STEPS
BLOCKS = TOK // TB
BG = STEPS * GROUPS
ALLG = BLOCKS * BG
PERIOD = 5
HH = H // 2
SR = GQ * HH
LT = 80
NLT = TB // LT
ROW = KVC + R
KT = 3
TROWS = KT * P
SLOTS = 6
FAR = -2.0 ** 127
IC = INTER // P
WR = 2 * KC * P + D
FRONT = 7
EARLY = 3
WR = 2 * KC * P + D


class Count:

    def __init__(self, per):
        self.per = per

    def __call__(self, b, k):
        return b * self.per + k


def build(nc, a):
    with ExitStack() as whole:
        def sb(name, shape, dt=F32, stack=whole):
            return stack.enter_context(nc.sbuf_tensor(name, shape, dt))

        def sem(name):
            return whole.enter_context(nc.semaphore(name))

        table = nc.dram_tensor("kv_table", [NB * TROWS, ROW], F32, kind="Internal").ap()
        x1 = nc.dram_tensor("x1_rows", [TOK, D], F32, kind="Internal").ap()
        ps = whole.enter_context(nc.psum_tensor("ps", [P, 8, 512], F32))
        ident = sb("ident", [P, P])
        rows = sb("rows", [LT, NLT, D])
        with ExitStack() as plain:
            rowsT32 = sb("rowsT32", [P, KC, TB], F32, plain)
            four32 = sb("four32", [P, KC, TB], F32, plain)
        rowsT = sb("rowsT", [P, KC, TB], F32R)
        four = sb("four", [P, KC, TB], F32R)
        ln_q = NormStage("lnq", sb, sem, rows, rowsT32, None, ps, ident)
        ln_f = NormStage("lnf", sb, sem, rows, rowsT, four, ps, ident)
        sums = [sb(f"residual{i}", [LT, D]) for i in range(2)]
        scale = sb("ffn_scale", [P, 2 * IC + KC])
        low_mass = sb("low_mass", [P, IC])
        low_any = sb("low_any", [P, 1])
        low_flag = sb("low_flag", [1, 1], I32)
        qc_mm = sem("qc_mm")

        ffn = {}
        with ExitStack() as places:
            width = 0
            for name, shape, dt in (("h_hi", [P, IC, TB], F32R), ("h_lo", [P, IC, TB], F32R),
                                    ("silu", [P, 2, TB], F32), ("hidden", [P, 2, TB], F32),
                                    ("yT", [P, KC, TB], F32), ("hi_back", [P, IC - FRONT, WR], F32R)):
                ffn[name] = sb(name, shape, dt, places)
                width += shape[1] * shape[2]
            sb("ffn_gap", [P, 2 * H * D - width], F32, places)
            with ExitStack() as plain:
                ffn["raw"] = sb("ffn_raw", [P, IC, WR], F32, plain)
            ffn["lo"] = sb("ffn_lo", [P, IC, WR], F32R, places)
            ffn["hi_front"] = sb("hi_front", [P, FRONT, WR], F32R, places)
            ffn["unread"] = sb("unread", [P, WR], F32, places)
        w = {}
        for name, shape, dt in (
            ("wvo_hi", [P, H, D], F32R), ("wvo_lo", [P, H, D], F32R),
            ("wl_hi", [P, H, P], F32R), ("wl_lo", [P, H, P], F32R), ("wl_2", [P, H, P], F32R),
            ("wr_hi", [P, H, R], F32R), ("wr_lo", [P, H, R], F32R), ("wr_2", [P, H, R], F32R),
            ("wdq", [P, KC, 2 * P], F32),
            ("mask", [SR, GR], F32), ("other", [P, SR], BF16), ("blocks", [P, GROUPS * GR], BF16),
            ("cosq", [GR, PERIOD * GROUPS, R // 2], F32),
            ("sinq", [GR, PERIOD * GROUPS, R], F32), ("idx_all", [GR, ALLG], I32),
            ("neg_all", [SR, ALLG * WIN], F32),
        ):
            w[name] = sb(name, shape, dt)
        build_setup(nc, a, w, ps, ident, table, rows, rowsT32, four32, ln_q, qc_mm)
        with ExitStack() as ctx:
            with nc.Block() as block:
                shared = build_attention(nc, block, ctx, a, w, ffn, ps, ident, table, x1, rows, rowsT32, four,
                                         ln_q, ln_f, sums, qc_mm)
                build_ffn(nc, block, ctx, a, ffn, ps, ident, x1, rows, rowsT, four, ln_f, sums, scale, shared,
                          low_mass, low_any, low_flag)


def compress(pe, b, m, w, rowsT, ps, ln, qc_mm):
    pe.wait_ge(ln.hi_ok, Count(NLT)(b, NLT))
    for c in range(KC):
        last = pe.matmul(ps[:, m, 0:TB], w["wdq"][:, c, m * P:(m + 1) * P], rowsT[:, c, :],
                         start=(c == 0), stop=(c == KC - 1))
    last.then_inc(qc_mm, 1)




def build_setup(nc, a, w, ps, ident, table, rows, rowsT, four, ln, qc_mm):
    with ExitStack() as ctx:
        def sb(name, shape, dt=F32, stack=ctx):
            return stack.enter_context(nc.sbuf_tensor(name, shape, dt))

        def sem(name):
            return ctx.enter_context(nc.semaphore(name))

        RAWS = 4
        UQ, UK, UV, QR, WO = 0, 2 * P, 3 * P, 4 * P, 5 * P
        HW = WO + D
        with ExitStack() as plain:
            raw = [sb(f"ctx_raw{i}", [P, KC, TROWS], F32, plain) for i in range(RAWS)]
        lo = [sb(f"ctx_lo{i}", [P, KC, TROWS], F32R) for i in range(RAWS)]
        hi = [sb("ctx_hi0", [P, KC, TROWS], F32R)]
        ksum = [sb(f"ctx_sum{i}", [P, KC]) for i in range(2)]
        with ExitStack() as index:
            segp = sb("segp", [GR, ALLG], I32, index)
            base = sb("row_base", [GR, ALLG], F32, index)
            joff = sb("joff", [GR, 1], F32, index)
            segf = sb("segf", [GR, ALLG], F32, index)
            key = sb("key", [GR, ALLG], F32, index)
            empty = sb("empty", [GR, ALLG], F32, index)
            over = sb("over", [GR, ALLG], F32, index)
            other32 = sb("other32", [P, SR], F32, index)
            blocks32 = sb("blocks32", [P, GR], F32, index)
        hi.append(sb("ctx_hi1", [P, KC, TROWS], F32R))
        part = [sb(f"tab_part{i}", [P, KT, ROW]) for i in range(2)]
        tab = [sb(f"tab{i}", [P, KT, ROW]) for i in range(2)]
        segh = sb("segh", [SR, ALLG], I32)
        seghf = sb("seghf", [SR, ALLG])
        joff9 = sb("joff9", [SR, WIN])
        keyh = sb("keyh", [SR, ALLG, WIN])
        zero = sb("zero", [P, KC, TROWS - LK - 1])
        rc = sb("rope_cos", [P, KT, R])
        rs = sb("rope_sin", [P, KT, R])
        cosk = sb("cosk", [P, KT, R // 2])
        sink = sb("sink", [P, KT, R])
        wkv_raw = four[:, :, 0:ROW]
        wkvcT = four[:, :, ROW:ROW + P]
        wkr = sb("wkr", [P, R])
        wkv = sb("wkv", [P, KC, 2 * ROW], F32R)
        hw = [sb(f"head_w{i}", [P, HW]) for i in range(2)]

        w_in, kr_in, seg_in, rk_in, const_in, mask_in = (
            sem(s) for s in ("w_in", "kr_in", "seg_in", "rk_in", "const_in", "mask_in"))
        ctx_in = [sem(f"ctx_in{i}") for i in range(RAWS)]
        hw_in = [sem(f"head_in{i}") for i in range(2)]
        fold, fold_ev, wkv_hi, wkv_lo = (sem(s) for s in ("fold", "fold_ev", "wkv_hi", "wkv_lo"))
        pad, sums, mean, ctx_hi, ctx_lo = (sem(s) for s in ("pad", "sums", "mean", "ctx_hi", "ctx_lo"))
        mm, part_ev, tab_sum, rope_c, rope_s, tab_done = (
            sem(s) for s in ("mm", "part_ev", "tab_sum", "rope_c", "rope_s", "tab_done"))
        tab_out = [sem(f"tab_out{i}") for i in range(2)]
        l_mm, l_hi, l_lo, v_mm, v_hi, v_lo, r_hi, r_lo = (
            sem(s) for s in ("l_mm", "l_hi", "l_lo", "v_mm", "v_hi", "v_lo", "r_hi", "r_lo"))
        chain, x_in = sem("index_chain"), sem("first_rows_in")
        index_ok, done_mark = sem("index_ok"), sb("done_mark", [1, 1])

        def turns(eng, turn, first=0):
            for n in range(4):
                turn(n, 0, n)
            with eng.Fori(1, NB // 4) as q:
                for i in range(4):
                    turn(4 * q + i, q, i)

        with nc.Block() as block:
            @block.sync
            def _(sp):
                def load_ctx(n, i):
                    sp.dma_start(raw[i][:, :, 0:LK], a["ctxT"][bass.ds(n, 1), :, :, :].rearrange("o p c k -> (o p) c k")
                                 ).then_inc(ctx_in[i], 16)

                def load_head(n, i):
                    sp.dma_start(hw[i][:, :], a["head_w"][bass.ds(n, 1), :, :].rearrange("o p c -> (o p) c")
                                 ).then_inc(hw_in[i], 16)

                sp.dma_start(wkvcT, a["wkvcT"].rearrange("p (c k) -> p c k", c=KC)).then_inc(kr_in, 16)
                sp.dma_start(wkr[:, :], a["wkr"]).then_inc(kr_in, 16)
                sp.dma_start(wkv_raw[:, :, 0:KVC], a["wkvc"]).then_inc(w_in, 16)
                load_ctx(0, 0)
                for dst, name in ((segp, "segp"), (segh, "segh"), (base, "row_base"), (joff, "joff"), (joff9, "joff9")):
                    sp.dma_start(dst[:, :], a[name]).then_inc(seg_in, 16)
                sp.dma_start(other32[:, :], a["other"]).then_inc(mask_in, 16)
                sp.dma_start(blocks32[:, :], a["blocks"]).then_inc(mask_in, 16)
                load_ctx(1, 1)
                load_head(0, 0)
                sp.dma_start(rows[:, :, :], a["x"][0:TB, :].rearrange("(t p) d -> p t d", p=LT)).then_inc(x_in, 16)
                load_ctx(2, 2)
                load_head(1, 1)
                load_ctx(3, 3)
                with sp.Fori(0, NB // 4 - 1) as q:
                    for i in range(4):
                        n = 4 * q + i + 2
                        sp.wait_ge(v_mm, n - 1)
                        sp.wait_ge(r_lo, 2 * n - 2)
                        load_head(n, i % 2)
                        sp.wait_ge(mm, n - 1)
                        load_ctx(n + 2, i)
                for n in (H - 2, H - 1):
                    sp.wait_ge(v_mm, n - 1)
                    sp.wait_ge(r_lo, 2 * n - 2)
                    load_head(n, n % 2)
                sp.wait_ge(const_in, 80)

            @block.gpsimd
            def _(pool):
                pool.memset(zero[:, :, :], 0.0).then_inc(pad, 1)
                pool.dma_start(cosk[:, :, :], a["cosk"]).then_inc(rk_in, 16)
                pool.dma_start(sink[:, :, :], a["sink"]).then_inc(rk_in, 16)
                pool.dma_start(ident[:, :], a["ident"]).then_inc(const_in, 16)
                pool.dma_start(w["mask"][:, :], a["mask"]).then_inc(const_in, 16)
                pool.dma_start(w["cosq"][:, :, :], a["cosq"]).then_inc(const_in, 16)
                pool.dma_start(w["sinq"][:, :, :], a["sinq"]).then_inc(const_in, 16)
                pool.dma_start(w["wdq"][:, :, :], a["wdq"]).then_inc(const_in, 16)
                pool.wait_ge(rk_in, 32)
                table_rows = table.rearrange("(b t p) c -> b p t c", t=KT, p=P)

                def rope(n, q, i):
                    t = tab[i % 2]
                    pool.wait_ge(tab_sum, n + 1)
                    for hf in range(2):
                        pool.tensor_tensor(rc[:, :, 32 * hf:32 * hf + 32], t[:, :, KVC + 32 * hf:KVC + 32 * hf + 32],
                                           cosk[:, :, :], ALU.mult).then_inc(rope_c, 1)
                        pool.tensor_tensor(rs[:, :, 32 * hf:32 * hf + 32],
                                           t[:, :, KVC + 32 - 32 * hf:KVC + 64 - 32 * hf],
                                           sink[:, :, 32 * hf:32 * hf + 32], ALU.mult).then_inc(rope_s, 1)
                    pool.wait_ge(rope_c, 2 * n + 2)
                    pool.wait_ge(rope_s, 2 * n + 2)
                    pool.tensor_tensor(t[:, :, KVC:ROW], rc[:, :, :], rs[:, :, :], ALU.add).then_inc(tab_done, 1)
                    pool.wait_ge(tab_done, n + 1)
                    pool.dma_start(table_rows[bass.ds(n, 1), :, :, :].rearrange("o p t c -> (o p) t c"),
                                   t[:, :, :]).then_inc(tab_out[i % 2], 16)
                    if isinstance(n, int) and n == 0:
                        ln.root(pool, 0)

                turns(pool, rope)
                for i in range(2):
                    pool.wait_ge(tab_out[i], 16 * (NB // 2))

            @block.scalar
            def _(act):
                act.wait_ge(pad, 1)
                for half in (*lo, hi[0]):
                    act.activation(half[:, :, LK + 1:TROWS], zero[:, :, :], ACT.Copy)
                act.wait_ge(fold, 1)
                act.activation(wkv_raw[:, :, KVC:ROW], ps[:, 7, 0:KC * R].rearrange("p (c r) -> p c r", c=KC),
                               ACT.Copy).then_inc(fold_ev, 1)
                act.wait_ge(fold_ev, 1)
                act.wait_ge(w_in, 16)
                act.activation(wkv[:, :, 0:ROW], wkv_raw[:, :, :], ACT.Copy).then_inc(wkv_hi, 1)

                def high_context(n, q, i):
                    act.wait_ge(ctx_in[i], 16 * (q + 1))
                    if not isinstance(n, int) or n >= 2:
                        act.wait_ge(mm, n - 1)
                    for c in range(KC):
                        act.activation(hi[i % 2][:, c, 0:LK], raw[i][:, c, 0:LK], ACT.Copy,
                                       accum_out=ksum[i % 2][:, c:c + 1]).then_inc(sums, 1)
                    act.wait_ge(sums, KC * (n + 1))
                    act.activation(raw[i][:, :, LK:LK + 1], ksum[i % 2][:, :].rearrange("p (c o) -> p c o", o=1),
                                   ACT.Copy, scale=1.0 / LK).then_inc(mean, 1)
                    act.wait_ge(mean, n + 1)
                    act.activation(hi[i % 2][:, :, LK:LK + 1], raw[i][:, :, LK:LK + 1], ACT.Copy).then_inc(ctx_hi, 1)

                def high_weights(n, i):
                    act.wait_ge(mm, n + 1)
                    b = 3 * (i % 2)
                    act.activation(part[i % 2][:, :, :], ps[:, b:b + 3, ROW:2 * ROW], ACT.Copy).then_inc(part_ev, 1)
                    act.wait_ge(l_mm, n + 1)
                    for k, name in enumerate(("wl_hi", "wl_2")):
                        act.activation(w[name][:, bass.ds(n, 1), :].rearrange("p o c -> p (o c)"),
                                       ps[:, 6, k * P:(k + 1) * P], ACT.Copy).then_inc(l_hi, 1)
                    act.wait_ge(v_mm, n + 1)
                    act.activation(w["wvo_hi"][:, bass.ds(n, 1), :].rearrange("p o c -> p (o c)"), ps[:, 7, :],
                                   ACT.Copy).then_inc(v_hi, 1)
                    for k, name in enumerate(("wr_hi", "wr_2")):
                        act.activation(w[name][:, bass.ds(n, 1), :].rearrange("p o c -> p (o c)"),
                                       hw[i % 2][:, QR + k * R:QR + (k + 1) * R], ACT.Copy).then_inc(r_hi, 1)

                def turn(n, q, i):
                    if isinstance(n, int) and n == 1:
                        act.wait_ge(index_ok, 1)
                        act.activation(hi[1][:, :, LK + 1:TROWS], zero[:, :, :], ACT.Copy)
                    high_context(n, q, i)
                    if not isinstance(n, int) or n >= 1:
                        high_weights(n - 1, i - 1)

                turns(act, turn)
                high_weights(NB - 1, NB - 1)
                for t in range(NLT):
                    ln.high(act, 0, t, (0, 1))

            @block.vector
            def _(dve):
                done = [0]

                def link(ins):
                    done[0] += 1
                    ins.then_inc(chain, 1)
                    dve.wait_ge(chain, done[0])

                def key_mask_work():
                    neg = w["neg_all"][:, :].rearrange("p (g j) -> p g j", j=WIN)
                    link(dve.tensor_copy(seghf[:, :], segh[:, :]))
                    link(dve.tensor_tensor(keyh[:, :, :], seghf[:, :].unsqueeze(2).to_broadcast([SR, ALLG, WIN]),
                                           joff9[:, :].unsqueeze(1).to_broadcast([SR, ALLG, WIN]), ALU.add))
                    link(dve.tensor_scalar(neg, keyh[:, :, :], 0.0, float(LK - 1), ALU.max, ALU.min))
                    link(dve.tensor_tensor(neg, neg, keyh[:, :, :], ALU.not_equal))
                    link(dve.tensor_scalar(neg, neg, NEG, None, ALU.mult))

                def index_work():
                    dve.wait_ge(seg_in, 80)
                    link(dve.tensor_copy(segf[:, :], segp[:, :]))
                    link(dve.tensor_scalar(key[:, :], segf[:, :], joff[:, 0:1], 0.0, ALU.add, ALU.max))
                    link(dve.tensor_scalar(key[:, :], key[:, :], float(LK - 1), None, ALU.min))
                    link(dve.tensor_scalar(empty[:, :], segf[:, :], 0.0, None, ALU.is_lt))
                    link(dve.tensor_scalar(over[:, :], segf[:, :], float(LK - 1 + LOOKBACK), None, ALU.is_gt))
                    link(dve.tensor_tensor(empty[:, :], empty[:, :], over[:, :], ALU.add))
                    link(dve.tensor_scalar(over[:, :], key[:, :], -1.0, float(LK), ALU.mult, ALU.add))
                    link(dve.tensor_tensor(over[:, :], over[:, :], empty[:, :], ALU.mult))
                    link(dve.tensor_tensor(key[:, :], key[:, :], over[:, :], ALU.add))
                    link(dve.tensor_tensor(key[:, :], key[:, :], base[:, :], ALU.add))
                    link(dve.tensor_copy(w["idx_all"][:, :], key[:, :]))
                    dve.wait_ge(mask_in, 32)
                    link(dve.tensor_copy(w["other"][:, :], other32[:, :]))
                    link(dve.tensor_copy(w["blocks"][:, :].rearrange("p (g k) -> p g k", g=GROUPS),
                                         blocks32[:, :].unsqueeze(1).to_broadcast([P, GROUPS, GR])))

                    dve.memset(done_mark[:, :], 0.0).then_inc(index_ok, 1)

                dve.wait_ge(wkv_hi, 1)
                dve.tensor_tensor(wkv[:, :, ROW:2 * ROW], wkv_raw[:, :, :], wkv[:, :, 0:ROW].bitcast(F32),
                                  ALU.subtract).then_inc(wkv_lo, 1)

                def low_weights(n, q, i):
                    dve.wait_ge(part_ev, n + 1)
                    if not isinstance(n, int) or n >= 2:
                        dve.wait_ge(tab_out[i % 2], 16 * (2 * q + i // 2))
                    b = 3 * (i % 2)
                    dve.tensor_tensor(tab[i % 2][:, :, :], ps[:, b:b + 3, 0:ROW], part[i % 2][:, :, :],
                                      ALU.add).then_inc(tab_sum, 1)

                    def at(name, rows=slice(0, P)):
                        return w[name][rows, bass.ds(n, 1), :].rearrange("p o c -> p (o c)")

                    dve.wait_ge(l_hi, 2 * n + 2)
                    dve.tensor_tensor(at("wl_lo"), ps[:, 6, 0:P], at("wl_hi").bitcast(F32),
                                      ALU.subtract).then_inc(l_lo, 1)
                    low = slice(R, P)
                    dve.tensor_tensor(at("wl_2", low), ps[low, 6, P:2 * P], at("wl_2", low).bitcast(F32),
                                      ALU.subtract).then_inc(l_lo, 1)
                    dve.wait_ge(v_hi, n + 1)
                    dve.tensor_tensor(at("wvo_lo"), ps[:, 7, :], at("wvo_hi").bitcast(F32),
                                      ALU.subtract).then_inc(v_lo, 1)
                    dve.wait_ge(r_hi, 2 * n + 2)
                    dve.tensor_tensor(at("wr_lo"), hw[i % 2][:, QR:QR + R], at("wr_hi").bitcast(F32),
                                      ALU.subtract).then_inc(r_lo, 1)
                    dve.tensor_tensor(at("wr_2", low), hw[i % 2][low, QR + R:QR + 2 * R],
                                      at("wr_2", low).bitcast(F32), ALU.subtract).then_inc(r_lo, 1)

                def turn(n, q, i):
                    dve.wait_ge(ctx_hi, n + 1)
                    dve.tensor_tensor(lo[i][:, :, 0:LK + 1], raw[i][:, :, 0:LK + 1], hi[i % 2][:, :, 0:LK + 1].bitcast(F32),
                                      ALU.subtract).then_inc(ctx_lo, 1)
                    if not isinstance(n, int) or n >= 1:
                        low_weights(n - 1, q, i - 1)
                    if isinstance(n, int) and n == 0:
                        index_work()
                    if isinstance(n, int):
                        for piece in ((0, 1, 2, 3), (4,), (5,), (6,))[n]:
                            ln.piece(dve, 0, piece, x_in)

                turns(dve, turn)
                low_weights(NB - 1, 0, NB - 1)
                key_mask_work()

            @block.tensor
            def _(pe):
                pe.wait_ge(kr_in, 32)
                for c in range(KC):
                    last = pe.matmul(ps[:, 7, c * R:(c + 1) * R], wkvcT[:, c, :], wkr[:, :],
                                     start=True, stop=True)
                last.then_inc(fold, 1)
                pe.wait_ge(wkv_lo, 1)

                def turn(n, q, i):
                    later = not isinstance(n, int)
                    b = 3 * (i % 2)
                    pe.wait_ge(ctx_hi, n + 1)
                    if later or n >= 2:
                        pe.wait_ge(tab_sum, n - 1)

                    def high(t, c):
                        return pe.matmul(ps[:, b + t, 0:2 * ROW], hi[i % 2][:, c, t * P:(t + 1) * P],
                                         wkv[:, c, :], start=(c == 0), stop=(c == KC - 1),
                                         skip_group_check=True)

                    for t in range(KT):
                        for c in range(KC - 1):
                            high(t, c)
                    pe.wait_ge(ctx_lo, n + 1)
                    for t in range(KT):
                        for c in range(KC):
                            pe.matmul(ps[:, b + t, 0:ROW], lo[i][:, c, t * P:(t + 1) * P],
                                      wkv[:, c, 0:ROW], start=False, stop=False, skip_group_check=True)
                        last = high(t, KC - 1)
                    last.then_inc(mm, 1)

                    hd = hw[i % 2]
                    pe.wait_ge(hw_in[i % 2], 16 * (2 * q + i // 2 + 1))
                    if later or n >= 1:
                        pe.wait_ge(l_lo, 2 * n)
                        pe.wait_ge(v_lo, 1 * n)
                    for k in range(2):
                        last = pe.matmul(ps[:, 6, k * P:(k + 1) * P], hd[:, UQ + k * P:UQ + (k + 1) * P],
                                         hd[:, UK:UK + P], start=True, stop=True)
                    last.then_inc(l_mm, 1)
                    pe.matmul(ps[:, 7, :], hd[:, UV:UV + P], hd[:, WO:HW], start=True, stop=True).then_inc(v_mm, 1)

                turns(pe, turn)
                pe.wait_ge(tab_sum, NB - 1)
                for t in range(NLT):
                    ln.turn(pe, 0, t, (0, 1))
                for m in range(2):
                    compress(pe, 0, m, w, rowsT, ps, ln, qc_mm)


class NormStage:

    def __init__(self, tag, sb, sem, rows, t_hi, t_lo, ps, ident):
        self.rows, self.t_hi, self.t_lo, self.ps, self.ident = rows, t_hi, t_lo, ps, ident
        self.st = sb(f"{tag}_st", [LT, NLT, 6])
        self.mv = sb(f"{tag}_mv", [LT, NLT, 2])
        self.var = sb(f"{tag}_var", [LT, NLT])
        self.rstd = sb(f"{tag}_rstd", [LT, NLT])
        self.power = sb(f"{tag}_power", [LT, NLT])
        self.stats_ok, self.power_ok, self.aggr_ok, self.var_ok, self.rstd_ok, self.norm_ok, self.turned, \
            self.hi_ok, self.lo_ok = (
                sem(f"{tag}_{s}") for s in ("stats", "power", "aggr", "var", "rstd", "norm", "turned", "hi", "lo"))
        self.read = self.hi_ok if t_lo is None else self.lo_ok
        self.c4, self.c1 = Count(NLT), Count(1)

    def stats(self, dve, b, t):
        dve.bn_stats(self.st[:, t, :], self.rows[:, t, :]).then_inc(self.stats_ok, 1)

    def variance(self, dve, b):
        dve.wait_ge(self.stats_ok, self.c4(b, NLT))
        dve.memset(self.power[:, :], -0.5).then_inc(self.power_ok, 1)
        for t in range(NLT):
            dve.bn_aggr(self.mv[:, t, :], self.st[:, t, :]).then_inc(self.aggr_ok, 1)
        dve.wait_ge(self.aggr_ok, self.c4(b, NLT))
        dve.tensor_scalar(self.var[:, :], self.mv[:, :, 1], EPS, None, ALU.add).then_inc(self.var_ok, 1)

    def root(self, pool, b):
        pool.wait_ge(self.power_ok, self.c1(b, 1))
        pool.wait_ge(self.var_ok, self.c1(b, 1))
        pool.tensor_tensor(self.rstd[:, :], self.var[:, :], self.power[:, :], ALU.pow).then_inc(self.rstd_ok, 1)

    def normalise(self, dve, b, t):
        dve.wait_ge(self.rstd_ok, self.c1(b, 1))
        dve.tensor_scalar(self.rows[:, t, :], self.rows[:, t, :], self.mv[:, t, 0:1],
                          self.rstd[:, t:t + 1], ALU.subtract, ALU.mult).then_inc(self.norm_ok, 1)

    def turn(self, pe, b, t, banks):
        pe.wait_ge(self.norm_ok, self.c4(b, t + 1))
        if t >= 2:
            pe.wait_ge(self.read, self.c4(b, t - 1))
        for c in range(KC):
            last = pe.transpose(self.ps[:, banks[t % 2], c * LT:(c + 1) * LT],
                                self.rows[:, t, c * P:(c + 1) * P], self.ident[0:LT, 0:LT])
        last.then_inc(self.turned, 1)

    def _bank(self, t, banks):
        return self.ps[:, banks[t % 2], 0:KC * LT].rearrange("p (c t) -> p c t", c=KC)

    def high(self, act, b, t, banks):
        act.wait_ge(self.turned, self.c4(b, t + 1))
        act.activation(self.t_hi[:, :, t * LT:(t + 1) * LT], self._bank(t, banks), ACT.Copy).then_inc(self.hi_ok, 1)

    def low(self, dve, b, t, banks):
        dve.wait_ge(self.hi_ok, self.c4(b, t + 1))
        cols = slice(t * LT, (t + 1) * LT)
        dve.tensor_tensor(self.t_lo[:, :, cols], self._bank(t, banks), self.t_hi[:, :, cols].bitcast(F32),
                          ALU.subtract).then_inc(self.lo_ok, 1)

    def piece(self, dve, b, n, x_in, loads=1):
        if n == 0:
            dve.wait_ge(x_in, 16 * loads)
        if n < NLT:
            self.stats(dve, b, n)
        elif n == NLT:
            self.variance(dve, b)
        else:
            for t in range(2):
                self.normalise(dve, b, 2 * (n - NLT - 1) + t)


def blocks_of(eng, body):
    body(0, True, False)
    with eng.Fori(1, BLOCKS - 1) as b:
        body(b, False, False)
    body(BLOCKS - 1, False, True)


def ffn_high(ffn, c):
    return ffn["hi_front"][:, c, :] if c < FRONT else ffn["hi_back"][:, c - FRONT, :]


class Residual:

    def __init__(self, tag, sem, rows, src, dst):
        self.src, self.dst, self.rows = src, dst, rows
        self.loaded = [sem(f"{tag}_in{i}") for i in range(2)]
        self.summed = sem(f"{tag}_sum")
        self.stored = [sem(f"{tag}_out{i}") for i in range(2)]

    def _tile(self, ap, b, t):
        return ap[bass.ds(b * TB + t * LT, LT), :]

    def load(self, sp, b, t, fresh=False):
        i = t % 2
        if not fresh:
            sp.wait_ge(self.stored[i], b * 32 + 16 * (t // 2))
        sp.dma_start(self.rows[i][:, :], self._tile(self.src, b, t)).then_inc(self.loaded[i], 16)

    def store(self, sp, b, t):
        sp.wait_ge(self.summed, Count(NLT)(b, t + 1))
        sp.dma_start(self._tile(self.dst, b, t), self.rows[t % 2][:, :]).then_inc(self.stored[t % 2], 16)

    def start(self, sp, b, fresh=False):
        self.load(sp, b, 0, fresh)
        self.load(sp, b, 1, fresh)

    def rest(self, sp, b):
        for t in range(0, NLT, 2):
            self.store(sp, b, t)
            self.store(sp, b, t + 1)
            if t + 2 < NLT:
                self.load(sp, b, t + 2)
                self.load(sp, b, t + 3)

    def add(self, dve, b, t, done, bank):
        i = t % 2
        dve.wait_ge(self.loaded[i], b * 32 + 16 * (t // 2) + 16)
        dve.wait_ge(done, Count(NLT)(b, t + 1))
        dve.tensor_tensor(self.rows[i][:, :], bank, self.rows[i][:, :], ALU.add).then_inc(self.summed, 1)

    def finish(self, sp):
        for s in self.stored:
            sp.wait_ge(s, 32 * BLOCKS)


def build_attention(nc, block, ctx, a, w, ffn, ps, ident, table, x1, rows, rowsT, four, ln, ln_f, sums, qc_mm):
    def sb(name, shape, dt=F32, stack=ctx):
        return stack.enter_context(nc.sbuf_tensor(name, shape, dt))

    def sem(name):
        return ctx.enter_context(nc.semaphore(name))

    E = 2 * GROUPS
    qc_hi, qc_lo, q2_hi, q2_lo = (four[:, i, :] for i in range(4))
    kvg = sb("gathered", [GR, SLOTS, GROUPS, ROW])
    ktn = [sb(f"key_latT{i}", [P, GROUPS * GR]) for i in range(2)]
    ktr = [sb(f"key_ropeT{i}", [P, 2, GROUPS * GR]) for i in range(2)]
    q_rope = sb("q_rope", [P, TB, HH])
    rot = [sb(f"rot{i}", [GR, GROUPS, R]) for i in range(2)]
    rc = sb("rot_c", [GR, GROUPS, R])
    rs = sb("rot_s", [GR, GROUPS, R])
    q_lat = sb("q_lat", [P, 2, TB, HH])
    with ExitStack() as s1:
        pf = [sb(f"prob_wide{i}", [SR, E, GR], stack=s1) for i in range(2)]
        pt = [sb(f"probT{i}", [GR, GROUPS * 2 * SR], stack=s1) for i in range(2)]
    with ExitStack() as s2:
        oT = sb("oT", [P, KC, TB], stack=s2)
        sb("oT_gap", [P, 2 * E * GR - KC * TB + 16], stack=s2)
        o_hi = [sb(f"o_hi{i}", [P, TB], F32R, stack=s2) for i in range(2)]
        o_lo = [sb(f"o_lo{i}", [P, TB], F32R, stack=s2) for i in range(2)]
    ctx.enter_context(nc.sbuf_tensor("shared_space", [P, 2 * E * GR + 4 * GROUPS * SR + 16], F32))

    idx = sb("idx", [GR, BG], I32)
    waited = sb("waited", [GR, STEPS])
    sc = sb("score", [SR, E, WIN])
    sa = sb("score_scaled", [SR, E, WIN])
    mx = sb("score_max", [SR, E])
    sd = [sb(f"score_shift{i}", [SR, E, WIN]) for i in range(2)]
    ex = [sb(f"score_exp{i}", [SR, E, WIN]) for i in range(2)]
    tot = sb("exp_sum", [SR, E])
    inv = sb("exp_inv", [SR, E])
    pn = sb("prob", [SR, E, WIN])

    zeros = sem("zeros")
    res = Residual("res", sem, sums, a["x"], x1)
    x_in, ffn_x_in, tick = sem("x_in"), sem("x1_in"), sem("waited_tick")
    ffn_in = [sem(f"ffn_in{c}") for c in range(IC)]
    whi_ok, wlo_ok = sem("ffn_hi_ok"), sem("ffn_lo_ok")
    qc_hi_ok, qc_lo_ok, q_mm, q_act, q_dve = (
        sem(s) for s in ("qc_hi_ok", "qc_lo_ok", "q_mm", "q_act", "q_dve"))
    idx_ok, rot_cs, rot_ok = (sem(s) for s in ("idx_ok", "rot_cos_sin", "rot_ok"))
    gath = [sem(f"gathered{i}") for i in range(SLOTS)]
    t_mm, t_ev, s_mm, s_red, s_scl, s_max, s_sub, s_exp, s_sum, s_inv, s_pn, pf_ok = (
        sem(s) for s in ("t_mm", "t_ev", "s_mm", "s_red", "s_scl", "s_max", "s_sub", "s_exp",
                         "s_sum", "s_inv", "s_pn", "pf_ok"))
    p_mm, p_ev, av_mm, lat_ev = (sem(s) for s in ("p_mm", "p_ev", "av_mm", "lat_ev"))
    oh_ok, ol_ok, o_mm, oT_act, oT_dve, bt_mm = (
        sem(s) for s in ("oh_ok", "ol_ok", "o_mm", "oT_act", "oT_dve", "bt_mm"))

    c1, c2, c4, c8, c16, c12, c24 = (Count(n) for n in (1, 2, NLT, STEPS, 16, 12, 24))
    slot_uses = [len(range(i, STEPS, SLOTS)) for i in range(SLOTS)]

    def gathered(b, s):
        i = s % SLOTS
        return b * (16 * GROUPS * slot_uses[i]) + 16 * GROUPS * (s // SLOTS + 1)

    q_out = [("lat", h) for h in range(H)] + [("rope", h) for h in range(HH)]

    def tiles_at(s):
        return {STEPS - 3: (0, 1), STEPS - 2: (2, 3)}.get(s, ())

    def key_bank(s):
        return 4 if s == 1 else 2

    def q_bank(o):
        return o % 4 if o < 20 else o - 16

    def q_dst(o):
        kind, h = q_out[o]
        return q_lat[:, h % 2, :, h // 2] if kind == "lat" else q_rope[:, :, h]

    def turn_back(pe, b):
        pe.wait_ge(oT_act, c2(b, 2))
        pe.wait_ge(oT_dve, c2(b, 2))
        for t in range(NLT):
            for c in range(KC):
                last = pe.transpose(ps[0:LT, 4 + t, c * P:(c + 1) * P], oT[:, c, t * LT:(t + 1) * LT],
                                    ident[:, :])
            last.then_inc(bt_mm, 1)

    def add_back(dve, b, t):
        res.add(dve, b, t, bt_mm, ps[0:LT, 4 + t, :])

    def split_high(act, c):
        act.wait_ge(ffn_in[c], 16)
        act.activation(ffn_high(ffn, c), ffn["raw"][:, c, :], ACT.Copy).then_inc(whi_ok, 1)

    def split_low(dve, c):
        dve.wait_ge(whi_ok, c + 1)
        dve.tensor_tensor(ffn["lo"][:, c, :], ffn["raw"][:, c, :], ffn_high(ffn, c).bitcast(F32),
                          ALU.subtract).then_inc(wlo_ok, 1)

    @block.sync
    def _(sp):
        def body(b, first, last):
            sp.wait_ge(ln.turned, c4(b, NLT))
            if not last:
                sp.dma_start(rows[:, :, :], a["x"][bass.ds((b + 1) * TB, TB), :]
                             .rearrange("(t p) d -> p t d", p=LT)).then_inc(x_in, 16)
            else:
                for s in res.stored:
                    sp.wait_ge(s, 32)
                sp.dma_start(rows[:, :, :], x1[0:TB, :].rearrange("(t p) d -> p t d", p=LT)
                             ).then_inc(ffn_x_in, 16)
            if not first:
                res.rest(sp, b - 1)
            res.start(sp, b, fresh=first)

        blocks_of(sp, body)

    @block.gpsimd
    def _(pool):
        for i in range(2):
            pool.memset(ktr[i][0:R, 1, :], 0.0).then_inc(zeros, 1)
            pool.memset(ktr[i][R:P, 0, :], 0.0).then_inc(zeros, 1)
        pool.wait_ge(zeros, 4)

        def gather(b, s):
            if s == 0:
                pool.wait_ge(idx_ok, c1(b, 1))
            elif s >= SLOTS:
                pool.wait_ge(av_mm, c8(b, s - SLOTS + 1))
            if s == 0 or s >= SLOTS:
                pool.tensor_tensor(waited[:, s:s + 1], ident[0:GR, 0:1], ident[0:GR, 0:1],
                                   ALU.add).then_inc(tick, 1)
            for g in range(GROUPS):
                k = s * GROUPS + g
                pool.indirect_dma_start(
                    out=kvg[:, s % SLOTS, g, :], out_offset=None, in_=table,
                    in_offset=bass.IndirectOffsetOnAxis(ap=idx[:, k:k + 1], axis=0),
                ).then_inc(gath[s % SLOTS], 16)

        def rotate(b, s, first):
            ph = ((b * STEPS + s) % PERIOD) * GROUPS
            kr = kvg[:, s % SLOTS, :, KVC:ROW]
            pool.wait_ge(gath[s % SLOTS], gathered(b, s))
            if s >= 2:
                pool.wait_ge(t_mm, c8(b, s - 1))
            if s >= 1 or not first:
                pool.wait_ge(rot_ok, c8(b, s))
            pool.tensor_tensor(rc[:, :, :].rearrange("p g (h r) -> p g h r", h=2),
                              kr.rearrange("p g (h r) -> p g h r", h=2),
                              w["cosq"][:, bass.ds(ph, GROUPS), :].unsqueeze(2)
                              .to_broadcast([GR, GROUPS, 2, R // 2]), ALU.mult).then_inc(rot_cs, 1)
            for hf in range(2):
                pool.tensor_tensor(rs[:, :, 32 * hf:32 * hf + 32], kr[:, :, 32 - 32 * hf:64 - 32 * hf],
                                  w["sinq"][:, bass.ds(ph, GROUPS), 32 * hf:32 * hf + 32],
                                  ALU.mult).then_inc(rot_cs, 1)
            pool.wait_ge(rot_cs, c24(b, 3 * s + 3))
            pool.tensor_tensor(rot[s % 2][:, :, :], rc[:, :, :], rs[:, :, :], ALU.add).then_inc(rot_ok, 1)

        def body(b, first, last):
            if not first:
                pool.wait_ge(av_mm, c8(b, 0))
                pool.wait_ge(tick, Count(1 + STEPS - SLOTS)(b, 0))
            pool.tensor_copy(idx[:, :], w["idx_all"][:, bass.ds(b * BG, BG)]).then_inc(idx_ok, 1)
            ahead = 3 if first else SLOTS
            for s in range(ahead):
                gather(b, s)
            for s in range(STEPS):
                rotate(b, s, first)
                if first and s >= 1 and s + 2 < SLOTS:
                    gather(b, s + 2)
                if SLOTS <= s + 1 < STEPS:
                    gather(b, s + 1)
            if not last:
                ln.root(pool, b + 1)

        blocks_of(pool, body)
        ln_f.root(pool, 0)
        pool.wait_ge(av_mm, BLOCKS * STEPS)
        for c in range(IC):
            pool.dma_start(ffn["raw"][:, c, :], a["ffn_w"][c]).then_inc(ffn_in[c], 16)

    @block.tensor
    def _(pe):
        pe.wait_ge(zeros, 4)

        def query(b, o):
            kind, h = q_out[o]
            if 4 <= o < 20:
                pe.wait_ge(q_dve if o % 2 else q_act, c12(b, (o - 4) // 2 + 1))
            if kind == "lat":
                v, hs = "wl", slice(h, h + 1)
            else:
                v, hs = "wr", slice(2 * h, 2 * h + 2)
            parts = ((f"{v}_hi", qc_hi), (f"{v}_hi", qc_lo), (f"{v}_lo", qc_hi),
                     (f"{v}_2", q2_hi), (f"{v}_2", q2_lo))
            for n, (wt, xs) in enumerate(parts):
                last = pe.matmul(ps[:, q_bank(o), 0:TB], w[wt][:, hs, :].rearrange("p h c -> p (h c)"), xs[:, :],
                                 start=(n == 0), stop=(n == len(parts) - 1))
            last.then_inc(q_mm, 1)

        def turn_keys(b, s):
            pe.wait_ge(rot_ok, c8(b, s + 1))
            if s >= 2:
                pe.wait_ge(t_ev, c8(b, 1 if s == 2 else s))
            for g in range(GROUPS):
                pe.transpose(ps[:, key_bank(s), g * GR:(g + 1) * GR], kvg[:, s % SLOTS, g, 0:KVC],
                             ident[0:GR, 0:GR])
            for g in range(GROUPS):
                last = pe.transpose(ps[0:R, key_bank(s) + 1, g * GR:(g + 1) * GR], rot[s % 2][:, g, :],
                                    ident[0:GR, 0:GR])
            last.then_inc(t_mm, 1)

        def scores(b, s):
            pe.wait_ge(t_ev, c8(b, s + 1))
            for e in range(2):
                if s >= 1:
                    pe.wait_ge(s_red, c16(b, 2 * s - 1 + e))
                pe.matmul(ps[0:SR, e, 0:GROUPS * GR], w["other"][:, :], w["blocks"][:, :],
                          start=True, stop=False, skip_group_check=True)
                for g in range(GROUPS):
                    out = ps[0:SR, e, g * GR:(g + 1) * GR]
                    q0 = s * STEP + GSTART[g]
                    pe.matmul(out, q_lat[:, e, q0:q0 + GQ, :].rearrange("p q i -> p (q i)"),
                              ktn[s % 2][:, g * GR:(g + 1) * GR], start=False, stop=False,
                              skip_group_check=True)
                    last = pe.matmul(out, q_rope[:, q0:q0 + GQ, :].rearrange("p q i -> p (q i)"),
                                     ktr[s % 2][:, e, g * GR:(g + 1) * GR], start=False, stop=True,
                                     skip_group_check=True)
                last.then_inc(s_mm, 1)

        def turn_probs(b, s):
            pe.wait_ge(pf_ok, c8(b, s + 1))
            if s >= 1:
                pe.wait_ge(p_ev, c16(b, 2 * s))
            for g in range(GROUPS):
                for e in range(2):
                    at = (g % 2) * 2 * SR + e * SR
                    last = pe.transpose(ps[0:GR, 4 + g // 2, at:at + SR],
                                        pf[s % 2][:, e * GROUPS + g, :], ident[0:SR, 0:SR])
            last.then_inc(p_mm, 1)

        def values(b, s):
            pe.wait_ge(p_ev, c16(b, 2 * s + 2))
            if s >= 1:
                pe.wait_ge(lat_ev, c24(b, 3 * s))
            for g in range(GROUPS):
                at = (g % 2) * 2 * SR
                last = pe.matmul(ps[:, 6 + g // 2, at:at + 2 * SR], kvg[:, s % SLOTS, g, 0:KVC],
                                 pt[s % 2][:, g * 2 * SR:(g + 1) * 2 * SR], start=True, stop=True)
            last.then_inc(av_mm, 1)

        def body(b, first, last_block):
            pe.wait_ge(qc_lo_ok, c2(b, 2))
            for o in range(4):
                query(b, o)
            if not first:
                turn_back(pe, b - 1)
            for o in range(4, len(q_out)):
                if o >= 20 and not first:
                    pe.wait_ge(res.summed, c4(b - 1, o - 19))
                if o == 22:
                    pe.wait_ge(q_act, c12(b, 10))
                    pe.wait_ge(q_dve, c12(b, 10))
                    turn_keys(b, 0)
                query(b, o)
            pe.wait_ge(q_act, c12(b, 11))
            pe.wait_ge(q_dve, c12(b, 11))
            turn_keys(b, 1)
            pe.wait_ge(q_act, c12(b, 12))
            pe.wait_ge(q_dve, c12(b, 12))
            scores(b, 0)
            turn_keys(b, 2)
            scores(b, 1)
            for s in range(STEPS):
                if s == 0:
                    turn_keys(b, 3)
                    scores(b, 2)
                turn_probs(b, s)
                if s >= 1 and s + 2 < STEPS:
                    scores(b, s + 2)
                if s + 4 < STEPS:
                    turn_keys(b, s + 4)
                for t in tiles_at(s):
                    if last_block:
                        ln_f.turn(pe, 0, t, (2, 3))
                    else:
                        ln.turn(pe, b + 1, t, (2, 3))
                if s == STEPS - 1 and not last_block:
                    pe.wait_ge(s_red, c16(b, 16))
                    compress(pe, b + 1, 0, w, rowsT, ps, ln, qc_mm)
                values(b, s)
            if not last_block:
                compress(pe, b + 1, 1, w, rowsT, ps, ln, qc_mm)
            for h in range(H):
                pe.wait_ge(ol_ok, c16(b, h + 1))
                for m in range(KC):
                    cols = slice(m * P, (m + 1) * P)
                    parts = (("wvo_hi", o_hi), ("wvo_hi", o_lo), ("wvo_lo", o_hi))
                    for n, (wt, xs) in enumerate(parts):
                        last = pe.matmul(ps[:, 4 + m, 0:TB], w[wt][:, h, cols], xs[h % 2][:, :],
                                         start=(h == 0 and n == 0), stop=(h == H - 1 and n == 2))
                last.then_inc(o_mm, 1)

        blocks_of(pe, body)

    @block.scalar
    def _(act):
        def split_compressed(b):
            for m, dst in enumerate((qc_hi, q2_hi)):
                act.wait_ge(qc_mm, c2(b, m + 1))
                act.activation(dst[:, :], ps[:, m, 0:TB], ACT.Copy).then_inc(qc_hi_ok, 1)

        def take_keys(b, s):
            act.wait_ge(t_mm, c8(b, s + 1))
            if s >= 2:
                act.wait_ge(s_mm, c16(b, 2 * s - 2))
            act.activation(ktn[s % 2][:, :], ps[:, key_bank(s), 0:GROUPS * GR], ACT.Copy)
            act.activation(ktr[s % 2][0:R, 0, :], ps[0:R, key_bank(s) + 1, 0:GROUPS * GR], ACT.Copy)
            act.activation(ktr[s % 2][R:P, 1, :], ps[0:R, key_bank(s) + 1, 0:GROUPS * GR], ACT.Copy).then_inc(t_ev, 1)

        def exps(b, s):
            act.wait_ge(s_sub, c8(b, s + 1))
            act.activation(ex[s % 2][:, :, :], sd[s % 2][:, :, :], ACT.Exp).then_inc(s_exp, 1)

        def take_probs(b, s):
            act.wait_ge(p_mm, c8(b, s + 1))
            act.activation(pt[s % 2][:, 0:4 * SR], ps[0:GR, 4, 0:4 * SR], ACT.Copy).then_inc(p_ev, 1)
            act.activation(pt[s % 2][:, 4 * SR:6 * SR], ps[0:GR, 5, 0:2 * SR], ACT.Copy).then_inc(p_ev, 1)

        def take_values(b, s):
            act.wait_ge(av_mm, c8(b, s + 1))
            for g in range(GROUPS):
                q0 = s * STEP + GSTART[g]
                at = (g % 2) * 2 * SR
                if g:
                    act.wait_ge(lat_ev, c24(b, 3 * s + g))
                act.activation(
                    q_lat[:, :, q0:q0 + GQ, :].rearrange("p e q i -> p e (q i)"),
                    ps[:, 6 + g // 2, at:at + 2 * SR].rearrange("p (e r) -> p e r", e=2),
                    ACT.Copy).then_inc(lat_ev, 1)

        def high_latent(b, h):
            if h >= 2:
                act.wait_ge(o_mm, c16(b, h - 1))
            act.activation(o_hi[h % 2][:, :], q_lat[:, h % 2, :, h // 2], ACT.Copy).then_inc(oh_ok, 1)

        def body(b, first, last):
            if first:
                split_compressed(b)
            for o in range(0, len(q_out), 2):
                if o == 22:
                    take_keys(b, 0)
                act.wait_ge(q_mm, c24(b, o + 1))
                act.activation(q_dst(o), ps[:, q_bank(o), 0:TB], ACT.Copy).then_inc(q_act, 1)
            take_keys(b, 1)
            exps(b, 0)
            take_keys(b, 2)
            for s in range(STEPS):
                if s + 1 < STEPS:
                    exps(b, s + 1)
                if s + 3 < STEPS:
                    take_keys(b, s + 3)
                take_probs(b, s)
                for t in tiles_at(s):
                    if last:
                        ln_f.high(act, 0, t, (2, 3))
                    else:
                        ln.high(act, b + 1, t, (2, 3))
                take_values(b, s)
            act.wait_ge(lat_ev, c24(b, 24))
            high_latent(b, 0)
            high_latent(b, 1)
            if not last:
                split_compressed(b + 1)
            for h in range(2, H):
                high_latent(b, h)
                if last and h % 3 == 2 and h >= 8:
                    split_high(act, (h - 8) // 3)
            act.wait_ge(o_mm, c16(b, H))
            for m in (0, 2):
                act.activation(oT[:, m, :], ps[:, 4 + m, 0:TB], ACT.Copy).then_inc(oT_act, 1)

        blocks_of(act, body)

    @block.vector
    def _(dve):
        def split_compressed(b):
            for m, (hi, lo) in enumerate(((qc_hi, qc_lo), (q2_hi, q2_lo))):
                dve.wait_ge(qc_hi_ok, c2(b, m + 1))
                dve.tensor_tensor(lo[:, :], ps[:, m, 0:TB], hi[:, :].bitcast(F32),
                                  ALU.subtract).then_inc(qc_lo_ok, 1)

        def window(b, s):
            for e in range(2):
                dve.wait_ge(s_mm, c16(b, 2 * s + e + 1))
                dve.tensor_reduce(sc[:, e * GROUPS:(e + 1) * GROUPS, :],
                                  ps[0:SR, e, 0:GROUPS * GR].rearrange("p (g q j) -> p g j q", g=GROUPS, q=GQ),
                                  AX.X, ALU.max).then_inc(s_red, 1)
            dve.wait_ge(s_red, c16(b, 2 * s + 2))
            dve.scalar_tensor_tensor(
                out=sa[:, :, :].rearrange("p (e g) j -> p e (g j)", e=2),
                in0=sc[:, :, :].rearrange("p (e g) j -> p e (g j)", e=2), scalar=SCALE,
                in1=w["neg_all"][:, bass.ds((b * STEPS + s) * GROUPS * WIN, GROUPS * WIN)].unsqueeze(1)
                .to_broadcast([SR, 2, GROUPS * WIN]),
                op0=ALU.mult, op1=ALU.add).then_inc(s_scl, 1)
            dve.wait_ge(s_scl, c8(b, s + 1))
            dve.tensor_reduce(mx[:, :], sa[:, :, :], AX.X, ALU.max).then_inc(s_max, 1)
            dve.wait_ge(s_max, c8(b, s + 1))
            dve.tensor_tensor(sd[s % 2][:, :, :], sa[:, :, :],
                              mx[:, :].unsqueeze(2).to_broadcast([SR, E, WIN]),
                              ALU.subtract).then_inc(s_sub, 1)

        def probs(b, s):
            dve.wait_ge(s_exp, c8(b, s + 1))
            dve.tensor_reduce(tot[:, :], ex[s % 2][:, :, :], AX.X, ALU.add).then_inc(s_sum, 1)
            dve.wait_ge(s_sum, c8(b, s + 1))
            dve.reciprocal(inv[:, :], tot[:, :]).then_inc(s_inv, 1)
            dve.wait_ge(s_inv, c8(b, s + 1))
            dve.tensor_tensor(pn[:, :, :], ex[s % 2][:, :, :],
                              inv[:, :].unsqueeze(2).to_broadcast([SR, E, WIN]),
                              ALU.mult).then_inc(s_pn, 1)
            dve.wait_ge(s_pn, c8(b, s + 1))
            if s >= 2:
                dve.wait_ge(p_mm, c8(b, s - 1))
            dve.tensor_tensor(
                pf[s % 2][:, :, :].rearrange("p x (q j) -> p x q j", q=GQ),
                pn[:, :, :].unsqueeze(2).to_broadcast([SR, E, GQ, WIN]),
                w["mask"][:, :].rearrange("p (q j) -> p q j", q=GQ).unsqueeze(1)
                .to_broadcast([SR, E, GQ, WIN]), ALU.mult).then_inc(pf_ok, 1)

        def low_latent(b, h):
            dve.wait_ge(oh_ok, c16(b, h + 1))
            dve.tensor_tensor(o_lo[h % 2][:, :], q_lat[:, h % 2, :, h // 2], o_hi[h % 2][:, :].bitcast(F32),
                              ALU.subtract).then_inc(ol_ok, 1)

        adds, stats = (5, 7, 13, 17), (3, 9, 15, 21)

        def next_norm(b, last, piece):
            if last:
                ln_f.piece(dve, 0, piece, ffn_x_in)
            else:
                ln.piece(dve, b + 1, piece, x_in, loads=b + 1)

        def body(b, first, last):
            if first:
                split_compressed(b)
            for o in range(1, len(q_out), 2):
                dve.wait_ge(q_mm, c24(b, o + 1))
                dve.tensor_copy(q_dst(o), ps[:, q_bank(o), 0:TB]).then_inc(q_dve, 1)
                if o in adds and not first:
                    add_back(dve, b - 1, adds.index(o))
                if o in stats:
                    next_norm(b, last, stats.index(o))
            window(b, 0)
            probs(b, 0)
            for s in range(STEPS):
                if s + 1 < STEPS:
                    window(b, s + 1)
                if s + 1 < STEPS:
                    probs(b, s + 1)
                if NLT <= s + 1 < NLT + 3:
                    next_norm(b, last, s + 1)
                if last:
                    for t in tiles_at(s):
                        ln_f.low(dve, 0, t, (2, 3))
            low_latent(b, 0)
            low_latent(b, 1)
            if not last:
                split_compressed(b + 1)
            for h in range(2, H):
                low_latent(b, h)
                if last and h % 3 == 0 and h >= 9:
                    split_low(dve, (h - 9) // 3)
            dve.wait_ge(o_mm, c16(b, H))
            for m in (1, 3):
                dve.tensor_copy(oT[:, m, :], ps[:, 4 + m, 0:TB]).then_inc(oT_dve, 1)

        blocks_of(dve, body)
    return res, turn_back, add_back, ffn_x_in, split_high, split_low, wlo_ok


def build_ffn(nc, block, ctx, a, ffn, ps, ident, x1, rows, rowsT, four, ln, sums, scale, attention,
              low_mass, low_any, low_flag):
    def sem(name):
        return ctx.enter_context(nc.semaphore(name))

    w_lo, h_hi, h_lo, act_g, hf, oT = (ffn[s] for s in ("lo", "h_hi", "h_lo", "silu", "hidden", "yT"))
    xT_hi, xT_lo = rowsT, four
    attn_res, attn_turn_back, attn_add_back, x_in, split_high, split_low, wlo_ok = attention
    s_in, tail_in, tail_out = sem("scale_in"), sem("tail_in"), sem("tail_out")
    mass_ok, any_step, any_mm, flag_ok = (sem(s) for s in ("mass_ok", "any_step", "any_mm", "flag_ok"))
    res = Residual("fres", sem, sums, x1, a["out"])
    g_mm, u_mm, silu_ok, hf_ok, hh_ok, hl_ok, d_mm, d_act, d_dve, y_mm = (
        sem(s) for s in ("g_mm", "u_mm", "silu_ok", "hf_ok", "hh_ok", "hl_ok", "d_mm", "d_act", "d_dve", "y_mm"))
    cI, c4, c2 = Count(IC), Count(NLT), Count(2)

    @block.sync
    def _(sp):
        def body(b, first, last):
            if not last:
                sp.wait_ge(ln.turned, c4(b, NLT))
                sp.dma_start(rows[:, :, :], x1[bass.ds((b + 1) * TB, TB), :]
                             .rearrange("(t p) d -> p t d", p=LT)).then_inc(x_in, 16)
            if first:
                attn_res.rest(sp, BLOCKS - 1)
                attn_res.finish(sp)
            else:
                res.rest(sp, b - 1)
            res.start(sp, b, fresh=first)

        sp.dma_start(scale[:, :], a["ffn_scale"]).then_inc(s_in, 16)
        for s in attn_res.stored:
            sp.wait_ge(s, 64)
        blocks_of(sp, body)
        tail = x1[bass.ds((BLOCKS - 1) * TB, TB), :], a["out"][bass.ds((BLOCKS - 1) * TB, TB), :]
        sp.wait_ge(ln.turned, NLT * BLOCKS)
        for t in range(2, NLT):
            sp.dma_start(rows[:, t, :], tail[0][t * LT:(t + 1) * LT, :]).then_inc(tail_in, 16)
        for t in range(2):
            res.store(sp, BLOCKS - 1, t)
        for t in range(2, NLT):
            sp.wait_ge(res.summed, NLT * (BLOCKS - 1) + t + 1)
            sp.dma_start(tail[1][t * LT:(t + 1) * LT, :], rows[:, t, :]).then_inc(tail_out, 16)
        for s in res.stored:
            sp.wait_ge(s, 32 * (BLOCKS - 1) + 16)
        sp.wait_ge(tail_out, 16 * (NLT - 2))

    @block.gpsimd
    def _(pool):
        with pool.Fori(1, BLOCKS) as b:
            ln.root(pool, b)

    def wt(part, c, which, k):
        cols = slice(which * KC * P + k * P, which * KC * P + (k + 1) * P)
        return ffn_high(ffn, c)[:, cols] if part == "hi" else w_lo[:, c, cols]

    @block.tensor
    def _(pe):
        def turn_back(b, t):
            if t == 0:
                pe.wait_ge(d_act, c2(b, 2))
                pe.wait_ge(d_dve, c2(b, 2))
            if t >= 2:
                pe.wait_ge(res.summed, c4(b, t - 1))
            for k in range(KC):
                last = pe.transpose(ps[0:LT, 6 + t % 2, k * P:(k + 1) * P],
                                    oT[:, k, t * LT:(t + 1) * LT], ident[:, :])
            last.then_inc(y_mm, 1)

        def low_products(first, some_low, products):
            if first:
                products()
            else:
                with pe.If(some_low != 0):
                    products()

        def body(b, first, last_block, some_low):
            pe.wait_ge(ln.lo_ok, c4(b, NLT))
            for c in range(IC):
                if first:
                    pe.wait_ge(wlo_ok, c + 1)

                def product(which, part, xs, k, **flags):
                    return pe.matmul(ps[:, 2 * which + c % 2, 0:TB], wt(part, c, which, k), xs[:, k, :],
                                     skip_group_check=True, **flags)

                def with_low():
                    for which in range(2):
                        for k in range(KC):
                            product(which, "lo", xT_hi, k, start=False, stop=False)

                for which in range(2):
                    if c >= 2:
                        pe.wait_ge(hf_ok if which else silu_ok, cI(b, c - 1))
                    for k in range(KC):
                        product(which, "hi", xT_lo, k, start=(k == 0), stop=False)
                    for k in range(KC - 1):
                        product(which, "hi", xT_hi, k, start=False, stop=False)
                low_products(first, some_low, with_low)
                for which, done in ((0, g_mm), (1, u_mm)):
                    product(which, "hi", xT_hi, KC - 1, start=False, stop=True).then_inc(done, 1)
                if first and c == 0:
                    attn_turn_back(pe, BLOCKS - 1)
                if not first and c in (0, 3):
                    for t in ((0, 1) if c == 0 else (2, 3)):
                        turn_back(b - 1, t)
            for m in range(KC):
                if m == KC - 1 and first:
                    pe.wait_ge(any_step, 2)
                    pe.matmul(ps[0:1, 0, 0:1], low_any[:, :], low_any[:, :], start=True,
                              stop=True).then_inc(any_mm, 1)
                if m >= 2:
                    pe.wait_ge(d_dve if m % 2 else d_act, c2(b, m // 2))

                def product(part, xs, c, **flags):
                    return pe.matmul(ps[:, 4 + m % 2, 0:TB], wt(part, c, 2, m), xs[:, c, :],
                                     skip_group_check=True, **flags)

                def with_low():
                    for c in range(IC):
                        product("lo", h_hi, c, start=False, stop=False)

                for c in range(IC):
                    if m == 0:
                        pe.wait_ge(hl_ok, cI(b, c + 1))
                    product("hi", h_lo, c, start=(c == 0), stop=False)
                    if c < IC - 1:
                        product("hi", h_hi, c, start=False, stop=False)
                low_products(first, some_low, with_low)
                product("hi", h_hi, IC - 1, start=False, stop=True).then_inc(d_mm, 1)
                if m < 2 and not last_block:
                    ln.turn(pe, b + 1, 2 * m, (6, 7))
                    ln.turn(pe, b + 1, 2 * m + 1, (6, 7))
            if last_block:
                for t in range(NLT):
                    turn_back(b, t)

        body(0, True, False, None)
        pe.wait_ge(flag_ok, 1)
        some_low = pe.value_load(low_flag[0:1, 0:1], min_val=0, max_val=P)
        with pe.Fori(1, BLOCKS - 1) as b:
            body(b, False, False, some_low)
        body(BLOCKS - 1, False, True, some_low)

    @block.scalar
    def _(act):
        def mass(c):
            act.wait_ge(wlo_ok, c + 1)
            if c:
                act.wait_ge(mass_ok, c)
            act.activation(ffn["unread"][:, :], w_lo[:, c, :].bitcast(F32), ACT.Abs,
                           accum_out=low_mass[:, c:c + 1]).then_inc(mass_ok, 1)

        masses = {2: (0,), 4: (1,), 6: (2,), 8: (3,), 9: (4,), 10: (5,)}
        late_masses = {-1: (6, 7), 0: (8, 9), 1: (10,)}

        def high(b, c):
            act.wait_ge(hf_ok, cI(b, c + 1))
            act.activation(h_hi[:, c, :], hf[:, c % 2, :], ACT.Copy).then_inc(hh_ok, 1)

        def body(b, first, last):
            for c in range(IC):
                act.wait_ge(g_mm, cI(b, c + 1))
                if c >= 2:
                    act.wait_ge(hf_ok, cI(b, c - 1))
                act.activation(act_g[:, c % 2, :], ps[:, c % 2, 0:TB], ACT.Silu,
                               scale=scale[:, c:c + 1]).then_inc(silu_ok, 1)
                if first and c + EARLY < IC:
                    split_high(act, c + EARLY)
                if c:
                    high(b, c - 1)
                if first:
                    for done in masses.get(c, ()):
                        mass(done)
            high(b, IC - 1)
            if first:
                for done in late_masses[-1]:
                    mass(done)
            for m in range(KC):
                if m % 2 == 0:
                    act.wait_ge(d_mm, c4(b, m + 1))
                    act.activation(oT[:, m, :], ps[:, 4 + m % 2, 0:TB], ACT.Copy,
                                   scale=scale[:, 2 * IC + m:2 * IC + m + 1]).then_inc(d_act, 1)
                if m < 2 and not last:
                    ln.high(act, b + 1, 2 * m, (6, 7))
                    ln.high(act, b + 1, 2 * m + 1, (6, 7))
                if first:
                    for done in late_masses.get(m, ()):
                        mass(done)

        act.wait_ge(s_in, 16)
        blocks_of(act, body)

    @block.vector
    def _(dve):
        def low_parts():
            dve.wait_ge(mass_ok, IC)
            dve.tensor_scalar(low_mass[:, :], low_mass[:, :], 0.0, None, ALU.not_equal).then_inc(any_step, 1)
            dve.wait_ge(any_step, 1)
            dve.tensor_reduce(low_any[:, :], low_mass[:, :], AX.X, ALU.max).then_inc(any_step, 1)

        def low(b, c):
            dve.wait_ge(hh_ok, cI(b, c + 1))
            dve.tensor_tensor(h_lo[:, c, :], hf[:, c % 2, :], h_hi[:, c, :].bitcast(F32),
                              ALU.subtract).then_inc(hl_ok, 1)

        def add_back(b, t):
            res.add(dve, b, t, y_mm, ps[0:LT, 6 + t % 2, :])

        def body(b, first, last):
            for c in range(IC):
                dve.wait_ge(u_mm, cI(b, c + 1))
                dve.wait_ge(silu_ok, cI(b, c + 1))
                if c >= 2:
                    dve.wait_ge(hl_ok, cI(b, c - 1))
                dve.scalar_tensor_tensor(out=hf[:, c % 2, :], in0=ps[:, 2 + c % 2, 0:TB],
                                         scalar=scale[:, IC + c:IC + c + 1], in1=act_g[:, c % 2, :],
                                         op0=ALU.mult, op1=ALU.mult).then_inc(hf_ok, 1)
                if first and c + EARLY < IC:
                    split_low(dve, c + EARLY)
                if c:
                    low(b, c - 1)
                if first and c < 2:
                    attn_add_back(dve, BLOCKS - 1, 2 * c)
                    attn_add_back(dve, BLOCKS - 1, 2 * c + 1)
                if not first and c in (0, 3):
                    for t in ((0, 1) if c == 0 else (2, 3)):
                        add_back(b - 1, t)
                if c >= IC - 7 and not last:
                    ln.piece(dve, b + 1, c - IC + 7, x_in, loads=b + 2)
            low(b, IC - 1)
            for m in range(KC):
                if m == 2 and first:
                    low_parts()
                    dve.wait_ge(any_mm, 1)
                    dve.tensor_copy(low_flag[:, :], ps[0:1, 0, 0:1]).then_inc(flag_ok, 1)
                if m % 2:
                    dve.wait_ge(d_mm, c4(b, m + 1))
                    dve.tensor_scalar(oT[:, m, :], ps[:, 4 + m % 2, 0:TB],
                                      scale[:, 2 * IC + m:2 * IC + m + 1], None, ALU.mult).then_inc(d_dve, 1)
                if m < 2 and not last:
                    ln.low(dve, b + 1, 2 * m, (6, 7))
                    ln.low(dve, b + 1, 2 * m + 1, (6, 7))
            if last:
                add_back(b, 0)
                add_back(b, 1)
                dve.wait_ge(tail_in, 16 * (NLT - 2))
                for t in range(2, NLT):
                    dve.wait_ge(y_mm, c4(b, t + 1))
                    dve.tensor_tensor(rows[:, t, :], ps[0:LT, 6 + t % 2, :], rows[:, t, :],
                                      ALU.add).then_inc(res.summed, 1)

        dve.wait_ge(s_in, 16)
        body(0, True, False)
        with dve.Fori(1, BLOCKS - 1) as b:
            body(b, False, False)
        body(BLOCKS - 1, False, True)


def constants():
    import numpy as np

    f = np.float32
    half = R // 2
    inv_freq = (1.0 / (f(10000.0) ** (np.arange(half, dtype=f) / f(half)))).astype(f)
    ang = np.arange(LK, dtype=f)[:, None] * inv_freq
    cos, sin = np.cos(ang).astype(f), np.sin(ang).astype(f)
    kpos = np.minimum(np.arange(TROWS), LK - 1).reshape(KT, P).T
    first = np.array([s * STEP + g for s in range(TOK // STEP) for g in GSTART])
    tok = first[None, :] + (np.arange(GR) // WIN)[:, None]
    qpos = tok[:, :PERIOD * GROUPS] % LQ
    same = (np.arange(SR) // HH)[:, None] == (np.arange(GR) // WIN)[None, :]
    query = np.arange(P)[:, None]
    other = (query < GQ) & (query != (np.arange(SR) // HH)[None, :])
    blocks = (query < GQ) & (query == (np.arange(GR) // WIN)[None, :])
    return tok, first, {
        "ident": np.eye(P, dtype=f),
        "mask": same.astype(f), "other": other.astype(f), "blocks": np.where(blocks, f(FAR), f(0)),
        "cosk": cos[kpos], "sink": np.concatenate([-sin[kpos], sin[kpos]], -1),
        "cosq": cos[qpos], "sinq": np.concatenate([sin[qpos], -sin[qpos]], -1),
        "row_base": (tok // LQ * TROWS).astype(f),
        "joff": (np.arange(GR) % WIN - LOOKBACK).astype(f)[:, None],
        "joff9": np.broadcast_to((np.arange(WIN) - LOOKBACK).astype(f), (SR, WIN)),
    }


def kernel(x, ctx_2048, itok_BxS_0_1023, L0_xattn_W_kvc, L0_xattn_W_dq, L0_xattn_W_uq, L0_xattn_W_qr,
           L0_xattn_W_uk, L0_xattn_W_kr, L0_xattn_W_uv, L0_xattn_W_o, L0_ffn_gate_w, L0_ffn_up_w,
           L0_ffn_down_w, L0_ffn_gate_s, L0_ffn_up_s, L0_ffn_down_s):
    import numpy as np
    import concourse.bacc as bacc
    from concourse.bass_utils import run_bass_kernel_spmd

    def twice(m):
        return np.concatenate([m, m[..., P:]], -1)

    tok, first, arrays = constants()
    seg = np.asarray(itok_BxS_0_1023).reshape(TOK)
    arrays["x"] = np.asarray(x).reshape(TOK, D)
    arrays["ctxT"] = np.asarray(ctx_2048).reshape(NB, LK, KC, P).transpose(0, 3, 2, 1)
    arrays["segp"] = seg[tok]
    arrays["segh"] = seg[first[None, :] + (np.arange(SR) // HH)[:, None]]
    arrays["wkvc"] = np.asarray(L0_xattn_W_kvc).reshape(KC, P, KVC).transpose(1, 0, 2)
    arrays["wkvcT"] = np.asarray(L0_xattn_W_kvc).T
    arrays["wkr"] = np.asarray(L0_xattn_W_kr)
    arrays["wdq"] = twice(np.asarray(L0_xattn_W_dq).reshape(KC, P, QC).transpose(1, 0, 2))
    uq = twice(np.asarray(L0_xattn_W_uq).reshape(QC, H, HD).transpose(1, 2, 0))
    uk = np.asarray(L0_xattn_W_uk).reshape(KVC, H, HD).transpose(1, 2, 0)
    uv = np.asarray(L0_xattn_W_uv).reshape(KVC, H, HD).transpose(1, 2, 0)
    qr = np.asarray(L0_xattn_W_qr).reshape(QC, H, R).transpose(1, 0, 2)
    arrays["head_w"] = np.concatenate([uq, uk, uv, qr[:, :P], np.concatenate([qr[:, P:], qr[:, P:]], 1),
                                       np.asarray(L0_xattn_W_o).reshape(H, HD, D)], -1)
    gate, up = (np.asarray(m).reshape(IC, P, KC, P).transpose(0, 3, 2, 1).reshape(IC, P, KC * P)
                for m in (L0_ffn_gate_w, L0_ffn_up_w))
    arrays["ffn_w"] = np.concatenate([gate, up, np.asarray(L0_ffn_down_w).T.reshape(IC, P, D)], -1)
    arrays["ffn_scale"] = np.concatenate(
        [np.asarray(m).reshape(-1, P).T for m in (L0_ffn_gate_s, L0_ffn_up_s, L0_ffn_down_s)], -1)

    nc = bacc.Bacc("TRN2", target_bir_lowering=False, num_devices=1)
    aps = {}
    for name in arrays:
        arrays[name] = np.ascontiguousarray(arrays[name])
        aps[name] = nc.dram_tensor(name + "_dram", arrays[name].shape, mybir.dt.from_np(arrays[name].dtype),
                                   kind="ExternalInput").ap()
    aps["out"] = nc.dram_tensor("out_dram", [TOK, D], F32, kind="ExternalOutput").ap()
    build(nc, aps)
    r = run_bass_kernel_spmd(nc, [{name + "_dram": v for name, v in arrays.items()}], core_ids=[0])
    return r.results[0]["out_dram"].reshape(NB, LQ, D)
```
